# Optimizing a Trainium2 kernel written in Bass

```python
import numpy as np
import jax
import jax.numpy as jnp

def _softmax(x, axis=-1):
    return jax.nn.softmax(x, axis=axis)

def _gelu(x):
    return jax.nn.gelu(x, approximate=True)

def _silu(x):
    return jax.nn.silu(x)

def _sigmoid(x):
    return jax.nn.sigmoid(x)

def _layernorm(x, axis=-1, eps=1e-05):
    m = jnp.mean(x, axis=axis, keepdims=True)
    v = jnp.var(x, axis=axis, keepdims=True)
    return (x - m) / jnp.sqrt(v + eps)

def _scatter_add(tgt, idx, src, axis=0):
    return tgt.at[idx].add(src)

def _segment_sum(src, seg, n):
    return jax.ops.segment_sum(src, seg, n)
kernel_name = 'mk_lm_tower_d2_tok_ids768_r4_9e1ddc'

def setup_inputs(seed: int=0):
    np.random.seed(seed)
    _w = jnp.asarray

    def _rec_inputs():
        import jax
        import jax.numpy as jnp
        _rk = jax.random.key(seed)
        x = jax.random.randint(jax.random.fold_in(_rk, 1), (8, 256), 0, 8000, jnp.int32)
        return x
    x = _rec_inputs()

    def _L0_tok_setup():
        import jax, jax.numpy as jnp
        import numpy as np
        N_QUBITS = 6
        N_LAYERS = 3
        DIM = 1 << N_QUBITS
        VOCAB = 8000
        EMBED = 192
        B, S = (16, 1024)

        def _cnot_perm(control, target):
            idx = np.arange(DIM)
            cbit = idx >> N_QUBITS - 1 - control & 1
            flipped = idx ^ 1 << N_QUBITS - 1 - target
            return np.where(cbit == 1, flipped, idx)
        _idx = np.arange(DIM)
        Z_SIGNS = np.stack([1.0 - 2.0 * (_idx >> N_QUBITS - 1 - q & 1) for q in range(N_QUBITS)], axis=1).astype(np.float32)

        def _apply_ry(state, theta, q):
            T = state.shape[0]
            left, right = (1 << q, 1 << N_QUBITS - 1 - q)
            s = state.reshape(T, left, 2, right)
            c = jnp.cos(theta * 0.5)[:, None, None]
            sn = jnp.sin(theta * 0.5)[:, None, None]
            a0, a1 = (s[:, :, 0, :], s[:, :, 1, :])
            out = jnp.stack([c * a0 - sn * a1, sn * a0 + c * a1], axis=2)
            return out.reshape(T, DIM)

        def _apply_rz(state, theta, q):
            T = state.shape[0]
            left, right = (1 << q, 1 << N_QUBITS - 1 - q)
            s = state.reshape(T, left, 2, right)
            ph = jnp.exp(1j * (theta * 0.5)).astype(state.dtype)[:, None, None]
            out = jnp.stack([jnp.conj(ph) * s[:, :, 0, :], ph * s[:, :, 1, :]], axis=2)
            return out.reshape(T, DIM)

        def _circuit_expvals(params):
            T = params.shape[0]
            state = jnp.zeros((T, DIM), dtype=jnp.complex64).at[:, 0].set(1.0)
            for layer in range(N_LAYERS):
                for q in range(N_QUBITS):
                    state = _apply_ry(state, params[:, layer, q, 0], q)
                    state = _apply_rz(state, params[:, layer, q, 1], q)
                if layer < N_LAYERS - 1:
                    for q in range(N_QUBITS - 1):
                        state = state[:, _cnot_perm(q, q + 1)]
                    if N_QUBITS > 2:
                        state = state[:, _cnot_perm(N_QUBITS - 1, 0)]
            probs = state.real ** 2 + state.imag ** 2
            return probs @ jnp.asarray(Z_SIGNS)
        key = jax.random.key(seed)
        k1, k2, k3, k4 = jax.random.split(key, 4)
        token_ids = jax.random.randint(k1, (B, S), 0, VOCAB)
        quantum_params = jax.random.normal(k2, (VOCAB, N_LAYERS, N_QUBITS, 2), dtype=jnp.float32) * 0.1
        post_w = jax.random.normal(k3, (EMBED, N_QUBITS), dtype=jnp.float32) / np.sqrt(N_QUBITS)
        post_b = jax.random.normal(k4, (EMBED,), dtype=jnp.float32) * 0.01
        return {'token_ids': token_ids, 'quantum_params': quantum_params, 'post_w': post_w, 'post_b': post_b}
    _L0_tok_all = _L0_tok_setup()
    _L0_tok_in = {k: v for k, v in _L0_tok_all.items() if k in ('quantum_params', 'post_w', 'post_b')}
    del _L0_tok_all

    def _L0_attn_setup():
        import jax, jax.numpy as jnp
        import numpy as np
        B, N, DIM, H = (4, 256, 192, 8)
        HD = DIM // H

        def qlinear(x, wr, wi, wj, wk, b=None):
            xr, xi, xj, xk = jnp.split(x, 4, axis=-1)
            r = xr @ wr - xi @ wi - xj @ wj - xk @ wk
            i = xr @ wi + xi @ wr + xj @ wk - xk @ wj
            j = xr @ wj - xi @ wk + xj @ wr + xk @ wi
            k = xr @ wk + xi @ wj - xj @ wi + xk @ wr
            out = jnp.concatenate([r, i, j, k], axis=-1)
            return out + b if b is not None else out
        key = jax.random.key(seed)
        ks = jax.random.split(key, 10)
        s = 0.02
        return {'x': jax.random.normal(ks[0], (B, N, DIM), jnp.float32), 'wqkv_r': jax.random.normal(ks[1], (DIM // 4, 3 * DIM // 4), jnp.float32) * s, 'wqkv_i': jax.random.normal(ks[2], (DIM // 4, 3 * DIM // 4), jnp.float32) * s, 'wqkv_j': jax.random.normal(ks[3], (DIM // 4, 3 * DIM // 4), jnp.float32) * s, 'wqkv_k': jax.random.normal(ks[4], (DIM // 4, 3 * DIM // 4), jnp.float32) * s, 'wp_r': jax.random.normal(ks[5], (DIM // 4, DIM // 4), jnp.float32) * s, 'wp_i': jax.random.normal(ks[6], (DIM // 4, DIM // 4), jnp.float32) * s, 'wp_j': jax.random.normal(ks[7], (DIM // 4, DIM // 4), jnp.float32) * s, 'wp_k': jax.random.normal(ks[8], (DIM // 4, DIM // 4), jnp.float32) * s, 'bp': jnp.zeros((DIM,), jnp.float32)}
    _L0_attn_all = _L0_attn_setup()
    _L0_attn_in = {k: v for k, v in _L0_attn_all.items() if k in ('wqkv_r', 'wqkv_i', 'wqkv_j', 'wqkv_k', 'wp_r', 'wp_i', 'wp_j', 'wp_k', 'bp')}
    del _L0_attn_all

    def _L0_ffn_setup():
        import jax, jax.numpy as jnp
        import numpy as np
        ATOM = {'vm': 0, 'im': 1, 'cm': 2, 'sc': 3, 'cc': 4}
        TASK_PAIRS = [('vm', 'sc'), ('vm', 'cc'), ('im', 'sc'), ('im', 'cc'), ('cm', 'sc'), ('cm', 'cc')]
        SRC_IDX = np.array([[ATOM[l], ATOM[r]] for l, r in TASK_PAIRS], dtype=np.int32)
        DST_IDX = np.array([[ATOM[r], ATOM[l]] for l, r in TASK_PAIRS], dtype=np.int32)
        NCLS = 6
        NATOMS = 5

        def _l2norm(x, eps=1e-12):
            return x / jnp.clip(jnp.linalg.norm(x, axis=-1, keepdims=True), eps)
        key = jax.random.key(seed)
        ks = jax.random.split(key, 12)
        B, NPATCH, D, H = (64, 197, 192, 768)
        std = 0.02
        x = jax.random.normal(ks[0], (B, NCLS + NPATCH, D), dtype=jnp.float32)
        fc1_w = jax.random.normal(ks[1], (H, D), dtype=jnp.float32) * std
        fc1_b = jnp.zeros((H,), jnp.float32)
        fc2_w = jax.random.normal(ks[2], (D, H), dtype=jnp.float32) * std
        fc2_b = jnp.zeros((D,), jnp.float32)
        gate_pair = jax.random.normal(ks[3], (NCLS, 2, D), dtype=jnp.float32) * std
        atom_in_w = jax.random.normal(ks[4], (NATOMS, H, D), dtype=jnp.float32) * std
        atom_in_b = jax.random.normal(ks[5], (NATOMS, H), dtype=jnp.float32) * std
        atom_out_w = jax.random.normal(ks[6], (NATOMS, D, H), dtype=jnp.float32) * std
        atom_out_b = jax.random.normal(ks[7], (NATOMS, D), dtype=jnp.float32) * std
        balance_bias = jnp.zeros((NCLS, 2), jnp.float32)
        return {'x': x, 'fc1_w': fc1_w, 'fc1_b': fc1_b, 'fc2_w': fc2_w, 'fc2_b': fc2_b, 'gate_pair': gate_pair, 'atom_in_w': atom_in_w, 'atom_in_b': atom_in_b, 'atom_out_w': atom_out_w, 'atom_out_b': atom_out_b, 'balance_bias': balance_bias}
    _L0_ffn_all = _L0_ffn_setup()
    _L0_ffn_in = {k: v for k, v in _L0_ffn_all.items() if k in ('fc1_w', 'fc1_b', 'fc2_w', 'fc2_b', 'gate_pair', 'atom_in_w', 'atom_in_b', 'atom_out_w', 'atom_out_b', 'balance_bias')}
    del _L0_ffn_all

    def _L1_attn_setup():
        import jax, jax.numpy as jnp
        import numpy as np
        ATTN_DIM = 192
        NEG = -1000000000.0
        key = jax.random.key(seed)
        x = jax.random.normal(key, (4, 1024, ATTN_DIM), dtype=jnp.float32)
        return {'x': x}
    _L1_attn_all = _L1_attn_setup()
    _L1_attn_in = {k: v for k, v in _L1_attn_all.items() if k in ()}
    del _L1_attn_all

    def _L1_ffn_setup():
        import jax, jax.numpy as jnp
        import numpy as np
        B, S, D = (4, 256, 192)
        E = 8
        H = 192
        HS = 768
        TOPK_ROUTED = 2
        key = jax.random.key(seed)
        ks = jax.random.split(key, 10)
        w = lambda k, shape: jax.random.normal(k, shape, dtype=jnp.float32) * 0.02
        return {'x': jax.random.normal(ks[0], (B, S, D), dtype=jnp.float32), 'router_w': w(ks[1], (D, E)), 'w_gate': w(ks[2], (E, D, H)), 'w_up': w(ks[3], (E, D, H)), 'w_down': w(ks[4], (E, H, D)), 'ws_gate': w(ks[5], (D, HS)), 'ws_up': w(ks[6], (D, HS)), 'ws_down': w(ks[7], (HS, D)), 'sg_w': w(ks[8], (D, 1)), 'sg_b': jnp.zeros((1,), jnp.float32)}
    _L1_ffn_all = _L1_ffn_setup()
    _L1_ffn_in = {k: v for k, v in _L1_ffn_all.items() if k in ('router_w', 'w_gate', 'w_up', 'w_down', 'ws_gate', 'ws_up', 'ws_down', 'sg_w', 'sg_b')}
    del _L1_ffn_all
    return {'x': x, 'L0_tok_quantum_params': _L0_tok_in['quantum_params'], 'L0_tok_post_w': _L0_tok_in['post_w'], 'L0_tok_post_b': _L0_tok_in['post_b'], 'L0_attn_wqkv_r': _L0_attn_in['wqkv_r'], 'L0_attn_wqkv_i': _L0_attn_in['wqkv_i'], 'L0_attn_wqkv_j': _L0_attn_in['wqkv_j'], 'L0_attn_wqkv_k': _L0_attn_in['wqkv_k'], 'L0_attn_wp_r': _L0_attn_in['wp_r'], 'L0_attn_wp_i': _L0_attn_in['wp_i'], 'L0_attn_wp_j': _L0_attn_in['wp_j'], 'L0_attn_wp_k': _L0_attn_in['wp_k'], 'L0_attn_bp': _L0_attn_in['bp'], 'L0_ffn_fc1_w': _L0_ffn_in['fc1_w'], 'L0_ffn_fc1_b': _L0_ffn_in['fc1_b'], 'L0_ffn_fc2_w': _L0_ffn_in['fc2_w'], 'L0_ffn_fc2_b': _L0_ffn_in['fc2_b'], 'L0_ffn_gate_pair': _L0_ffn_in['gate_pair'], 'L0_ffn_atom_in_w': _L0_ffn_in['atom_in_w'], 'L0_ffn_atom_in_b': _L0_ffn_in['atom_in_b'], 'L0_ffn_atom_out_w': _L0_ffn_in['atom_out_w'], 'L0_ffn_atom_out_b': _L0_ffn_in['atom_out_b'], 'L0_ffn_balance_bias': _L0_ffn_in['balance_bias'], 'L1_ffn_router_w': _L1_ffn_in['router_w'], 'L1_ffn_w_gate': _L1_ffn_in['w_gate'], 'L1_ffn_w_up': _L1_ffn_in['w_up'], 'L1_ffn_w_down': _L1_ffn_in['w_down'], 'L1_ffn_ws_gate': _L1_ffn_in['ws_gate'], 'L1_ffn_ws_up': _L1_ffn_in['ws_up'], 'L1_ffn_ws_down': _L1_ffn_in['ws_down'], 'L1_ffn_sg_w': _L1_ffn_in['sg_w'], 'L1_ffn_sg_b': _L1_ffn_in['sg_b']}

def reference(x, L0_tok_quantum_params, L0_tok_post_w, L0_tok_post_b, L0_attn_wqkv_r, L0_attn_wqkv_i, L0_attn_wqkv_j, L0_attn_wqkv_k, L0_attn_wp_r, L0_attn_wp_i, L0_attn_wp_j, L0_attn_wp_k, L0_attn_bp, L0_ffn_fc1_w, L0_ffn_fc1_b, L0_ffn_fc2_w, L0_ffn_fc2_b, L0_ffn_gate_pair, L0_ffn_atom_in_w, L0_ffn_atom_in_b, L0_ffn_atom_out_w, L0_ffn_atom_out_b, L0_ffn_balance_bias, L1_ffn_router_w, L1_ffn_w_gate, L1_ffn_w_up, L1_ffn_w_down, L1_ffn_ws_gate, L1_ffn_ws_up, L1_ffn_ws_down, L1_ffn_sg_w, L1_ffn_sg_b):
    import jax
    import jax.numpy as jnp

    def _L0_tok_ref(token_ids, quantum_params, post_w, post_b):
        import jax, jax.numpy as jnp
        import numpy as np
        N_QUBITS = 6
        N_LAYERS = 3
        DIM = 1 << N_QUBITS
        VOCAB = 8000
        EMBED = 192
        B, S = (16, 1024)

        def _cnot_perm(control, target):
            idx = np.arange(DIM)
            cbit = idx >> N_QUBITS - 1 - control & 1
            flipped = idx ^ 1 << N_QUBITS - 1 - target
            return np.where(cbit == 1, flipped, idx)
        _idx = np.arange(DIM)
        Z_SIGNS = np.stack([1.0 - 2.0 * (_idx >> N_QUBITS - 1 - q & 1) for q in range(N_QUBITS)], axis=1).astype(np.float32)

        def _apply_ry(state, theta, q):
            T = state.shape[0]
            left, right = (1 << q, 1 << N_QUBITS - 1 - q)
            s = state.reshape(T, left, 2, right)
            c = jnp.cos(theta * 0.5)[:, None, None]
            sn = jnp.sin(theta * 0.5)[:, None, None]
            a0, a1 = (s[:, :, 0, :], s[:, :, 1, :])
            out = jnp.stack([c * a0 - sn * a1, sn * a0 + c * a1], axis=2)
            return out.reshape(T, DIM)

        def _apply_rz(state, theta, q):
            T = state.shape[0]
            left, right = (1 << q, 1 << N_QUBITS - 1 - q)
            s = state.reshape(T, left, 2, right)
            ph = jnp.exp(1j * (theta * 0.5)).astype(state.dtype)[:, None, None]
            out = jnp.stack([jnp.conj(ph) * s[:, :, 0, :], ph * s[:, :, 1, :]], axis=2)
            return out.reshape(T, DIM)

        def _circuit_expvals(params):
            T = params.shape[0]
            state = jnp.zeros((T, DIM), dtype=jnp.complex64).at[:, 0].set(1.0)
            for layer in range(N_LAYERS):
                for q in range(N_QUBITS):
                    state = _apply_ry(state, params[:, layer, q, 0], q)
                    state = _apply_rz(state, params[:, layer, q, 1], q)
                if layer < N_LAYERS - 1:
                    for q in range(N_QUBITS - 1):
                        state = state[:, _cnot_perm(q, q + 1)]
                    if N_QUBITS > 2:
                        state = state[:, _cnot_perm(N_QUBITS - 1, 0)]
            probs = state.real ** 2 + state.imag ** 2
            return probs @ jnp.asarray(Z_SIGNS)
        b, s = token_ids.shape
        params = quantum_params[token_ids.reshape(-1)]
        ev = _circuit_expvals(params)
        emb = ev @ post_w.T + post_b
        return emb.reshape(b, s, -1)

    def _L0_attn_ref(x, wqkv_r, wqkv_i, wqkv_j, wqkv_k, wp_r, wp_i, wp_j, wp_k, bp):
        import jax, jax.numpy as jnp
        import numpy as np
        B, N, DIM, H = (4, 256, 192, 8)
        HD = DIM // H

        def qlinear(x, wr, wi, wj, wk, b=None):
            xr, xi, xj, xk = jnp.split(x, 4, axis=-1)
            r = xr @ wr - xi @ wi - xj @ wj - xk @ wk
            i = xr @ wi + xi @ wr + xj @ wk - xk @ wj
            j = xr @ wj - xi @ wk + xj @ wr + xk @ wi
            k = xr @ wk + xi @ wj - xj @ wi + xk @ wr
            out = jnp.concatenate([r, i, j, k], axis=-1)
            return out + b if b is not None else out
        Bb, Nn, C = x.shape
        hd = C // H
        qkv = qlinear(x, wqkv_r, wqkv_i, wqkv_j, wqkv_k)
        qkv = qkv.reshape(Bb, Nn, 3, H, hd).transpose(2, 0, 3, 1, 4)
        q, k, v = (qkv[0], qkv[1], qkv[2])
        q = q * hd ** (-0.5)
        qr, qi, qj, qk_ = jnp.split(q, 4, axis=-1)
        kr, ki, kj, kk = jnp.split(k, 4, axis=-1)
        mm = lambda a, b: jnp.einsum('bhnd,bhmd->bhnm', a, b)
        sr = mm(qr, kr) - mm(qi, ki) - mm(qj, kj) - mm(qk_, kk)
        si = mm(qr, ki) + mm(qi, kr) + mm(qj, kk) - mm(qk_, kj)
        sj = mm(qr, kj) - mm(qi, kk) + mm(qj, kr) + mm(qk_, ki)
        sk = mm(qr, kk) + mm(qi, kj) - mm(qj, ki) + mm(qk_, kr)
        ar = jax.nn.softmax(sr, axis=-1)
        ai = jax.nn.softmax(si, axis=-1)
        aj = jax.nn.softmax(sj, axis=-1)
        ak = jax.nn.softmax(sk, axis=-1)
        vr, vi, vj, vk = jnp.split(v, 4, axis=-1)
        o_r = ar @ vr - ai @ vi - aj @ vj - ak @ vk
        o_i = ar @ vi + ai @ vr + aj @ vk - ak @ vj
        o_j = ar @ vj - ai @ vk + aj @ vr + ak @ vi
        o_k = ar @ vk + ai @ vj - aj @ vi + ak @ vr
        out = jnp.concatenate([o_r, o_i, o_j, o_k], axis=-1)
        out = out.transpose(0, 2, 1, 3).reshape(Bb, Nn, C)
        return qlinear(out, wp_r, wp_i, wp_j, wp_k, bp)

    def _L0_ffn_ref(x, fc1_w, fc1_b, fc2_w, fc2_b, gate_pair, atom_in_w, atom_in_b, atom_out_w, atom_out_b, balance_bias):
        import jax, jax.numpy as jnp
        import numpy as np
        ATOM = {'vm': 0, 'im': 1, 'cm': 2, 'sc': 3, 'cc': 4}
        TASK_PAIRS = [('vm', 'sc'), ('vm', 'cc'), ('im', 'sc'), ('im', 'cc'), ('cm', 'sc'), ('cm', 'cc')]
        SRC_IDX = np.array([[ATOM[l], ATOM[r]] for l, r in TASK_PAIRS], dtype=np.int32)
        DST_IDX = np.array([[ATOM[r], ATOM[l]] for l, r in TASK_PAIRS], dtype=np.int32)
        NCLS = 6
        NATOMS = 5

        def _l2norm(x, eps=1e-12):
            return x / jnp.clip(jnp.linalg.norm(x, axis=-1, keepdims=True), eps)
        src = jnp.asarray(SRC_IDX)
        dst = jnp.asarray(DST_IDX)
        D = x.shape[-1]
        H = atom_in_w.shape[1]
        cls_tokens = x[:, :NCLS]
        patch_tokens = x[:, NCLS:]
        patch_out = jax.nn.gelu(patch_tokens @ fc1_w.T + fc1_b, approximate=False) @ fc2_w.T + fc2_b
        gate_in = _l2norm(cls_tokens.astype(jnp.float32))
        gate_w = _l2norm(gate_pair.astype(jnp.float32))
        gate_logits = jnp.einsum('bnd,nrd->bnr', gate_in, gate_w) + balance_bias[None]
        route_probs = jax.nn.softmax(gate_logits, axis=-1)
        chosen_route = jnp.argmax(route_probs, axis=-1)
        hid_all = jax.nn.gelu(jnp.einsum('bnd,ahd->bnah', cls_tokens, atom_in_w) + atom_in_b[None, None], approximate=False)
        sh_pair = hid_all[:, jnp.arange(NCLS)[:, None], src, :]
        route_out_w = atom_out_w[dst.reshape(-1)].reshape(NCLS, 2, D, H)
        route_candidates = jnp.einsum('bnrh,nrdh->bnrd', sh_pair, route_out_w) + atom_out_b[dst][None]
        chosen_w = jnp.take_along_axis(route_probs, chosen_route[..., None], axis=-1)
        chosen_cand = jnp.take_along_axis(route_candidates, chosen_route[:, :, None, None], axis=2)[:, :, 0]
        cls_out = chosen_cand * chosen_w.astype(chosen_cand.dtype)
        return jnp.concatenate([cls_out, patch_out], axis=1)

    def _L1_attn_ref(x):
        import jax, jax.numpy as jnp
        import numpy as np
        ATTN_DIM = 192
        NEG = -1000000000.0
        B, S, D = x.shape
        scores = jnp.einsum('bsd,btd->bst', x, x) / jnp.sqrt(jnp.float32(D))
        row = jax.lax.broadcasted_iota(jnp.int32, (S, S), 0)
        col = jax.lax.broadcasted_iota(jnp.int32, (S, S), 1)
        causal = col <= row
        scores = jnp.where(causal[None, :, :], scores, NEG)
        attn = jax.nn.softmax(scores, axis=-1)
        out = jnp.einsum('bst,btd->bsd', attn, x)
        return out

    def _L1_ffn_ref(x, router_w, w_gate, w_up, w_down, ws_gate, ws_up, ws_down, sg_w, sg_b):
        import jax, jax.numpy as jnp
        import numpy as np
        B, S, D = (4, 256, 192)
        E = 8
        H = 192
        HS = 768
        TOPK_ROUTED = 2
        probs = jax.nn.softmax(x @ router_w, axis=-1)
        gates, idx = jax.lax.top_k(probs, TOPK_ROUTED)
        gates = gates / jnp.sum(gates, axis=-1, keepdims=True)
        n_exp = router_w.shape[1]
        dense_g = jnp.sum(jax.nn.one_hot(idx, n_exp, dtype=x.dtype) * gates[..., None], axis=-2)
        g = jax.nn.silu(jnp.einsum('bsd,edh->bseh', x, w_gate))
        u = jnp.einsum('bsd,edh->bseh', x, w_up)
        expert_out = jnp.einsum('bseh,ehd->bsed', g * u, w_down)
        routed = jnp.einsum('bse,bsed->bsd', dense_g, expert_out)
        shared = jax.nn.silu(x @ ws_gate) * (x @ ws_up) @ ws_down
        alpha = jax.nn.sigmoid(x @ sg_w + sg_b)
        return alpha * shared + (1.0 - alpha) * routed
    h = _L0_tok_ref(x, L0_tok_quantum_params, L0_tok_post_w, L0_tok_post_b)
    h = h + _L0_attn_ref(_layernorm(h, axis=-1), L0_attn_wqkv_r, L0_attn_wqkv_i, L0_attn_wqkv_j, L0_attn_wqkv_k, L0_attn_wp_r, L0_attn_wp_i, L0_attn_wp_j, L0_attn_wp_k, L0_attn_bp)
    h = h + _L0_ffn_ref(_layernorm(h, axis=-1), L0_ffn_fc1_w, L0_ffn_fc1_b, L0_ffn_fc2_w, L0_ffn_fc2_b, L0_ffn_gate_pair, L0_ffn_atom_in_w, L0_ffn_atom_in_b, L0_ffn_atom_out_w, L0_ffn_atom_out_b, L0_ffn_balance_bias)
    h = h + _L1_attn_ref(_layernorm(h, axis=-1))
    h = h + _L1_ffn_ref(_layernorm(h, axis=-1), L1_ffn_router_w, L1_ffn_w_gate, L1_ffn_w_up, L1_ffn_w_down, L1_ffn_ws_gate, L1_ffn_ws_up, L1_ffn_ws_down, L1_ffn_sg_w, L1_ffn_sg_b)
    return h

_drawn_inputs = setup_inputs


def setup_inputs(seed=0):
    import zlib

    import numpy as np

    out = dict(_drawn_inputs(seed))
    spreads = {'L0_attn_bp': (0.0, 0.1),
     'L0_ffn_fc1_b': (0.0, 0.1),
     'L0_ffn_fc2_b': (0.0, 0.1),
     'L0_ffn_balance_bias': (0.0, 0.8)}
    factors = {'L0_tok_quantum_params': 5.379,
     'L0_tok_post_b': 5.856,
     'L0_ffn_gate_pair': 64.0,
     'L0_ffn_atom_in_w': 8.0,
     'L0_ffn_atom_in_b': 8.0,
     'L0_ffn_atom_out_w': 8.0,
     'L0_ffn_atom_out_b': 34.307,
     'L1_ffn_router_w': 8.0,
     'L1_ffn_w_gate': 8.0,
     'L1_ffn_w_up': 8.0,
     'L1_ffn_w_down': 8.0,
     'L1_ffn_ws_gate': 8.0,
     'L1_ffn_ws_up': 8.0,
     'L1_ffn_ws_down': 8.0,
     'L1_ffn_sg_w': 8.0}
    for name, (base, spread) in spreads.items():
        noise = np.random.default_rng([zlib.crc32(name.encode()), seed]).standard_normal(out[name].shape)
        drawn = base * np.exp(spread * noise) if base else spread * noise
        out[name] = jnp.asarray(drawn.astype(out[name].dtype))
    for name, factor in factors.items():
        out[name] = (out[name] * factor).astype(out[name].dtype)
    return out
```

```python
import math
from contextlib import ExitStack

import numpy as np
import concourse.bass as bass
from concourse import mybir
from concourse.alu_op_type import AluOpType as ALU

F32 = mybir.dt.float32
F32R = mybir.dt.float32r
I32 = mybir.dt.int32
ACT = mybir.ActivationFunctionType
AX = mybir.AxisListType

P = 128
B, SEQ, D = 8, 256, 192
TPB = SEQ // P
NT = B * TPB
DA, DB = P, D - P
NQ, NL = 6, 3
NANG = NL * 2 * NQ
VOCAB = 8000
EPS = 1e-5
TWO_PI = 2.0 * math.pi
PI_SAFE = 3.1415925
ROUND = 1.5 * 2.0 ** 23
TWO_PI_HI = 6.28125
TWO_PI_LO = TWO_PI - TWO_PI_HI
EVW = 32
NBANK = 512


def angle(layer, rz, q0=0, n=NQ):
    at = (2 * layer + rz) * NQ + q0
    return slice(at, at + n)


class Chain:

    def __init__(self, eng, sem):
        self.eng, self.sem, self.n = eng, sem, 0

    def __call__(self, ins):
        self.n += 1
        ins.then_inc(self.sem, 1)
        self.eng.wait_ge(self.sem, self.n)

    def go(self, ins):
        self.n += 1
        ins.then_inc(self.sem, 1)
        return self.n

    def after(self, n):
        self.eng.wait_ge(self.sem, n)


def statistics_on_vector(eng, link, sem, buf, stage):
    H, st, mv, rstd, nmr = buf["H"], buf["st"], buf["mv"], buf["rstd"], buf["nmr"]
    for t in range(NT):
        n = link.go(eng.bn_stats(st[:, t, :], H[:, t, :]))
    for t in range(NT):
        link.after(n - NT + 1 + t)
        m = link.go(eng.bn_aggr(mv[:, t, :], st[:, t, :]))
    link.after(m)
    eng.tensor_scalar(rstd[:, :], mv[:, :, 1], EPS, None, ALU.add).then_inc(sem["var_ready"], 1)
    eng.wait_ge(sem["std_ready"], stage + 1)
    link(eng.reciprocal(rstd[:, :], rstd[:, :]))
    link(eng.scalar_tensor_tensor(nmr[:, :], mv[:, :, 0], -1.0, rstd[:, :], ALU.mult, ALU.mult))


def root_on_scalar(eng, sem, buf, stage):
    eng.wait_ge(sem["var_ready"], stage + 1)
    eng.activation(buf["rstd"][:, :], buf["rstd"][:, :], ACT.Sqrt).then_inc(sem["std_ready"], 1)


def circuit_on_vector(eng, link, sem, buf):
    v = eng
    T16 = NT
    theta, red, sn, cs = buf["theta"], buf["red"], buf["sn"], buf["cs"]
    R, ZM, XP, W, U, M = buf["R"], buf["ZM"], buf["XP"], buf["W"], buf["U"], buf["M"]
    E, PP, TZ, G, OZ, OX, evp = buf["E"], buf["PP"], buf["TZ"], buf["G"], buf["OZ"], buf["OX"], buf["evp"]

    def mul(o, a, b):
        link(v.tensor_tensor(o, a, b, ALU.mult))

    def add(o, a, b):
        link(v.tensor_tensor(o, a, b, ALU.add))

    def neg(o, a):
        link(v.tensor_scalar(o, a, -1.0, None, ALU.mult))

    def wide(a, shape):
        return a.broadcast_to(shape)

    link(v.memset(W[:, :, :, :], 0.0))
    link(v.memset(evp[:, :, :], 0.0))
    link(v.memset(evp[:, :, NQ:NQ + 1], 1.0))
    v_theta = theta[:, :, :]
    v.wait_ge(sem["theta_in"], 16 * NT)
    link(v.tensor_scalar(red[:, 1, :, :].rearrange("p c t -> p t c"), v_theta, 1.0 / TWO_PI, ROUND, ALU.mult, ALU.add))
    link(v.tensor_scalar(red[:, 1, :, :], red[:, 1, :, :], -ROUND, None, ALU.add))
    link(v.scalar_tensor_tensor(red[:, 0, :, :].rearrange("p c t -> p t c"), red[:, 1, :, :].rearrange("p c t -> p t c"),
                                -TWO_PI_HI, v_theta, ALU.mult, ALU.add))
    link(v.scalar_tensor_tensor(red[:, 0, :, :], red[:, 1, :, :], -TWO_PI_LO, red[:, 0, :, :], ALU.mult, ALU.add))
    link(v.tensor_scalar(red[:, 0, :, :], red[:, 0, :, :], PI_SAFE, -PI_SAFE, ALU.min, ALU.max))
    link(v.scalar_tensor_tensor(red[:, 1, :, :], red[:, 0, :, :], -1.0, red[:, 0, :, :], ALU.mult, ALU.min))
    v.tensor_scalar(red[:, 1, :, :], red[:, 1, :, :], math.pi / 2, None, ALU.add).then_inc(sem["angles_ready"], 1)

    v.wait_ge(sem["trig_ready"], 2)
    mul(R[:, 0, :, :], sn[:, angle(0, 0), :], cs[:, angle(0, 1), :])
    mul(R[:, 1, :, :], sn[:, angle(0, 0), :], sn[:, angle(0, 1), :])
    link(v.tensor_copy(R[:, 2, :, :], cs[:, angle(0, 0), :]))
    neg(R[:, 3, :, :], R[:, 1, :, :])
    neg(R[:, 4, :, :], R[:, 0, :, :])
    rX, rY, rZ, nrY, nrX = (R[:, i, :, :] for i in range(5))
    link(v.tensor_copy(ZM[:, 0, :, :], cs[:, angle(1, 0), :]))
    neg(ZM[:, 1, :, :], sn[:, angle(1, 0), :])
    neg(ZM[:, 2, :, :], sn[:, angle(1, 0), :])
    link(v.tensor_copy(ZM[:, 3, :, :], cs[:, angle(1, 0), :]))
    zZ, zX = ZM[:, 0, :, :], ZM[:, 1, :, :]
    mul(XP[:, 0, :, :], cs[:, angle(1, 1), :], cs[:, angle(1, 0), :])
    neg(XP[:, 1, :, :], sn[:, angle(1, 1), :])
    mul(XP[:, 2, :, :], cs[:, angle(1, 1), :], sn[:, angle(1, 0), :])
    link(v.tensor_copy(XP[:, 3, :, :], sn[:, angle(1, 1), :]))
    xX, xY, xZ, nxY = (XP[:, i, :, :] for i in range(4))

    link(v.memset(TZ[:, 3, :], 1.0))
    link(v.tensor_copy(TZ[:, 2, :], rZ[:, 5, :]))
    mul(TZ[:, 1, :], TZ[:, 2, :], rZ[:, 4, :])
    mul(TZ[:, 0, :], TZ[:, 1, :], rZ[:, 3, :])

    mul(W[:, 1, 8:0:-2, :], zX[:, 1:5, :], rX[:, 2:6, :])
    link(v.tensor_copy(W[:, 3, 8:0:-2, :], zZ[:, 1:5, :]))
    mul(G[:, 0:4, :], zZ[:, 1:5, :], rZ[:, 2:6, :])
    mul(W[:, 0, 9:1:-2, :], G[:, 0:4, :], TZ[:, :, :])
    mul(G[:, 0:4, :], zX[:, 1:5, :], nrY[:, 2:6, :])
    mul(W[:, 2, 9:1:-2, :], G[:, 0:4, :], TZ[:, :, :])
    link(v.tensor_copy(W[:, 1, 0, :], zX[:, 4, :]))
    mul(W[:, 3, 0, :], zZ[:, 4, :], rX[:, 5, :])
    mul(W[:, 0, 1, :], zZ[:, 4, :], rY[:, 5, :])
    mul(W[:, 2, 1, :], zX[:, 4, :], rZ[:, 5, :])
    mul(W[:, 1:3, 10, :], XP[:, 0:2, 1, :], wide(rX[:, 2, :].unsqueeze(1), [P, 2, T16]))
    link(v.tensor_copy(W[:, 3, 10, :], xZ[:, 1, :]))
    mul(W[:, 0, 11, :], xZ[:, 1, :], rZ[:, 2, :])
    mul(W[:, 1, 11, :], xY[:, 1, :], rY[:, 2, :])
    mul(W[:, 2, 11, :], xX[:, 1, :], nrY[:, 2, :])

    def contract(q, n):
        mul(M[:, 0:2, 0:n, :], W[:, 1::-1, 0:n, :], wide(rX[:, q, :].unsqueeze(1).unsqueeze(1), [P, 2, n, T16]))
        add(U[:, 3:0:-2, 0:n, :], W[:, 0:2, 0:n, :], M[:, 0:2, 0:n, :])
        mul(M[:, 0:2, 0:n, :], W[:, 2:4, 0:n, :], wide(R[:, 1:3, q, :].unsqueeze(2), [P, 2, n, T16]))
        mul(M[:, 2:4, 0:n, :], W[:, 2:4, 0:n, :], wide(R[:, 2:4, q, :].unsqueeze(2), [P, 2, n, T16]))
        add(U[:, 0:3:2, 0:n, :], M[:, 0:4:2, 0:n, :], M[:, 1:4:2, 0:n, :])

    for q in (3, 2, 1):
        n = 4 + 2 * (3 - q)
        contract(q + 1, n)
        mul(W[:, :, 0:n, :], U[:, :, 0:n, :], wide(ZM[:, :, q, :].unsqueeze(2), [P, 4, n, T16]))
    contract(1, 12)
    mul(M[:, 0:2, :, :], U[:, 0:4:3, :, :], wide(rZ[:, 0, :].unsqueeze(1).unsqueeze(1), [P, 2, 12, T16]))
    add(E[:, 0:2, :, :], U[:, 3::-3, :, :], M[:, 0:2, :, :])
    mul(M[:, 0:2, :, :], U[:, 1:3, :, :], wide(R[:, 0:2, 0, :].unsqueeze(2), [P, 2, 12, T16]))
    add(E[:, 2, :, :], M[:, 0, :, :], M[:, 1, :, :])
    mul(M[:, 0:2, :, :], U[:, 1:3, :, :], wide(R[:, 1:5:3, 0, :].unsqueeze(2), [P, 2, 12, T16]))
    add(E[:, 3, :, :], M[:, 0, :, :], M[:, 1, :, :])
    E_I, E_Z, E_X, E_Y = (E[:, i, :, :] for i in range(4))
    X4, Y4, I4, Z4, P1, T1 = 0, 1, 2, 3, 10, 11

    def dot(o, pairs, g=0):
        for n, (a, b) in enumerate(pairs):
            mul(o if n == 0 else G[:, g, :], a, b)
            if n:
                add(o, o, G[:, g, :])

    mul(G[:, 0:4, :], E_X[:, 8:0:-2, :], wide(zX[:, 0, :].unsqueeze(1), [P, 4, T16]))
    mul(G[:, 4:8, :], E_Z[:, 9:1:-2, :], wide(zZ[:, 0, :].unsqueeze(1), [P, 4, T16]))
    add(OZ[:, 1:5, :], G[:, 0:4, :], G[:, 4:8, :])
    dot(OZ[:, 0, :], [(zZ[:, 5, :], E_I[:, Z4, :]), (zX[:, 5, :], E_X[:, X4, :])])
    dot(G[:, 1, :], [(zX[:, 0, :], E_X[:, Z4, :]), (zZ[:, 0, :], E_Z[:, I4, :])])
    mul(G[:, 2, :], zX[:, 0, :], E_I[:, X4, :])
    mul(G[:, 3, :], zZ[:, 0, :], E_Y[:, Y4, :])
    link(v.tensor_tensor(G[:, 2, :], G[:, 2, :], G[:, 3, :], ALU.subtract))
    dot(OZ[:, 5, :], [(zZ[:, 5, :], G[:, 1, :]), (zX[:, 5, :], G[:, 2, :])])

    mul(PP[:, 0:2, 0:3, :], XP[:, 0:2, 2:5, :], wide(rX[:, 3:6, :].unsqueeze(1), [P, 2, 3, T16]))
    link(v.tensor_copy(PP[:, 2, 0:3, :], xZ[:, 2:5, :]))
    link(v.tensor_copy(PP[:, 0:2, 3, :], XP[:, 0:2, 5, :]))
    link(v.memset(PP[:, 2, 3, :], 0.0))
    pA, pB, pD = G[:, 8:12, :], G[:, 12:16, :], G[:, 16:20, :]
    pC = PP[:, 0, :, :]
    t0, t1 = G[:, 0:4, :], G[:, 4:8, :]
    vI, vX, vY, vZ = (G[:, 20 + 4 * i:24 + 4 * i, :] for i in range(4))
    mul(pA, PP[:, 0, :, :], rX[:, 2:6, :])
    mul(t0, PP[:, 1, :, :], rY[:, 2:6, :])
    mul(t1, PP[:, 2, :, :], rZ[:, 2:6, :])
    add(pB, t0, t1)
    mul(t0, PP[:, 1, :, :], rZ[:, 2:6, :])
    mul(t1, PP[:, 2, :, :], nrY[:, 2:6, :])
    add(pD, t0, t1)
    mul(vI, xZ[:, 1:5, :], pB)
    mul(vZ, xZ[:, 1:5, :], pA)
    mul(t0, xX[:, 1:5, :], pC)
    mul(t1, nxY[:, 1:5, :], pD)
    add(vX, t0, t1)
    mul(t0, xY[:, 1:5, :], pC)
    mul(t1, xX[:, 1:5, :], pD)
    add(vY, t0, t1)
    mul(t0, vX, rX[:, 1:5, :])
    add(pA, vI, t0)
    mul(t0, vY, rY[:, 1:5, :])
    mul(t1, vZ, rZ[:, 1:5, :])
    add(pB, t0, t1)
    CZ = G[:, 36:40, :]
    link(v.tensor_copy(CZ[:, 0, :], rZ[:, 0, :]))
    for q in (1, 2, 3):
        mul(CZ[:, q, :], CZ[:, q - 1, :], rZ[:, q, :])
    mul(t0[:, 0:3, :], pB[:, 0:3, :], CZ[:, 0:3, :])
    add(OX[:, 1:4, :], pA[:, 0:3, :], t0[:, 0:3, :])
    s = [G[:, 40 + i, :] for i in range(8)]
    mul(s[0], pA[:, 3, :], rX[:, 1, :])
    mul(s[0], s[0], rX[:, 0, :])
    mul(s[1], rZ[:, 3, :], rZ[:, 2, :])
    mul(s[1], s[1], pB[:, 3, :])
    mul(s[1], s[1], nrY[:, 1, :])
    mul(s[1], s[1], rY[:, 0, :])
    add(OX[:, 4, :], s[0], s[1])
    mul(s[0], xY[:, 4, :], rY[:, 5, :])
    mul(s[0], s[0], rX[:, 4, :])
    mul(s[1], xZ[:, 4, :], rZ[:, 5, :])
    add(s[0], s[0], s[1])
    mul(s[1], xX[:, 4, :], nrY[:, 5, :])
    mul(s[1], s[1], rY[:, 4, :])
    mul(s[1], s[1], CZ[:, 3, :])
    add(s[0], s[0], s[1])
    mul(s[0], s[0], xZ[:, 5, :])
    add(OX[:, 4, :], OX[:, 4, :], s[0])
    zeta, zeta5 = s[2], s[3]
    mul(zeta, rZ[:, 4, :], rZ[:, 3, :])
    mul(zeta5, zeta, rZ[:, 5, :])
    dot(s[4], [(xY[:, 0, :], E_Y[:, T1, :]), (xZ[:, 0, :], E_Z[:, T1, :])])
    dot(OX[:, 0, :], [(xX[:, 0, :], E_X[:, P1, :]), (zeta5, s[4])])
    dot(s[4], [(xY[:, 0, :], E_Y[:, P1, :]), (xZ[:, 0, :], E_Z[:, P1, :])])
    mul(s[5], xX[:, 0, :], zeta5)
    mul(s[5], s[5], E_X[:, T1, :])
    add(s[4], s[4], s[5])
    mul(OX[:, 5, :], xZ[:, 5, :], s[4])
    mul(s[5], zeta, rY[:, 5, :])
    mul(s[4], s[5], E_I[:, T1, :])
    mul(s[4], s[4], xY[:, 5, :])
    mul(s[6], rX[:, 5, :], E_I[:, P1, :])
    mul(s[6], s[6], xX[:, 5, :])
    add(s[4], s[4], s[6])
    mul(s[4], s[4], xX[:, 0, :])
    add(OX[:, 5, :], OX[:, 5, :], s[4])
    mul(s[4], xY[:, 0, :], E_Z[:, P1, :])
    mul(s[6], xZ[:, 0, :], E_Y[:, P1, :])
    link(v.tensor_tensor(s[4], s[4], s[6], ALU.subtract))
    mul(s[4], s[4], nxY[:, 5, :])
    mul(s[4], s[4], rX[:, 5, :])
    add(OX[:, 5, :], OX[:, 5, :], s[4])
    mul(s[4], xY[:, 0, :], E_Z[:, T1, :])
    mul(s[6], xZ[:, 0, :], E_Y[:, T1, :])
    link(v.tensor_tensor(s[4], s[4], s[6], ALU.subtract))
    mul(s[4], s[4], xX[:, 5, :])
    mul(s[4], s[4], s[5])
    add(OX[:, 5, :], OX[:, 5, :], s[4])

    mul(OZ[:, :, :], OZ[:, :, :], cs[:, angle(2, 0), :])
    mul(OX[:, :, :], OX[:, :, :], sn[:, angle(2, 0), :])
    v.tensor_tensor(evp[:, :, 0:NQ].rearrange("p t q -> p q t"), OZ[:, :, :], OX[:, :, :],
                    ALU.subtract).then_inc(sem["ev_ready"], 1)
NH, HD, NC = 8, 24, 4
QD = HD // NC
NU = NC + 1
HG = 4
SROW = 3 * 32 + HD
BIAS_ROWS = 2
VBLK = 32
VPAD = P - VBLK
QSIGN = [[1, -1, -1, -1], [1, 1, -1, 1], [1, 1, 1, -1], [1, -1, 1, 1]]
VSIGN = [[1, 1, 1, 1], [1, -1, 1, -1], [1, -1, -1, 1], [1, 1, -1, -1]]
LSIGN = [[1, 1, 1, 1], [-1, 1, -1, 1], [-1, 1, 1, -1], [-1, -1, 1, 1]]
NQKV = 2 * NU * P + D
BANK_MAX, BANK_EXP, BANK_AV, BANK_MISC = 0, 2, 6, 7


def misc_uses():
    at, n = {}, 0
    for i in range(-2, B):
        for h in range(NH):
            for item in misc_items(i, h):
                at[item] = n
                n += 1
        for item in tail_items(i):
            at[item] = n
            n += 1
    return at


def misc_items(i, h):
    items = []
    if i + 2 < B:
        items += {0: [("x", i + 2)], 2: [("u", i + 2, 0), ("u", i + 2, 1)], 3: [("u", i + 2, 2), ("u", i + 2, 3)],
                  4: [("u", i + 2, 4), ("v", i + 2)]}.get(h, [])
    if i >= 0 and h in (3, 5, 7):
        items.append(("pair", i, (h - 3) // 2))
    return items


def tail_items(i):
    items = []
    if 0 <= i + 1 < B:
        items.append(("max", i + 1))
    if i >= 0:
        items += [("pair", i, 3), ("ot", i), ("proj", i)]
    return items


def attention_on_tensor(nc, eng, sem, buf, ps, base):
    use = misc_uses()
    W, xa, xb = buf["wqkv"], buf["xa"], buf["xb"]
    QK, VS, PT, OTs, ident = buf["QK"], buf["VS"], buf["PT"], buf["OTs"], buf["ident"]
    misc = ps[:, BANK_MISC, :]

    def claim(item):
        if use[item] > 0:
            eng.wait_ge(sem["misc_free"], use[item])

    def five(out, sets, x, stationary_is_weight, ins=None):
        pairs = [(sets[0], x[0]), (sets[1], x[0]), (sets[0], x[1]), (sets[2], x[2]), (sets[3], x[2])]
        for n, (w, xx) in enumerate(pairs):
            a, b = (w, xx) if stationary_is_weight else (xx, w)
            ins = eng.matmul(out, a, b, start=n == 0, stop=n == 4)
        return ins

    def do_misc(item):
        claim(item)
        kind, b = item[0], item[1]
        if kind == "x":
            eng.wait_ge(sem["xn_ready"], b + 1)
            for t in range(TPB):
                eng.transpose(misc[:, P * t:P * t + P], buf["xn"][:, b % 2, t, 0:DA], ident[:, :])
            for t in range(TPB):
                ins = eng.transpose(misc[0:DB, SEQ + P * t:SEQ + P * t + P], buf["xn"][:, b % 2, t, DA:D], ident[:, :])
        elif kind == "u":
            eng.wait_ge(sem["xs_half"], b + 1)
            u = item[2]
            x = [xa[:, 0, :], xa[:, 1, :], xb[:, :]]
            for g in range(2):
                c = (2 * u + g) * P
                ins = five(misc[:, SEQ * g:SEQ * g + SEQ], [W[:, s, c:c + P] for s in range(4)], x, True)
        elif kind == "v":
            for t in range(TPB):
                cols = slice(P * t, P * t + P)
                x = [xa[:, 0, cols], xa[:, 1, cols], xb[:, cols]]
                ins = five(misc[:, D * t:D * t + D], [W[:, s, 2 * NU * P:NQKV] for s in range(4)], x, False)
        elif kind == "pair":
            k = item[2]
            eng.wait_ge(sem["av_out"], NH * b + 2 * k + 2)
            for hh in range(2):
                for t in range(TPB):
                    at = P * (2 * hh + t)
                    ins = eng.transpose(misc[:, at:at + P], OTs[:, (2 * k + hh) % 4, P * t:P * t + P], ident[:, :])
        elif kind == "max":
            eng.wait_ge(sem["mx_done"], 4 * NH * (b + 1))
            for t in range(TPB):
                ins = eng.transpose(misc[0:NC * NH, P * t:P * t + P], buf["mx"][:, b % 2, t, :], ident[:, :])
        elif kind == "ot":
            eng.wait_ge(sem["o_ready"], 4 * (b + 1))
            for t in range(TPB):
                eng.transpose(misc[:, P * t:P * t + P], buf["o"][:, t, 0:DA], ident[:, :])
            for t in range(TPB):
                ins = eng.transpose(misc[0:DB, SEQ + P * t:SEQ + P * t + P], buf["o"][:, t, DA:D], ident[:, :])
        elif kind == "proj":
            eng.wait_ge(sem["ot_half"], b + 1)
            for t in range(TPB):
                out = misc[:, D * t:D * t + D]
                eng.matmul(out, buf["ot"][:, P * t:P * t + P], buf["wp"][:, 0, :], start=True, stop=False)
                ins = eng.matmul(out, buf["ot"][0:DB, SEQ + P * t:SEQ + P * t + P], buf["wp"][0:DB, 1, :],
                                 start=False, stop=True)
        ins.then_inc(sem["misc_full"], 1)

    def scores_for_max(b, h):
        eng.wait_ge(sem["qk_in"][h], 96 * (b + 1))
        for k in range(4):
            t, cp = k // 2, k % 2
            n = 4 * (NH * b + h) + k
            if n >= 2:
                eng.wait_ge(sem["mx_done"], n - 1)
            for c in (2 * cp, 2 * cp + 1):
                ins = eng.matmul(ps[:, BANK_MAX + n % 2, SEQ * (c % 2):SEQ * (c % 2) + SEQ],
                                 QK[0:SROW, b % 2, c, h, P * t:P * t + P], QK[0:SROW, b % 2, NC, h, :],
                                 start=True, stop=True)
            ins.then_inc(sem["p1_full"], 1)

    def scores_for_exp(b, h):
        if h == 0:
            eng.wait_ge(sem["nm_in"], 32 * (b + 1))
        for t in range(TPB):
            n = 2 * (NH * b + h) + t
            if n >= 2:
                eng.wait_ge(sem["exp_done"], n - 1)
            for cp in range(2):
                ins = eng.matmul(ps[:, BANK_EXP + 2 * t + cp, :], QK[0:SROW + BIAS_ROWS, b % 2, NC, h, P * t:P * t + P],
                                 QK[0:SROW + BIAS_ROWS, b % 2, 2 * cp:2 * cp + 2, h, :], start=True, stop=True)
            ins.then_inc(sem["p2_full"], 1)

    def values(b, h):
        n = NH * b + h
        if h == 0:
            eng.wait_ge(sem["vs_half"], b + 1)
        eng.wait_ge(sem["exp_done"], 2 * (n + 1))
        if n:
            eng.wait_ge(sem["av_out"], n)
        for t in range(TPB):
            for c in range(NC):
                at = VPAD + P * h - VBLK * c
                ins = eng.matmul(ps[:, BANK_AV, 0:SEQ], VS[:, b % 3, t, at:at + P], PT[:, n % 2, t, c, :],
                                 start=t + c == 0, stop=t == TPB - 1 and c == NC - 1)
        ins.then_inc(sem["av_full"], 1)

    eng.wait_ge(sem["wqkv_ready"], 1)
    eng.wait_ge(sem["wp_ready"], 1)
    eng.wait_ge(sem["vs_clear"], 1)
    for i in range(-2, B):
        for h in range(NH):
            if 0 <= i + 1 < B:
                scores_for_max(i + 1, h)
            for item in misc_items(i, h):
                if item[0] != "pair":
                    do_misc(item)
            if i >= 0:
                scores_for_exp(i, h)
                if h:
                    values(i, h - 1)
            for item in misc_items(i, h):
                if item[0] == "pair":
                    do_misc(item)
        for item in tail_items(i):
            if item == ("pair", i, 3):
                values(i, NH - 1)
            do_misc(item)


def attention_on_scalar(nc, eng, sem, buf, ps, base):
    use = misc_uses()
    misc = ps[:, BANK_MISC, :]
    QK, VS, PT, OTs, HL = buf["QK"], buf["VS"], buf["PT"], buf["OTs"], buf["HL"]

    def arrive(item):
        eng.wait_ge(sem["misc_full"], use[item] + 1)

    def do_misc(item):
        kind, b = item[0], item[1]
        if kind == "x":
            arrive(item)
            if b:
                eng.wait_ge(sem["misc_full"], use[("v", b - 1)] + 1)
            eng.activation(buf["xa"][:, 0, :], misc[:, 0:SEQ], ACT.Copy).then_inc(sem["hi_ready"], 1)
            eng.activation(buf["xb"][0:DB, :], misc[0:DB, SEQ:2 * SEQ], ACT.Copy).then_inc(sem["hi_ready"], 1)
        elif kind == "u":
            arrive(item)
            u = item[2]
            if b and u == 0:
                for h in range(NH):
                    eng.wait_ge(sem["qk_in"][h], 96 * b)
            eng.activation(HL[:, :, 0, u, :], misc[:, :].rearrange("p (g n) -> p g n", g=2), ACT.Copy).then_inc(sem["hi_ready"], 1)
        elif kind == "v":
            arrive(item)
            if b >= 3:
                eng.wait_ge(sem["av_full"], NH * (b - 2))
            for t in range(TPB):
                dst = VS[:, b % 3, t, VPAD:VPAD + NH * P].rearrange("p (h a e) -> p h a e", h=NH, e=8)[:, :, 0:NC, 0:QD]
                src = misc[:, D * t:D * t + D].rearrange("p (h a e) -> p h a e", h=NH, e=QD)
                ins = eng.activation(dst, src, ACT.Copy)
                if t == 0:
                    ins.then_inc(sem["vs_half"], 1)
                else:
                    ins.then_inc(sem["misc_free"], 1)
        elif kind == "ot":
            arrive(item)
            eng.activation(buf["ot"][:, 0:SEQ], misc[:, 0:SEQ], ACT.Copy).then_inc(sem["ot_half"], 1)
            eng.activation(buf["ot"][0:DB, SEQ:2 * SEQ], misc[0:DB, SEQ:2 * SEQ], ACT.Copy).then_inc(sem["misc_free"], 1)

    def exponentials(b, h):
        for t in range(TPB):
            n = NH * b + h
            eng.wait_ge(sem["p2_full"], 2 * n + t + 1)
            if n >= 2:
                eng.wait_ge(sem["av_full"], n - 1)
            eng.activation(PT[:, n % 2, t, :, :].rearrange("p c n -> p (c n)"),
                           ps[:, BANK_EXP + 2 * t:BANK_EXP + 2 * t + 2, :].rearrange("p k n -> p (k n)"),
                           ACT.Exp, scale=float(HD) ** -0.5).then_inc(sem["exp_done"], 1)

    def copy_out(b, h):
        n = NH * b + h
        eng.wait_ge(sem["av_full"], n + 1)
        if n >= 4:
            m = n - 4
            eng.wait_ge(sem["misc_full"], use[("pair", m // NH, m % NH // 2)] + 1)
        eng.activation(OTs[:, h % 4, :], ps[:, BANK_AV, 0:SEQ], ACT.Copy).then_inc(sem["av_out"], 1)

    for i in range(-2, B):
        for h in range(NH):
            for item in misc_items(i, h):
                do_misc(item)
            if i >= 0:
                exponentials(i, h)
                if h:
                    copy_out(i, h - 1)
        for item in tail_items(i):
            if item == ("pair", i, 3):
                copy_out(i, NH - 1)
            do_misc(item)


def attention_on_vector(nc, eng, link, sem, buf, ps, base):
    use = misc_uses()
    misc = ps[:, BANK_MISC, :]
    H, HL = buf["H"], buf["HL"]
    hi_seen = [0]

    def hi():
        hi_seen[0] += 1
        eng.wait_ge(sem["hi_ready"], hi_seen[0])

    def normalize(b):
        if b >= 2:
            eng.wait_ge(sem["misc_full"], use[("x", b - 2)] + 1)
        for t in range(TPB):
            k = TPB * b + t
            ins = eng.tensor_scalar(buf["xn"][:, b % 2, t, :], H[:, k, :], buf["rstd"][:, k:k + 1], buf["nmr"][:, k:k + 1],
                                    ALU.mult, ALU.add)
            if t < TPB - 1:
                link(ins)
            else:
                ins.then_inc(sem["xn_ready"], 1)

    def do_misc(item):
        kind, b = item[0], item[1]
        if kind == "x":
            hi()
            hi()
            eng.tensor_tensor(buf["xa"][:, 1, :], misc[:, 0:SEQ], buf["xa"][:, 0, :].bitcast(F32), ALU.subtract).then_inc(sem["xs_half"], 1)
            eng.tensor_tensor(buf["xb"][DB:P, :], misc[0:DB, SEQ:2 * SEQ], buf["xb"][0:DB, :].bitcast(F32),
                              ALU.subtract).then_inc(sem["misc_free"], 1)
        elif kind == "u":
            u = item[2]
            hi()
            eng.tensor_tensor(HL[:, :, 1, u, :], misc[:, :].rearrange("p (g n) -> p g n", g=2),
                              HL[:, :, 0, u, :].bitcast(F32), ALU.subtract).then_inc(sem["misc_free"], 1)
        elif kind == "pair":
            k = item[2]
            eng.wait_ge(sem["misc_full"], use[item] + 1)
            G = misc[:, :].rearrange("p (g e) -> p g e", e=8)
            link(eng.reciprocal(buf["rec"][:, :], G[:, 0:64:NC, QD]))
            link(eng.tensor_tensor(buf["rs"][:, :, :, :], buf["rec"][:, :].rearrange("p (k c) -> p k c", c=NC).unsqueeze(3).broadcast_to([P, 4, NC, NC]),
                                   buf["vsign"][:, :, :].unsqueeze(1).broadcast_to([P, 4, NC, NC]), ALU.mult))
            TM = buf["TM"]
            eng.tensor_tensor(TM[:, :, :, :, :].rearrange("p c k a e -> p k c a e"),
                              G[:, :, 0:QD].rearrange("p (k c a) e -> p k c a e", c=NC, a=NC),
                              buf["rs"][:, :, :, :].unsqueeze(4).broadcast_to([P, 4, NC, NC, QD]), ALU.mult).then_inc(sem["misc_free"], 1)
            eng.wait_ge(sem["misc_free"], use[item] + 1)
            T0, T1, T2, T3 = (TM[:, c, :, :, :] for c in range(NC))
            f = lambda a: a.rearrange("p k (x y) e -> p (k x) y e", y=2)
            link(eng.tensor_tensor(f(T0), f(T0), f(T1)[:, :, ::-1, :], ALU.add))
            g = lambda a: a.rearrange("p k (x y) e -> p k x (y e)", y=2)
            link(eng.tensor_tensor(g(T0), g(T0), g(T2)[:, :, ::-1, :], ALU.add))
            dst = buf["o"][:, :, 2 * HD * k:2 * HD * k + 2 * HD].rearrange("p t (h a e) -> p h t a e", h=2, a=NC)
            m = lambda a: a.rearrange("p (h t) a e -> p h t a e", h=2)
            eng.tensor_tensor(dst, m(T0), m(T3[:, :, ::-1, :]), ALU.add).then_inc(sem["o_ready"], 1)
            eng.wait_ge(sem["o_ready"], 4 * b + k + 1)
        elif kind == "max":
            eng.wait_ge(sem["misc_full"], use[item] + 1)
            if b:
                eng.wait_ge(sem["nm_in"], 32 * b)
            M = NC * NH
            eng.tensor_scalar(buf["nm"][0:M, 0, :], misc[0:M, 0:SEQ], -1.0, None, ALU.mult).then_inc(sem["nm_ready"], 1)
            eng.wait_ge(sem["nm_ready"], b + 1)
            eng.scalar_tensor_tensor(buf["nm"][0:M, 1, :], misc[0:M, 0:SEQ], -1.0, buf["nm"][0:M, 0, :].bitcast(F32),
                                     ALU.mult, ALU.subtract).then_inc(sem["misc_free"], 1)
        elif kind == "proj":
            eng.wait_ge(sem["misc_full"], use[item] + 1)
            eng.wait_ge(sem["bp_added"], b + 1)
            dst = H[:, TPB * b:TPB * b + TPB, :]
            eng.tensor_tensor(dst, misc[:, 0:TPB * D].rearrange("p (t d) -> p t d", t=TPB), dst, ALU.add).then_inc(sem["misc_free"], 1)

    def maxima(b, h):
        if b >= 2 and h == 0:
            eng.wait_ge(sem["misc_full"], use[("max", b - 2)] + 1)
        for k in range(4):
            t, cp = k // 2, k % 2
            n = 4 * (NH * b + h) + k
            eng.wait_ge(sem["p1_full"], n + 1)
            eng.reduce_max(buf["mx"][:, b % 2, t, :].rearrange("p (c h) -> p c h", h=NH)[:, 2 * cp:2 * cp + 2, h],
                           ps[:, BANK_MAX + n % 2, :].rearrange("p (c n) -> p c n", c=2), AX.X).then_inc(sem["mx_done"], 1)

    normalize(0)
    for i in range(-2, B):
        for h in range(NH):
            if 0 <= i + 1 < B:
                maxima(i + 1, h)
            for item in misc_items(i, h):
                do_misc(item)
        if i + 3 < B:
            normalize(i + 3)
        for item in tail_items(i):
            do_misc(item)


def attention_on_sync(nc, eng, sem, buf):
    use = misc_uses()
    QK, HL, nm = buf["QK"], buf["HL"], buf["nm"]

    def maxima_rows(b):
        eng.wait_ge(sem["nm_ready"], b + 1)
        eng.wait_ge(sem["misc_free"], use[("max", b)] + 1)
        if b >= 2:
            eng.wait_ge(sem["p2_full"], 2 * NH * (b - 1))
        for k in range(2):
            eng.dma_start(QK[SROW + k:SROW + k + 1, b % 2, 0:NC, :, :].bitcast(F32),
                          nm[0:NC * NH, k, :].bitcast(F32)).then_inc(sem["nm_in"], 16)

    eng.wait_ge(sem["qk_clear"], 2)
    for i in range(-2, B):
        b = i + 2
        if b < B:
            eng.wait_ge(sem["misc_free"], use[("u", b, NU - 1)] + 1)
            for h in range(NH):
                if b >= 2:
                    eng.wait_ge(sem["p2_full"], 2 * (NH * (b - 2) + h + 1))
                g, j = h // HG, h % HG
                src = HL[32 * j:32 * j + HD, g, :, :, :]
                for blk, parts in ((0, [(0, 0, NU)]), (1, [(1, 0, NC), (0, NC, NU)]), (2, [(0, 0, NC), (1, NC, NU)]), (3, [(1, 0, NU)])):
                    for half, u0, u1 in parts:
                        eng.dma_start(QK[32 * blk:32 * blk + HD, b % 2, u0:u1, h, :].bitcast(F32),
                                      src[:, half, u0:u1, :].bitcast(F32)).then_inc(sem["qk_in"][h], 16)
        if 0 <= i + 1 < B:
            maxima_rows(i + 1)
GT = 4
NG = NT // GT
GW = GT * P
SPLIT = (True, False, True)
HI_BASE = (0, 2 * NG, 3 * NG)


def transposed_on_vector(eng, link, sem, buf, ps, k):
    H, xn = buf["H"], buf[f"xn{k}"]
    for t in range(NT):
        eng.tensor_scalar(xn[:, t, :], H[:, t, :], buf["rstd"][:, t:t + 1], buf["nmr"][:, t:t + 1],
                          ALU.mult, ALU.add).then_inc(sem["xt_xn"], 1)
    if SPLIT[k]:
        xa, xb = buf[f"xa{k}"], buf[f"xb{k}"]
        for g in range(NG):
            cols, bank = slice(GW * g, GW * g + GW), 2 * (g % 2)
            eng.wait_ge(sem["xt_hi"], HI_BASE[k] + 2 * (g + 1))
            eng.tensor_tensor(xa[:, 1, cols], ps[:, bank, :], xa[:, 0, cols].bitcast(F32), ALU.subtract).then_inc(sem["xt_lo"], 1)
            eng.tensor_tensor(xb[DB:P, cols], ps[0:DB, bank + 1, :], xb[0:DB, cols].bitcast(F32), ALU.subtract).then_inc(sem["xt_free"], 1)


def transposed_on_tensor(eng, sem, buf, ps, k):
    for g in range(NG):
        n, bank = NG * k + g, 2 * (g % 2)
        eng.wait_ge(sem["xt_xn"], NT * k + GT * (g + 1))
        if n >= 2:
            eng.wait_ge(sem["xt_free"], n - 1)
        for t in range(GT):
            eng.transpose(ps[:, bank, P * t:P * t + P], buf[f"xn{k}"][:, GT * g + t, 0:DA], buf["ident"][:, :])
        for t in range(GT):
            ins = eng.transpose(ps[0:DB, bank + 1, P * t:P * t + P], buf[f"xn{k}"][:, GT * g + t, DA:D], buf["ident"][:, :])
        ins.then_inc(sem["xt_full"], 1)


def transposed_on_scalar(eng, sem, buf, ps, k):
    for g in range(NG):
        cols, bank = slice(GW * g, GW * g + GW), 2 * (g % 2)
        eng.wait_ge(sem["xt_full"], NG * k + g + 1)
        if SPLIT[k]:
            eng.activation(buf[f"xa{k}"][:, 0, cols], ps[:, bank, :], ACT.Copy).then_inc(sem["xt_hi"], 1)
            eng.activation(buf[f"xb{k}"][0:DB, cols], ps[0:DB, bank + 1, :], ACT.Copy).then_inc(sem["xt_hi"], 1)
        else:
            eng.activation(buf["xtA"][:, cols], ps[:, bank, :], ACT.Copy).then_inc(sem["xt_hi"], 1)
            eng.activation(buf["xtB"][:, cols], ps[0:DB, bank + 1, :], ACT.Copy).then_inc(sem["xt_free"], 1)


def x_ready(eng, sem, k, g):
    eng.wait_ge(sem["xt_free"], NG * k + g + 1)
    eng.wait_ge(sem["xt_hi"], HI_BASE[k] + (2 if SPLIT[k] else 1) * (g + 1))
    if SPLIT[k]:
        eng.wait_ge(sem["xt_lo"], NG * (k // 2) + g + 1)


def five(eng, out, w, xa, xb, cols, stationary_is_weight):
    pairs = [(w[0], xa[:, 0, cols]), (w[1], xa[:, 0, cols]), (w[0], xa[:, 1, cols]), (w[2], xb[:, cols]), (w[3], xb[:, cols])]
    for n, (ww, xx) in enumerate(pairs):
        a, b = (ww, xx) if stationary_is_weight else (xx, ww)
        ins = eng.matmul(out, a, b, start=n == 0, stop=n == 4)
    return ins


def load_runs(eng, dst, src, sem):
    eng.dma_start(dst[:, 0, :], src[0:DA, :]).then_inc(sem, 16)
    for half in range(2):
        eng.dma_start(dst[DB * half:DB * half + DB, 1, :], src[DA:D, :]).then_inc(sem, 16)


HF = 768
MF = HF // P
NCLS, NA = 6, 5
NCT = B * NCLS
LEFT = 3


def classes_of(atom):
    return slice(2 * atom, 2 * atom + 2) if atom < LEFT else slice(atom - LEFT, NCLS, 2)


def ffn0_on_sync(eng, sem, buf, io):
    eng.wait_ge(sem["misc_free"], len(misc_uses()))
    load_runs(eng, buf["w1f"], io["fc1"], sem["w1_in"])
    eng.dma_start(buf["b1"][:, :], io["fc1_b"]).then_inc(sem["b1_in"], 16)
    eng.dma_start(buf["w2"][:, :, :], io["fc2"].rearrange("(m p) d -> p m d", p=P)).then_inc(sem["w2_in"], 16)
    eng.dma_start(buf["gp"][0:NCT, :, :], io["gate_pair"]).then_inc(sem["gate_in"], 16)
    eng.dma_start(buf["bal"][0:NCT, :], io["balance"]).then_inc(sem["gate_in"], 16)
    eng.dma_start(buf["aob"][0:NCT, :, :], io["atom_out_b"]).then_inc(sem["aob_in"], 16)
    eng.dma_start(buf["ain"][:, :, 0, :], io["atom_in"][:, 0:DA, :].rearrange("a p h -> p a h")).then_inc(sem["ain_in"], 16)
    eng.dma_start(buf["ain"][0:DB + 1, :, 1, :], io["atom_in"][:, DA:D + 1, :].rearrange("a p h -> p a h")).then_inc(sem["ain_in"], 16)
    eng.dma_start(buf["aout"][:, :, :, :], io["atom_out"].rearrange("a (m p) d -> p a m d", p=P)).then_inc(sem["aout_in"], 16)
    eng.dma_start(buf["b2"][:, :], io["fc2_b"].partition_broadcast(P)).then_inc(sem["b2_in"], 16)
    for b in range(B):
        eng.dma_start(buf["hc"][NCLS * b:NCLS * b + NCLS, :], buf["H"][0:NCLS, TPB * b, :]).then_inc(sem["hc_in"], 16)
    for b in range(B):
        eng.wait_ge(sem["xt_xn"], TPB * b + 1)
        eng.dma_start(buf["xc"][NCLS * b:NCLS * b + NCLS, :], buf["xn0"][0:NCLS, TPB * b, :]).then_inc(sem["xc_in"], 16)
    eng.wait_ge(sem["cls_done"], 1)
    eng.wait_ge(sem["f0_add"], NT)
    for b in range(B):
        eng.dma_start(buf["H"][0:NCLS, TPB * b, :], buf["hc"][NCLS * b:NCLS * b + NCLS, :]).then_inc(sem["h2_in"], 16)


def ffn0_on_gpsimd(eng, link, sem, buf):
    W, wf = buf["w1"], buf["w1f"]
    eng.wait_ge(sem["w1_in"], 48)
    link(eng.tensor_copy(W[:, 0:4:2, :], wf[:, :, :]))
    eng.tensor_tensor(W[:, 1:4:2, :], wf[:, :, :], W[:, 0:4:2, :].bitcast(F32), ALU.subtract).then_inc(sem["w1_ready"], 1)
    eng.memset(buf["mh"][:, :, :, :], 0.0).then_inc(sem["mh_zero"], 1)
    eng.memset(buf["xct"][:, :, :], 1.0).then_inc(sem["xct_ones"], 1)
    eng.wait_ge(sem["b2_in"], 16)
    eng.wait_ge(sem["hc_in"], 16 * B)
    for t in range(0, NT, 2):
        eng.wait_ge(sem["xt_xn"], t + 2)
        tiles = buf["H"][:, t:t + 2, :]
        eng.tensor_tensor(tiles, tiles, buf["b2"][:, :].unsqueeze(1).broadcast_to([P, 2, D]), ALU.add).then_inc(sem["b2_added"], 1)


def ffn0_on_tensor(eng, sem, buf, ps):
    w1, w2, hid, mh, ident = buf["w1"], buf["w2"], buf["hid0"], buf["mh"], buf["ident"]
    xct = buf["xct"]
    transposed_on_tensor(eng, sem, buf, ps, 0)

    def hidden(g):
        x_ready(eng, sem, 0, g)
        for m in range(MF):
            n = MF * g + m
            if n >= 2:
                eng.wait_ge(sem["f0_act"], n - 1)
            five(eng, ps[:, 4 + n % 2, :], [w1[:, s, P * m:P * m + P] for s in range(4)], buf["xa0"], buf["xb0"],
                 slice(GW * g, GW * g + GW), True).then_inc(sem["f0_full"], 1)

    def down(g):
        eng.wait_ge(sem["f0_act"], MF * (g + 1))
        for t in range(GT):
            n = GT * g + t
            if n >= 2:
                eng.wait_ge(sem["f0_add"], n - 1)
            for m in range(MF):
                ins = eng.matmul(ps[:, 6 + n % 2, 0:D], hid[:, g % 2, m, P * t:P * t + P], w2[:, m, :],
                                 start=m == 0, stop=m == MF - 1)
            ins.then_inc(sem["f0_out"], 1)

    eng.wait_ge(sem["w1_ready"], 1)
    hidden(0)
    eng.wait_ge(sem["xc_in"], 16 * B)
    eng.wait_ge(sem["xt_free"], NG)
    eng.transpose(ps[:, 0, 0:NCT], buf["xc"][0:NCT, 0:DA], ident[0:NCT, 0:NCT])
    eng.transpose(ps[0:DB, 0, 64:64 + NCT], buf["xc"][0:NCT, DA:D], ident[0:NCT, 0:NCT]).then_inc(sem["xct_psum"], 1)
    hidden(1)
    eng.wait_ge(sem["xct_ready"], 2)
    eng.wait_ge(sem["ain_in"], 32)
    for a in range(NA):
        n = 2 if a < LEFT else 3
        if a >= 2:
            eng.wait_ge(sem["atom_act"], sum(2 if x < LEFT else 3 for x in range(a - 1)))
        xs = [xct[0:k, r, :].rearrange("k (b n) -> k b n", n=NCLS)[:, :, classes_of(a)] for r, k in ((0, P), (1, DB + 1))]
        for m in range(MF):
            out = ps[:, 1 + a % 2, 24 * m:24 * m + B * n].rearrange("p (b n) -> p b n", n=n)
            eng.matmul(out, buf["ain"][:, a, 0, P * m:P * m + P], xs[0], start=True, stop=False)
            ins = eng.matmul(out, buf["ain"][0:DB + 1, a, 1, P * m:P * m + P], xs[1], start=False, stop=True)
        ins.then_inc(sem["atom_full"], 1)
    eng.wait_ge(sem["w2_in"], 16)
    down(0)
    hidden(2)
    down(1)
    eng.wait_ge(sem["aout_in"], 16)
    eng.wait_ge(sem["atom_act"], 12)
    for r, atoms in ((0, (3, 4)), (1, (0, 1, 2))):
        for i, a in enumerate(atoms):
            for m in range(MF):
                ins = eng.matmul(ps[0:NCT, 3, D * r:D * r + D], mh[:, a, m, :], buf["aout"][:, a, m, :],
                                 start=i + m == 0, stop=i == len(atoms) - 1 and m == MF - 1)
    ins.then_inc(sem["cand_full"], 1)
    hidden(3)
    down(2)
    down(3)


def ffn0_on_scalar(eng, sem, buf, ps):
    transposed_on_scalar(eng, sem, buf, ps, 0)
    eng.wait_ge(sem["gate_sq"], 1)
    eng.activation(buf["gs"][0:NCT, 2:5], buf["gs"][0:NCT, 2:5], ACT.Sqrt).then_inc(sem["gate_root"], 1)
    eng.wait_ge(sem["gate_shift"], 1)
    eng.activation(buf["ge"][0:NCT, :], buf["gl"][0:NCT, :], ACT.Exp).then_inc(sem["gate_exp"], 1)
    eng.wait_ge(sem["b1_in"], 16)

    def gelus(g):
        for m in range(MF):
            n = MF * g + m
            eng.wait_ge(sem["f0_full"], n + 1)
            if g >= 2:
                eng.wait_ge(sem["f0_out"], GT * (g - 1))
            eng.activation(buf["hid0"][:, g % 2, m, :], ps[:, 4 + n % 2, :], ACT.Gelu, bias=buf["b1"][:, m:m + 1]).then_inc(sem["f0_act"], 1)

    gelus(0)
    eng.wait_ge(sem["xct_psum"], 1)
    eng.wait_ge(sem["xct_ones"], 1)
    eng.activation(buf["xct"][:, 0, :], ps[:, 0, 0:NCT], ACT.Copy).then_inc(sem["xct_ready"], 1)
    eng.activation(buf["xct"][0:DB, 1, :], ps[0:DB, 0, 64:64 + NCT], ACT.Copy).then_inc(sem["xct_ready"], 1)
    gelus(1)
    eng.wait_ge(sem["mh_zero"], 1)
    for a in range(NA):
        eng.wait_ge(sem["atom_full"], a + 1)
        first, n = (2 * a, 2) if a < LEFT else (a - LEFT, 3)
        for k in range(n):
            cls = first + (k if a < LEFT else 2 * k)
            dst = LEFT + cls % 2 if a < LEFT else cls // 2
            src = ps[:, 1 + a % 2, 0:24 * MF].rearrange("p (m j) -> p m j", j=24)[:, :, k:k + (B - 1) * n + 1:n]
            out = buf["mh"][:, dst, :, :].rearrange("p m (b c) -> p m b c", c=NCLS)[:, :, :, cls]
            eng.activation(out, src, ACT.Gelu).then_inc(sem["atom_act"], 1)
    gelus(2)
    gelus(3)


def ffn0_on_vector(eng, link, sem, buf, ps):
    eng.wait_ge(sem["misc_free"], len(misc_uses()))
    statistics_on_vector(eng, link, sem, buf, 1)
    transposed_on_vector(eng, link, sem, buf, ps, 0)
    xc, gp, gq, gs, gl, ge, gr = (buf[n] for n in ("xc", "gp", "gq", "gs", "gl", "ge", "gr"))
    C = slice(0, NCT)
    eng.wait_ge(sem["xc_in"], 16 * B)
    eng.wait_ge(sem["gate_in"], 32)
    link(eng.tensor_tensor(gq[C, 0:2, :], gp[C, :, :], xc[C, :].unsqueeze(1).broadcast_to([NCT, 2, D]), ALU.mult))
    link(eng.tensor_tensor(gq[C, 2:4, :], gp[C, :, :], gp[C, :, :], ALU.mult))
    link(eng.tensor_tensor(gq[C, 4, :], xc[C, :], xc[C, :], ALU.mult))
    eng.reduce_sum(gs[C, 0:5], gq[C, :, :], AX.X).then_inc(sem["gate_sq"], 1)
    eng.wait_ge(sem["gate_root"], 1)
    link(eng.tensor_scalar(gs[C, 2:5], gs[C, 2:5], 1e-12, None, ALU.max))
    link(eng.reciprocal(gs[C, 2:5], gs[C, 2:5]))
    link(eng.tensor_tensor(gl[C, :], gs[C, 0:2], gs[C, 2:4], ALU.mult))
    link(eng.scalar_tensor_tensor(gl[C, :], gl[C, :], gs[C, 4:5], buf["bal"][C, :], ALU.mult, ALU.add))
    link(eng.tensor_tensor(gr[C, 0:1], gl[C, 0:1], gl[C, 1:2], ALU.max))
    eng.tensor_scalar(gl[C, :], gl[C, :], gr[C, 0:1], None, ALU.subtract).then_inc(sem["gate_shift"], 1)
    eng.wait_ge(sem["gate_exp"], 1)
    link(eng.tensor_tensor(gr[C, 0:1], ge[C, 0:1], ge[C, 1:2], ALU.add))
    link(eng.reciprocal(gr[C, 0:1], gr[C, 0:1]))
    link(eng.tensor_scalar(ge[C, :], ge[C, :], gr[C, 0:1], None, ALU.mult))
    link(eng.tensor_tensor(gr[C, 1:2], ge[C, 0:1], ge[C, 1:2], ALU.is_ge))
    link(eng.tensor_tensor(gr[C, 2:3], ge[C, 0:1], ge[C, 1:2], ALU.max))
    link(eng.tensor_tensor(gr[C, 0:1], gr[C, 1:2], gr[C, 2:3], ALU.mult))
    link(eng.tensor_tensor(gr[C, 1:2], gr[C, 2:3], gr[C, 0:1], ALU.subtract))

    def adds(g):
        for t in range(GT):
            n = GT * g + t
            eng.wait_ge(sem["f0_out"], n + 1)
            eng.wait_ge(sem["b2_added"], n // 2 + 1)
            eng.tensor_tensor(buf["H"][:, n, :], ps[:, 6 + n % 2, 0:D], buf["H"][:, n, :], ALU.add).then_inc(sem["f0_add"], 1)

    adds(0)
    adds(1)
    eng.wait_ge(sem["cand_full"], 1)
    eng.wait_ge(sem["aob_in"], 16)
    eng.wait_ge(sem["hc_in"], 16 * B)
    cand = buf["cand"]
    link(eng.tensor_tensor(cand[C, :, :], ps[C, 3, 0:2 * D].rearrange("p (r d) -> p r d", r=2), buf["aob"][C, :, :], ALU.add))
    link(eng.scalar_tensor_tensor(buf["hc"][C, :], cand[C, 0, :], gr[C, 0:1], buf["hc"][C, :], ALU.mult, ALU.add))
    eng.scalar_tensor_tensor(buf["hc"][C, :], cand[C, 1, :], gr[C, 1:2], buf["hc"][C, :], ALU.mult, ALU.add).then_inc(sem["cls_done"], 1)
    adds(2)
    adds(3)


SCW = 3 * P


def attn1_on_tensor(eng, sem, buf, ps):
    A, Bm, xn, ident = buf["xtA"], buf["xtB"], buf["xn1"], buf["ident"]
    transposed_on_tensor(eng, sem, buf, ps, 1)

    def scores(b):
        x_ready(eng, sem, 1, b // 2)
        if b >= 2:
            eng.wait_ge(sem["a1_masked"], b - 1)
        for t, (at, w) in enumerate(((0, P), (P, 2 * P))):
            rows, cols = slice(SEQ * b + P * t, SEQ * b + P * t + P), slice(SEQ * b, SEQ * b + w)
            out = ps[:, 4 + b % 2, at:at + w]
            eng.matmul(out, A[:, rows], A[:, cols], start=True, stop=False)
            ins = eng.matmul(out, Bm[:, rows], Bm[:, cols], start=False, stop=True)
        ins.then_inc(sem["a1_scores"], 1)

    scores(0)
    for b in range(B):
        if b + 1 < B:
            scores(b + 1)
        eng.wait_ge(sem["a1_exp"], 2 * (b + 1))
        if b:
            eng.wait_ge(sem["a1_pt"], b)
        for k in range(3):
            ins = eng.transpose(ps[:, 6, P * k:P * k + P], buf["p1"][:, b % 2, P * k:P * k + P], ident[:, :])
        ins.then_inc(sem["a1_pt_psum"], 1)
        eng.wait_ge(sem["a1_pt"], b + 1)
        if b:
            eng.wait_ge(sem["a1_add"], 2 * b)
        pt = buf["pt1"][:, b % 2, :]
        eng.matmul(ps[:, 7, 0:D], pt[:, 0:P], xn[:, TPB * b, :], start=True, stop=True)
        eng.matmul(ps[:, 7, D:2 * D], pt[:, P:2 * P], xn[:, TPB * b, :], start=True, stop=False)
        eng.matmul(ps[:, 7, D:2 * D], pt[:, 2 * P:3 * P], xn[:, TPB * b + 1, :], start=False, stop=True).then_inc(sem["a1_av"], 1)


def attn1_on_scalar(eng, sem, buf, ps):
    transposed_on_scalar(eng, sem, buf, ps, 1)
    for b in range(B):
        eng.wait_ge(sem["a1_shift"], b + 1)
        if b >= 2:
            eng.wait_ge(sem["a1_pt_psum"], b - 1)
        for t, (at, w) in enumerate(((0, P), (P, 2 * P))):
            eng.activation(buf["p1"][:, b % 2, at:at + w], buf["sc1"][:, b % 2, at:at + w], ACT.Exp,
                           bias=buf["m1"][:, b % 2, t:t + 1], accum_out=buf["sum1"][:, b % 2, t:t + 1]).then_inc(sem["a1_exp"], 1)
        eng.wait_ge(sem["a1_pt_psum"], b + 1)
        if b >= 2:
            eng.wait_ge(sem["a1_av"], b - 1)
        eng.activation(buf["pt1"][:, b % 2, :], ps[:, 6, 0:SCW], ACT.Copy).then_inc(sem["a1_pt"], 1)


def attn1_on_vector(eng, link, sem, buf, ps):
    eng.wait_ge(sem["h2_in"], 16 * B)
    statistics_on_vector(eng, link, sem, buf, 2)
    transposed_on_vector(eng, link, sem, buf, ps, 1)
    eng.wait_ge(sem["mask_ready"], 2)

    def mask(b):
        eng.wait_ge(sem["a1_scores"], b + 1)
        if b >= 2:
            eng.wait_ge(sem["a1_exp"], 2 * (b - 1))
        eng.scalar_tensor_tensor(buf["sc1"][:, b % 2, :], ps[:, 4 + b % 2, 0:SCW], float(D) ** -0.5, buf["mask"][:, :],
                                 ALU.mult, ALU.add).then_inc(sem["a1_masked"], 1)
        eng.wait_ge(sem["a1_masked"], b + 1)
        link(eng.reduce_max(buf["m1"][:, b % 2, 0:1], buf["sc1"][:, b % 2, 0:P], AX.X))
        link(eng.reduce_max(buf["m1"][:, b % 2, 1:2], buf["sc1"][:, b % 2, P:SCW], AX.X))
        eng.tensor_scalar(buf["m1"][:, b % 2, :], buf["m1"][:, b % 2, :], -1.0, None, ALU.mult).then_inc(sem["a1_shift"], 1)

    mask(0)
    for b in range(B):
        if b + 1 < B:
            mask(b + 1)
        eng.wait_ge(sem["a1_exp"], 2 * (b + 1))
        if b:
            eng.wait_ge(sem["a1_add"], TPB * b)
        link(eng.reciprocal(buf["rec1"][:, :], buf["sum1"][:, b % 2, :]))
        eng.wait_ge(sem["a1_av"], b + 1)
        for t in range(TPB):
            h = buf["H"][:, TPB * b + t, :]
            eng.scalar_tensor_tensor(h, ps[:, 7, D * t:D * t + D], buf["rec1"][:, t:t + 1], h, ALU.mult, ALU.add).then_inc(sem["a1_add"], 1)


NE, TOPK = 8, 2
HE, HS = D, HF
HALL = NE * HE + HS
MR, MA = NE * HE // P, HALL // P
RW = NE + 2
LOROW = 32
NGATE = NE + 1
WC = HF // 2
NWC = 2 * HALL // WC


def ffn1_on_sync(eng, sem, buf, io):
    eng.wait_ge(sem["h2_in"], 16 * B)
    eng.dma_start(buf["wd"][:, :, :], io["w_down"].rearrange("(m p) d -> p m d", p=P)).then_inc(sem["wd_in"], 16)
    eng.dma_start(buf["sgb"][:, :], io["sg_b"].partition_broadcast(P)).then_inc(sem["sgb_in"], 16)
    load_runs(eng, buf["wrf"], io["router"], sem["wr_in"])
    for n in range(NWC):
        if n >= 2:
            eng.wait_ge(sem["wgu_ready"], n - 1)
        load_runs(eng, buf["wgf"][:, n % 2, :, :], io["w_gate_up"][:, WC * n:WC * n + WC], sem[f"wgu_in{n % 2}"])


def ffn1_on_gpsimd(eng, link, sem, buf, io):
    eng.wait_ge(sem["h2_in"], 16 * B)
    eng.dma_start(buf["sel"][0:2 * LOROW, :, :], io["select"]).then_inc(sem["sel_in"], 16)
    eng.memset(buf["mask"][:, :], 0.0).then_inc(sem["mask_zero"], 1)
    eng.wait_ge(sem["mask_zero"], 1)
    for k in (0, 2):
        tile = buf["mask"][:, P * k:P * k + P]
        eng.affine_select(out=tile, in_=tile, compare_op=ALU.is_ge, fill=-1e9, base=0, pattern=[[-1, P]],
                          channel_multiplier=1).then_inc(sem["mask_ready"], 1)
    eng.memset(buf["gt"][:, :].bitcast(F32), 0.0).then_inc(sem["gt_zero"], 1)
    eng.wait_ge(sem["wr_in"], 48)
    link(eng.tensor_copy(buf["wr"][:, 0:4:2, :], buf["wrf"][:, :, :]))
    eng.tensor_tensor(buf["wr"][:, 1:4:2, :], buf["wrf"][:, :, :], buf["wr"][:, 0:4:2, :].bitcast(F32), ALU.subtract).then_inc(sem["wr_ready"], 1)
    for n in range(NWC):
        eng.wait_ge(sem[f"wgu_in{n % 2}"], 48 * (n // 2 + 1))
        cols, wf, W = slice(WC * n, WC * n + WC), buf["wgf"][:, n % 2, :, :], buf["wgu"]
        link(eng.tensor_copy(W[:, 0:4:2, cols], wf))
        eng.tensor_tensor(W[:, 1:4:2, cols], wf, W[:, 0:4:2, cols].bitcast(F32), ALU.subtract).then_inc(sem["wgu_ready"], 1)
    for g in range(NG):
        for m in range(MA):
            n = MA * g + m
            eng.wait_ge(sem["f1_prod"], n + 1)
            eng.wait_ge(sem["f1_gb"], gb_count(g, m))
            if g:
                eng.wait_ge(sem["f1_out"], GT * g)
            gb = buf["gb"][:, m % 2, :] if m < MR else buf["gbs"][:, :]
            eng.tensor_tensor(buf["hid1"][:, m, :], buf["prod"][:, n % 2, :], gb, ALU.mult).then_inc(sem["f1_hid"], 1)


def gb_count(g, m):
    return (MR + 1) * g + min(m, MR) + 1


def ffn1_on_tensor(eng, sem, buf, ps):
    W, wd, hid, ident = buf["wgu"], buf["wd"], buf["hid1"], buf["ident"]
    transposed_on_tensor(eng, sem, buf, ps, 2)
    eng.wait_ge(sem["wr_ready"], 1)
    for t in range(NT):
        x_ready(eng, sem, 2, t // GT)
        ins = five(eng, ps[:, 4, RW * t:RW * t + RW], [buf["wr"][:, s, :] for s in range(4)], buf["xa2"], buf["xb2"],
                   slice(P * t, P * t + P), False)
    ins.then_inc(sem["router_psum"], 1)

    def gate_up(g, m):
        n = MA * g + m
        cols = slice(GW * g, GW * g + GW)
        if n >= 2:
            eng.wait_ge(sem["f1_silu"], n - 1)
        five(eng, ps[:, n % 2, :], [W[:, s, P * m:P * m + P] for s in range(4)], buf["xa2"], buf["xb2"], cols, True)\
            .then_inc(sem["f1_gate"], 1)
        if n >= 2:
            eng.wait_ge(sem["f1_prod"], n - 1)
        five(eng, ps[:, 2 + n % 2, :], [W[:, s, HALL + P * m:HALL + P * m + P] for s in range(4)], buf["xa2"], buf["xb2"], cols, True)\
            .then_inc(sem["f1_up"], 1)

    def spread(g, m):
        k = (MR + 1) * g + m
        if k >= 2:
            eng.wait_ge(sem["f1_gb"], k - 1)
        eng.matmul(ps[:, 4 + k % 2, :], buf["sel"][0:2 * LOROW, m, :], buf["gt"][0:2 * LOROW, GW * g:GW * g + GW],
                   start=True, stop=True).then_inc(sem["f1_spread"], 1)

    def down(g):
        for t in range(GT):
            n = GT * g + t
            if n >= 2:
                eng.wait_ge(sem["f1_add"], n - 1)
            eng.wait_ge(sem["f1_hid"], MA * (g + 1))
            for m in range(MA):
                ins = eng.matmul(ps[:, 6 + n % 2, 0:D], hid[:, m, P * t:P * t + P], wd[:, m, :], start=m == 0, stop=m == MA - 1)
            ins.then_inc(sem["f1_out"], 1)

    eng.wait_ge(sem["wd_in"], 16)
    for g in range(NG):
        for m in range(MA):
            if g == 0:
                eng.wait_ge(sem["wgu_ready"], (HALL + P * m + P - 1) // WC + 1)
            gate_up(g, m)
            if g == 0 and m == 1:
                eng.wait_ge(sem["gates_ready"], 1)
                for t in range(NT):
                    if t % GT == 0 and t >= 2 * GT:
                        eng.wait_ge(sem["gt_done"], t // GT - 1)
                    ins = eng.transpose(ps[0:NGATE, 6 + t // GT % 2, P * (t % GT):P * (t % GT) + P], buf["ga"][:, t, :], ident[:, :])
                    if t % GT == GT - 1:
                        ins.then_inc(sem["gt_psum"], 1)
                eng.wait_ge(sem["gt_done"], NG)
                eng.wait_ge(sem["sel_in"], 16)
                spread(g, 0)
                spread(g, 1)
            elif (g or m > 1) and m <= MR:
                spread(g, m)
        down(g)


def ffn1_on_scalar(eng, sem, buf, ps):
    transposed_on_scalar(eng, sem, buf, ps, 2)
    eng.wait_ge(sem["router_shift"], 1)
    eng.activation(buf["rl"][:, :, :], buf["rl"][:, :, :], ACT.Exp).then_inc(sem["router_exp"], 1)
    for k in range(NG):
        rows = slice(0, NGATE)
        cols = slice(GW * k, GW * k + GW)
        eng.wait_ge(sem["gt_zero"], 1)
        eng.wait_ge(sem["gt_psum"], k + 1)
        eng.activation(buf["gt"][rows, cols], ps[rows, 6 + k % 2, :], ACT.Copy).then_inc(sem["gt_hi"], 1)
    for g in range(NG):
        for m in range(MA):
            n = MA * g + m
            eng.wait_ge(sem["f1_gate"], n + 1)
            if n >= 2:
                eng.wait_ge(sem["f1_prod"], n - 1)
            eng.activation(buf["sg"][:, n % 2, :], ps[:, n % 2, :], ACT.Silu).then_inc(sem["f1_silu"], 1)
            if m <= MR:
                k = (MR + 1) * g + m
                eng.wait_ge(sem["f1_spread"], k + 1)
                last = MA * g + m - 2 if m < MR else MA * g - 1
                if last >= 0:
                    eng.wait_ge(sem["f1_hid"], last + 1)
                dst = buf["gb"][:, m % 2, :] if m < MR else buf["gbs"][:, :]
                eng.activation(dst, ps[:, 4 + k % 2, :], ACT.Copy).then_inc(sem["f1_gb"], 1)


def ffn1_on_vector(eng, link, sem, buf, ps):
    statistics_on_vector(eng, link, sem, buf, 3)
    transposed_on_vector(eng, link, sem, buf, ps, 2)
    rl, mx, ga, cmp, rk = (buf[n] for n in ("rl", "rmx", "ga", "cmp", "rk"))
    eng.wait_ge(sem["router_psum"], 1)
    eng.wait_ge(sem["sgb_in"], 16)
    R = ps[:, 4, 0:NT * RW].rearrange("p (t r) -> p t r", r=RW)
    link(eng.reduce_max(mx[:, :], R[:, :, 0:NE], AX.X))
    link(eng.tensor_tensor(rl[:, :, 0:NE], R[:, :, 0:NE], mx[:, :].unsqueeze(2).broadcast_to([P, NT, NE]), ALU.subtract))
    eng.tensor_scalar(rl[:, :, NE], R[:, :, NE], buf["sgb"][:, 0:1], -1.0, ALU.add, ALU.mult).then_inc(sem["router_shift"], 1)
    eng.wait_ge(sem["router_exp"], 1)
    link(eng.tensor_scalar(mx[:, :], rl[:, :, NE], 1.0, None, ALU.add))
    link(eng.reciprocal(ga[:, :, NE], mx[:, :]))
    for e in range(NE):
        q = rl[:, :, e:e + 1].broadcast_to([P, NT, NE])
        link(eng.tensor_tensor(cmp[:, :, e, :], rl[:, :, 0:NE], q, ALU.is_gt))
    for e in range(1, NE):
        q = rl[:, :, e:e + 1].broadcast_to([P, NT, e])
        link(eng.tensor_tensor(cmp[:, :, e, 0:e], rl[:, :, 0:e], q, ALU.is_ge))
    link(eng.reduce_sum(rk[:, :, :], cmp[:, :, :, :], AX.X))
    link(eng.tensor_scalar(rk[:, :, :], rk[:, :, :], float(TOPK), None, ALU.is_lt))
    link(eng.tensor_tensor(rk[:, :, :], rk[:, :, :], rl[:, :, 0:NE], ALU.mult))
    link(eng.reduce_sum(mx[:, :], rk[:, :, :], AX.X))
    link(eng.reciprocal(mx[:, :], mx[:, :]))
    link(eng.tensor_scalar(buf["oma"][:, :], ga[:, :, NE], -1.0, 1.0, ALU.mult, ALU.add))
    link(eng.tensor_tensor(mx[:, :], mx[:, :], buf["oma"][:, :], ALU.mult))
    eng.tensor_tensor(ga[:, :, 0:NE], rk[:, :, :], mx[:, :].unsqueeze(2).broadcast_to([P, NT, NE]), ALU.mult).then_inc(sem["gates_ready"], 1)

    def product(n):
        eng.wait_ge(sem["f1_up"], n + 1)
        eng.wait_ge(sem["f1_silu"], n + 1)
        if n >= 2:
            eng.wait_ge(sem["f1_hid"], n - 1)
        eng.tensor_tensor(buf["prod"][:, n % 2, :], ps[:, 2 + n % 2, :], buf["sg"][:, n % 2, :], ALU.mult).then_inc(sem["f1_prod"], 1)

    for k in range(NG):
        eng.wait_ge(sem["gt_hi"], k + 1)
        rows, cols = slice(0, NGATE), slice(GW * k, GW * k + GW)
        eng.tensor_tensor(buf["gt"][LOROW:LOROW + NGATE, cols], ps[rows, 6 + k % 2, :], buf["gt"][rows, cols].bitcast(F32),
                          ALU.subtract).then_inc(sem["gt_done"], 1)
    for g in range(NG):
        for m in range(MA):
            product(MA * g + m)
        for t in range(GT):
            n = GT * g + t
            eng.wait_ge(sem["f1_out"], n + 1)
            h = buf["H"][:, n, :]
            eng.tensor_tensor(h, ps[:, 6 + n % 2, 0:D], h, ALU.add).then_inc(sem["f1_add"], 1)
SEMS = ["ids_in", "theta_in", "angles_ready", "trig_ready", "ev_ready", "ident_zero", "ident_ready", "pw_zero", "pw_in",
        "evt_psum", "evt_ready", "emb_psum", "h_ready", "dve_step", "pool_step", "out_sent",
        "var_ready", "std_ready", "wqkv_in", "wqkv_ready", "wp_in", "wp_ready", "bp_in", "bp_added", "vsign_in",
        "vs_clear", "qk_clear", "xn_ready", "misc_full", "misc_free", "hi_ready", "xs_half", "vs_half", "ot_half",
        "p1_full", "mx_done", "nm_ready", "nm_in", "p2_full", "exp_done", "av_full", "av_out", "o_ready",
        "xt_xn", "xt_full", "xt_hi", "xt_lo", "xt_free",
        "w1_in", "w1_ready", "b1_in", "w2_in", "b2_in", "b2_added", "gate_in", "aob_in", "ain_in", "aout_in", "hc_in", "xc_in",
        "mh_zero", "xct_ones", "xct_psum", "xct_ready", "atom_full", "atom_act", "cand_full", "cls_done", "h2_in",
        "gate_sq", "gate_root", "gate_shift", "gate_exp", "f0_full", "f0_act", "f0_out", "f0_add",
        "mask_zero", "mask_ready", "a1_scores", "a1_masked", "a1_shift", "a1_exp", "a1_pt_psum", "a1_pt", "a1_av", "a1_add",
        "wd_in", "sel_in", "sgb_in", "wr_in", "wr_ready", "wgu_in0", "wgu_in1", "wgu_ready", "gt_zero", "router_psum",
        "router_shift", "router_exp", "gates_ready", "gt_psum", "gt_hi", "gt_done", "f1_gate", "f1_up", "f1_silu",
        "f1_spread", "f1_gb", "f1_prod", "f1_hid", "f1_out", "f1_add"]


def embedding_on_tensor(eng, sem, buf, ps):
    evt, pw, ident = buf["evt"], buf["pw"], buf["ident"]
    eng.wait_ge(sem["ident_ready"], 1)
    eng.wait_ge(sem["ev_ready"], 1)
    for c in range(4):
        eng.transpose(ps[:, 0, P * c:P * c + P], buf["evp"][:, 4 * c:4 * c + 4, :].rearrange("p t e -> p (t e)"),
                      ident[:, :]).then_inc(sem["evt_psum"], 1)
    eng.wait_ge(sem["pw_in"], 64)
    for c in range(4):
        eng.wait_ge(sem["evt_ready"], c + 1)
        for k in range(2):
            if c >= 2:
                eng.wait_ge(sem["h_ready"], 2 * c + k - 3)
            eng.matmul(ps[:, 1 + (2 * c + k) % 4, 0:2 * D], evt[:, c, :],
                       pw[:, 2 * k:2 * k + 2, :].rearrange("p t d -> p (t d)"), start=True, stop=True).then_inc(sem["emb_psum"], 1)


def embedding_on_scalar(eng, sem, buf, ps):
    eng.wait_ge(sem["angles_ready"], 1)
    eng.activation(buf["sn"][:, :, :], buf["red"][:, 0, :, :], ACT.Sin).then_inc(sem["trig_ready"], 1)
    eng.activation(buf["cs"][:, :, :], buf["red"][:, 1, :, :], ACT.Sin).then_inc(sem["trig_ready"], 1)
    for c in range(4):
        eng.wait_ge(sem["evt_psum"], 4)
        eng.activation(buf["evt"][:, c, :], ps[:, 0, P * c:P * c + P], ACT.Copy).then_inc(sem["evt_ready"], 1)
    for i in range(8):
        eng.wait_ge(sem["emb_psum"], i + 1)
        eng.activation(buf["H"][:, 2 * i:2 * i + 2, :].rearrange("p t d -> p (t d)"), ps[:, 1 + i % 4, 0:2 * D],
                       ACT.Copy).then_inc(sem["h_ready"], 1)


def program(nc, io, out):
    ctx = ExitStack()
    with ctx:
        def alloc(scope, buf, name, shape, dt=F32):
            buf[name] = scope.enter_context(nc.sbuf_tensor(name, shape, dt))

        sem = {n: ctx.enter_context(nc.semaphore(n)) for n in SEMS}
        sem["qk_in"] = [ctx.enter_context(nc.semaphore(f"qk_in{h}")) for h in range(NH)]
        buf = {}
        for name, shape, dt in (("H", [P, NT, D], F32), ("ident", [P, P], F32), ("st", [P, NT, 6], F32),
                                ("mv", [P, NT, 2], F32), ("rstd", [P, NT], F32), ("nmr", [P, NT], F32),
                                ):
            alloc(ctx, buf, name, shape, dt)
        first = ctx.enter_context(ExitStack())
        for name, shape, dt in (("wqkv", [P, 4, NQKV], F32R), ("wp", [P, 2, D], F32), ("wps", [P, 2, D], F32),
                                ("bp", [P, D], F32), ("vsign", [P, NC, NC], F32)):
            alloc(first, buf, name, shape, dt)
        with ExitStack() as scope:
            for name, shape in (("theta", [P, NT, NANG]), ("red", [P, 2, NANG, NT]), ("sn", [P, NANG, NT]),
                                ("cs", [P, NANG, NT]), ("R", [P, 5, NQ, NT]), ("ZM", [P, 4, NQ, NT]),
                                ("XP", [P, 4, NQ, NT]), ("W", [P, 4, 12, NT]), ("U", [P, 4, 12, NT]),
                                ("M", [P, 4, 12, NT]), ("E", [P, 4, 12, NT]), ("PP", [P, 3, 4, NT]),
                                ("TZ", [P, 4, NT]), ("G", [P, 48, NT]), ("OZ", [P, NQ, NT]), ("OX", [P, NQ, NT]),
                                ("evp", [P, NT, EVW]), ("evt", [P, 4, P]), ("pw", [P, 4, D]),
                                ("wf", [P, 2, NQKV]), ("wsg", [P, 2, NQKV])):
                alloc(scope, buf, name, shape)
            alloc(scope, buf, "ids", [P, NT], I32)
        with ExitStack() as scope:
            for name, shape, dt in (("QK", [P, 2, NU, NH, SEQ], F32R), ("HL", [P, 2, 2, NU, SEQ], F32R),
                                    ("VS", [P, 3, TPB, VPAD + NH * P], F32), ("PT", [P, 2, TPB, NC, SEQ], F32),
                                    ("OTs", [P, 4, SEQ], F32), ("o", [P, TPB, D], F32), ("ot", [P, 2 * SEQ], F32),
                                    ("TM", [P, NC, 4, NC, QD], F32), ("rec", [P, 16], F32), ("rs", [P, 4, NC, NC], F32),
                                    ("nm", [P, 2, SEQ], F32R), ("mx", [P, 2, TPB, NC * NH], F32),
                                    ("xn", [P, 2, TPB, D], F32), ("xa", [P, 2, SEQ], F32R), ("xb", [P, SEQ], F32R)):
                alloc(scope, buf, name, shape, dt)
        first.close()
        with ExitStack() as scope:
            for name, shape, dt in (("xn0", [P, NT, D], F32), ("xa0", [P, 2, NT * P], F32R), ("xb0", [P, NT * P], F32R),
                                    ("w1f", [P, 2, HF], F32), ("w1", [P, 4, HF], F32R), ("b1", [P, MF], F32),
                                    ("w2", [P, MF, D], F32), ("b2", [P, D], F32), ("hid0", [P, 2, MF, GW], F32),
                                    ("gp", [P, 2, D], F32), ("bal", [P, 2], F32), ("aob", [P, 2, D], F32),
                                    ("ain", [P, NA, 2, HF], F32), ("aout", [P, NA, MF, D], F32), ("hc", [P, D], F32),
                                    ("xc", [P, D], F32), ("xct", [P, 2, NCT], F32), ("mh", [P, NA, MF, NCT], F32),
                                    ("gq", [P, 5, D], F32), ("gs", [P, 5], F32), ("gl", [P, 2], F32), ("ge", [P, 2], F32),
                                    ("gr", [P, 3], F32), ("cand", [P, 2, D], F32)):
                alloc(scope, buf, name, shape, dt)
        for name, shape, dt in (("wgu", [P, 4, 2 * HALL], F32R), ("wd", [P, MA, D], F32), ("sel", [P, MR + 1, P], F32R),
                                ("wgf", [P, 2, 2, WC], F32), ("wrf", [P, 2, RW], F32), ("wr", [P, 4, RW], F32R),
                                ("sgb", [P, 1], F32), ("mask", [P, SCW], F32), ("gt", [P, NT * P], F32R)):
            alloc(ctx, buf, name, shape, dt)
        with ExitStack() as scope:
            for name, shape, dt in (("xn1", [P, NT, D], F32), ("xtA", [P, NT * P], F32), ("xtB", [DB, NT * P], F32),
                                    ("sc1", [P, 2, SCW], F32), ("p1", [P, 2, SCW], F32), ("pt1", [P, 2, SCW], F32),
                                    ("m1", [P, 2, TPB], F32), ("sum1", [P, 2, TPB], F32), ("rec1", [P, TPB], F32)):
                alloc(scope, buf, name, shape, dt)
        with ExitStack() as scope:
            for name, shape, dt in (("hid1", [P, MA, GW], F32), ("xa2", [P, 2, NT * P], F32R), ("xb2", [P, NT * P], F32R),
                                    ("sg", [P, 2, GW], F32), ("prod", [P, 2, GW], F32), ("gb", [P, 2, GW], F32),
                                    ("gbs", [P, GW], F32), ("rl", [P, NT, NGATE], F32), ("ga", [P, NT, NGATE], F32),
                                    ("rmx", [P, NT], F32), ("oma", [P, NT], F32), ("rk", [P, NT, NE], F32),
                                    ("cmp", [P, NT, NE, NE], F32)):
                alloc(scope, buf, name, shape, dt)
        buf["xn2"] = buf["hid1"][:, 0:NT * D // GW, :].rearrange("p m n -> p (m n)").rearrange("p (t d) -> p t d", d=D)
        ps = ctx.enter_context(nc.psum_tensor("ps", [P, 8, NBANK], F32))
        block = ctx.enter_context(nc.Block())

        @block.sync
        def _(eng):
            eng.dma_start(buf["ids"][:, :], io["ids"]).then_inc(sem["ids_in"], 16)
            for dst, name in ((buf["wf"], "wqkv"), (buf["wsg"], "wqkv_sign")):
                eng.dma_start(dst[:, 0, :], io[name][0:DA, :]).then_inc(sem["wqkv_in"], 16)
                for half in range(2):
                    eng.dma_start(dst[DB * half:DB * half + DB, 1, :], io[name][DA:D, :]).then_inc(sem["wqkv_in"], 16)
            for dst, name in ((buf["wp"], "wp"), (buf["wps"], "wp_sign")):
                eng.dma_start(dst[:, 0, :], io[name][0:DA, :]).then_inc(sem["wp_in"], 16)
                eng.dma_start(dst[0:DB, 1, :], io[name][DA:D, :]).then_inc(sem["wp_in"], 16)
            eng.dma_start(buf["bp"][:, :], io["bp"].partition_broadcast(P)).then_inc(sem["bp_in"], 16)
            eng.dma_start(buf["vsign"][:, :, :], io["vsign"].partition_broadcast(P)).then_inc(sem["vsign_in"], 16)
            eng.wait_ge(sem["pw_zero"], 1)
            for j in range(4):
                eng.dma_start(buf["pw"][EVW * j:EVW * j + NQ + 1, j, :], io["post"]).then_inc(sem["pw_in"], 16)
            attention_on_sync(nc, eng, sem, buf)
            ffn0_on_sync(eng, sem, buf, io)
            ffn1_on_sync(eng, sem, buf, io)
            eng.wait_ge(sem["f1_add"], NT)
            eng.dma_start(out.rearrange("a (h p) d -> p (a h) d", p=P), buf["H"][:, :, :]).then_inc(sem["out_sent"], 16)
            eng.wait_ge(sem["out_sent"], 16)

        @block.gpsimd
        def _(eng):
            link = Chain(eng, sem["pool_step"])
            eng.memset(buf["pw"][:, :, :], 0.0).then_inc(sem["pw_zero"], 1)
            eng.memset(buf["ident"][:, :], 0.0).then_inc(sem["ident_zero"], 1)
            eng.wait_ge(sem["ids_in"], 16)
            for t in range(NT):
                eng.indirect_dma_start(buf["theta"][:, t, :], None, io["qp"],
                                       bass.IndirectOffsetOnAxis(ap=buf["ids"][:, t:t + 1], axis=0)).then_inc(sem["theta_in"], 16)
            eng.wait_ge(sem["ident_zero"], 1)
            eng.affine_select(out=buf["ident"][:, :], in_=buf["ident"][:, :], compare_op=ALU.not_equal, fill=1.0, base=0,
                              pattern=[[-1, P]], channel_multiplier=1).then_inc(sem["ident_ready"], 1)
            W, wf = buf["wqkv"], buf["wf"]
            eng.wait_ge(sem["wqkv_in"], 96)
            link(eng.tensor_tensor(wf[:, :, :], wf[:, :, :], buf["wsg"][:, :, :], ALU.mult))
            link(eng.tensor_copy(W[:, 0:4:2, :], wf[:, :, :]))
            eng.tensor_tensor(W[:, 1:4:2, :], wf[:, :, :], W[:, 0:4:2, :].bitcast(F32), ALU.subtract).then_inc(sem["wqkv_ready"], 1)
            eng.wait_ge(sem["wp_in"], 64)
            link(eng.tensor_tensor(buf["wp"][:, 0, :], buf["wp"][:, 0, :], buf["wps"][:, 0, :], ALU.mult))
            eng.tensor_tensor(buf["wp"][0:DB, 1, :], buf["wp"][0:DB, 1, :], buf["wps"][0:DB, 1, :], ALU.mult).then_inc(sem["wp_ready"], 1)
            eng.wait_ge(sem["wqkv_ready"], 1)
            eng.wait_ge(sem["h_ready"], 8)
            for s in range(2):
                link(eng.memset(buf["QK"][:, s, :, :, :].rearrange("p u h n -> p (u h n)").bitcast(F32), 0.0))
                eng.memset(buf["QK"][96:P, s, NC, :, :].rearrange("p h n -> p (h n)").bitcast(F32), 1.0).then_inc(sem["qk_clear"], 1)
                eng.wait_ge(sem["qk_clear"], s + 1)
            link(eng.memset(buf["VS"][:, :, :, :], 0.0))
            eng.memset(buf["VS"][:, :, :, VPAD:VPAD + NH * P].rearrange("p s t (h w) -> p (s t) h w", h=NH)[:, :, :, QD:QD + 1], 1.0)\
               .then_inc(sem["vs_clear"], 1)
            eng.wait_ge(sem["bp_in"], 16)
            for b in range(B):
                eng.wait_ge(sem["xn_ready"], b + 1)
                tiles = buf["H"][:, TPB * b:TPB * b + TPB, :]
                eng.tensor_tensor(tiles, tiles, buf["bp"][:, :].unsqueeze(1).broadcast_to([P, TPB, D]), ALU.add).then_inc(sem["bp_added"], 1)
            ffn0_on_gpsimd(eng, link, sem, buf)
            ffn1_on_gpsimd(eng, link, sem, buf, io)

        @block.scalar
        def _(eng):
            embedding_on_scalar(eng, sem, buf, ps)
            root_on_scalar(eng, sem, buf, 0)
            eng.wait_ge(sem["vs_clear"], 1)
            attention_on_scalar(nc, eng, sem, buf, ps, 0)
            root_on_scalar(eng, sem, buf, 1)
            ffn0_on_scalar(eng, sem, buf, ps)
            root_on_scalar(eng, sem, buf, 2)
            attn1_on_scalar(eng, sem, buf, ps)
            root_on_scalar(eng, sem, buf, 3)
            ffn1_on_scalar(eng, sem, buf, ps)

        @block.vector
        def _(eng):
            link = Chain(eng, sem["dve_step"])
            circuit_on_vector(eng, link, sem, buf)
            eng.wait_ge(sem["h_ready"], 8)
            statistics_on_vector(eng, link, sem, buf, 0)
            eng.wait_ge(sem["vsign_in"], 16)
            attention_on_vector(nc, eng, link, sem, buf, ps, 0)
            ffn0_on_vector(eng, link, sem, buf, ps)
            attn1_on_vector(eng, link, sem, buf, ps)
            eng.wait_ge(sem["a1_add"], NT)
            ffn1_on_vector(eng, link, sem, buf, ps)

        @block.tensor
        def _(eng):
            embedding_on_tensor(eng, sem, buf, ps)
            eng.wait_ge(sem["h_ready"], 8)
            attention_on_tensor(nc, eng, sem, buf, ps, 0)
            ffn0_on_tensor(eng, sem, buf, ps)
            attn1_on_tensor(eng, sem, buf, ps)
            ffn1_on_tensor(eng, sem, buf, ps)


def quaternion_layout(parts):
    return np.concatenate([np.concatenate([parts[r ^ c] for c in range(NC)], 1) for r in range(NC)], 0)


def arrange(inputs):
    a = {}
    get = lambda n: np.asarray(inputs[n])
    a["ids"] = get("x").reshape(NT, P).T
    a["qp"] = get("L0_tok_quantum_params").transpose(0, 1, 3, 2).reshape(VOCAB, NANG)
    a["post"] = np.concatenate([get("L0_tok_post_w").T, get("L0_tok_post_b")[None]], 0)
    full = quaternion_layout([get(f"L0_attn_wqkv_{c}") for c in "rijk"])
    sign = np.repeat(np.repeat(np.array(LSIGN, np.float32), D // NC, 0), 3 * D // NC, 1)
    w = np.zeros((D, NQKV), np.float32)
    s = np.zeros((D, NQKV), np.float32)
    for u in range(NU):
        for h in range(NH):
            for comp in range(NC):
                src = (0 if u < NC else D) + h * HD + ((u ^ comp) if u < NC else comp) * QD
                dst = (2 * u + h // HG) * P + 32 * (h % HG) + comp * QD
                w[:, dst:dst + QD] = full[:, src:src + QD]
                s[:, dst:dst + QD] = sign[:, src:src + QD] * (QSIGN[u][comp] if u < NC else 1)
    w[:, 2 * NU * P:] = full[:, 2 * D:]
    s[:, 2 * NU * P:] = sign[:, 2 * D:]
    a["wqkv"], a["wqkv_sign"] = w, s
    a["wp"] = quaternion_layout([get(f"L0_attn_wp_{c}") for c in "rijk"])
    a["wp_sign"] = np.repeat(np.repeat(np.array(LSIGN, np.float32), D // NC, 0), D // NC, 1)
    a["bp"] = get("L0_attn_bp")
    a["vsign"] = np.array(VSIGN, np.float32)
    left, right = [n // 2 for n in range(NCLS)], [LEFT + n % 2 for n in range(NCLS)]
    a["fc1"], a["fc1_b"] = get("L0_ffn_fc1_w").T, get("L0_ffn_fc1_b").reshape(MF, P).T
    a["fc2"], a["fc2_b"] = get("L0_ffn_fc2_w").T, get("L0_ffn_fc2_b")
    a["gate_pair"] = np.concatenate([get("L0_ffn_gate_pair")] * B, 0)
    a["balance"] = np.concatenate([get("L0_ffn_balance_bias")] * B, 0)
    ob = get("L0_ffn_atom_out_b")
    a["atom_out_b"] = np.concatenate([np.stack([ob[right], ob[left]], 1)] * B, 0)
    a["atom_in"] = np.concatenate([get("L0_ffn_atom_in_w").transpose(0, 2, 1), get("L0_ffn_atom_in_b")[:, None]], 1)
    a["atom_out"] = get("L0_ffn_atom_out_w").transpose(0, 2, 1)
    flat = lambda n: get(n).transpose(1, 0, 2).reshape(D, NE * HE)
    a["w_gate_up"] = np.concatenate([flat("L1_ffn_w_gate"), get("L1_ffn_ws_gate"), flat("L1_ffn_w_up"), get("L1_ffn_ws_up")], 1)
    a["w_down"] = np.concatenate([get("L1_ffn_w_down").reshape(NE * HE, D), get("L1_ffn_ws_down")], 0)
    a["router"] = np.concatenate([get("L1_ffn_router_w"), get("L1_ffn_sg_w"), np.zeros((D, 1), np.float32)], 1)
    a["sg_b"] = get("L1_ffn_sg_b")
    select = np.zeros((2 * LOROW, MR + 1, P), np.float32)
    for m in range(MR + 1):
        for p in range(P):
            e = min((P * m + p) // HE, NE)
            select[e, m, p] = select[LOROW + e, m, p] = 1
    a["select"] = select
    return {n: np.ascontiguousarray(x) for n, x in a.items()}


def kernel(**inputs):
    import concourse.bacc as _bacc
    from concourse import mybir as _mybir
    from concourse.bass_utils import run_bass_kernel_spmd as _run
    arrays = arrange(inputs)
    nc = _bacc.Bacc("TRN2", target_bir_lowering=False, num_devices=1)
    io = {n: nc.dram_tensor("in_" + n, a.shape, _mybir.dt.from_np(a.dtype), kind="ExternalInput").ap() for n, a in arrays.items()}
    o = nc.dram_tensor("out0", (B, SEQ, D), _mybir.dt.float32, kind="ExternalOutput").ap()
    program(nc, io, o)
    r = _run(nc, [{"in_" + n: a for n, a in arrays.items()}], core_ids=[0])
    return r.results[0]["out0"]
```

```python
import math
from contextlib import ExitStack

import numpy as np
import concourse.bass as bass
from concourse import mybir
from concourse.alu_op_type import AluOpType as ALU

F32 = mybir.dt.float32
F32R = mybir.dt.float32r
I32 = mybir.dt.int32
ACT = mybir.ActivationFunctionType
AX = mybir.AxisListType

P = 128
B, SEQ, D = 8, 256, 192
TPB = SEQ // P
NT = B * TPB
DA, DB = P, D - P
NQ, NL = 6, 3
NANG = NL * 2 * NQ
VOCAB = 8000
EPS = 1e-5
TWO_PI = 2.0 * math.pi
PI_SAFE = 3.1415925
ROUND = 1.5 * 2.0 ** 23
TWO_PI_HI = 6.28125
TWO_PI_LO = TWO_PI - TWO_PI_HI
EVW = 32
NBANK = 512


def angle(layer, rz, q0=0, n=NQ):
    at = (2 * layer + rz) * NQ + q0
    return slice(at, at + n)


class Chain:

    def __init__(self, eng, sem):
        self.eng, self.sem, self.n = eng, sem, 0

    def __call__(self, ins):
        self.n += 1
        ins.then_inc(self.sem, 1)
        self.eng.wait_ge(self.sem, self.n)

    def go(self, ins):
        self.n += 1
        ins.then_inc(self.sem, 1)
        return self.n

    def after(self, n):
        self.eng.wait_ge(self.sem, n)


def moments(eng, link, buf, tiles):
    for t in tiles:
        n = link.go(eng.bn_stats(buf["st"][:, t, :], buf["H"][:, t, :]))
    for i, t in enumerate(tiles):
        link.after(n - len(tiles) + 1 + i)
        m = link.go(eng.bn_aggr(buf["mv"][:, t, :], buf["st"][:, t, :]))
    link.after(m)


def statistics_on_vector(eng, link, sem, buf, stage):
    mv, rstd, nmr = buf["mv"], buf["rstd"], buf["nmr"]
    eng.tensor_scalar(rstd[:, :], mv[:, :, 1], EPS, None, ALU.add).then_inc(sem["var_ready"], 1)
    eng.wait_ge(sem["std_ready"], stage + 1)
    link(eng.reciprocal(rstd[:, :], rstd[:, :]))
    link(eng.scalar_tensor_tensor(nmr[:, :], mv[:, :, 0], -1.0, rstd[:, :], ALU.mult, ALU.mult))


def root_on_scalar(eng, sem, buf, stage):
    eng.wait_ge(sem["var_ready"], stage + 1)
    eng.activation(buf["rstd"][:, :], buf["rstd"][:, :], ACT.Sqrt).then_inc(sem["std_ready"], 1)


def five(eng, out, w, xa, xb, cols, stationary_is_weight):
    pairs = [(w[0], xa[:, 0, cols]), (w[1], xa[:, 0, cols]), (w[0], xa[:, 1, cols]), (w[2], xb[:, cols]), (w[3], xb[:, cols])]
    for n, (ww, xx) in enumerate(pairs):
        a, b = (ww, xx) if stationary_is_weight else (xx, ww)
        ins = eng.matmul(out, a, b, start=n == 0, stop=n == 4)
    return ins


def circuit_on_vector(eng, link, sem, buf):
    v = eng
    T16 = NT
    theta, red, sn, cs = buf["theta"], buf["red"], buf["sn"], buf["cs"]
    R, ZM, XP, W, U, M = buf["R"], buf["ZM"], buf["XP"], buf["W"], buf["U"], buf["M"]
    E, PP, TZ, G, OZ, OX, evp = buf["E"], buf["PP"], buf["TZ"], buf["G"], buf["OZ"], buf["OX"], buf["evp"]

    def mul(o, a, b):
        link(v.tensor_tensor(o, a, b, ALU.mult))

    def add(o, a, b):
        link(v.tensor_tensor(o, a, b, ALU.add))

    def neg(o, a):
        link(v.tensor_scalar(o, a, -1.0, None, ALU.mult))

    def wide(a, shape):
        return a.broadcast_to(shape)

    link(v.memset(W[:, :, :, :], 0.0))
    link(v.memset(evp[:, :, :], 0.0))
    link(v.memset(evp[:, :, NQ:NQ + 1], 1.0))
    v_theta = theta[:, :, :]
    v.wait_ge(sem["theta_in"], 16 * NT)
    link(v.tensor_scalar(red[:, 1, :, :].rearrange("p c t -> p t c"), v_theta, 1.0 / TWO_PI, ROUND, ALU.mult, ALU.add))
    link(v.tensor_scalar(red[:, 1, :, :], red[:, 1, :, :], -ROUND, None, ALU.add))
    link(v.scalar_tensor_tensor(red[:, 0, :, :].rearrange("p c t -> p t c"), red[:, 1, :, :].rearrange("p c t -> p t c"),
                                -TWO_PI_HI, v_theta, ALU.mult, ALU.add))
    link(v.scalar_tensor_tensor(red[:, 0, :, :], red[:, 1, :, :], -TWO_PI_LO, red[:, 0, :, :], ALU.mult, ALU.add))
    link(v.tensor_scalar(red[:, 0, :, :], red[:, 0, :, :], PI_SAFE, -PI_SAFE, ALU.min, ALU.max))
    link(v.scalar_tensor_tensor(red[:, 1, :, :], red[:, 0, :, :], -1.0, red[:, 0, :, :], ALU.mult, ALU.min))
    v.tensor_scalar(red[:, 1, :, :], red[:, 1, :, :], math.pi / 2, None, ALU.add).then_inc(sem["angles_ready"], 1)

    v.wait_ge(sem["trig_ready"], 2)
    mul(R[:, 0, :, :], sn[:, angle(0, 0), :], cs[:, angle(0, 1), :])
    mul(R[:, 1, :, :], sn[:, angle(0, 0), :], sn[:, angle(0, 1), :])
    link(v.tensor_copy(R[:, 2, :, :], cs[:, angle(0, 0), :]))
    neg(R[:, 3, :, :], R[:, 1, :, :])
    neg(R[:, 4, :, :], R[:, 0, :, :])
    rX, rY, rZ, nrY, nrX = (R[:, i, :, :] for i in range(5))
    link(v.tensor_copy(ZM[:, 0, :, :], cs[:, angle(1, 0), :]))
    neg(ZM[:, 1, :, :], sn[:, angle(1, 0), :])
    neg(ZM[:, 2, :, :], sn[:, angle(1, 0), :])
    link(v.tensor_copy(ZM[:, 3, :, :], cs[:, angle(1, 0), :]))
    zZ, zX = ZM[:, 0, :, :], ZM[:, 1, :, :]
    mul(XP[:, 0, :, :], cs[:, angle(1, 1), :], cs[:, angle(1, 0), :])
    neg(XP[:, 1, :, :], sn[:, angle(1, 1), :])
    mul(XP[:, 2, :, :], cs[:, angle(1, 1), :], sn[:, angle(1, 0), :])
    link(v.tensor_copy(XP[:, 3, :, :], sn[:, angle(1, 1), :]))
    xX, xY, xZ, nxY = (XP[:, i, :, :] for i in range(4))

    link(v.memset(TZ[:, 3, :], 1.0))
    link(v.tensor_copy(TZ[:, 2, :], rZ[:, 5, :]))
    mul(TZ[:, 1, :], TZ[:, 2, :], rZ[:, 4, :])
    mul(TZ[:, 0, :], TZ[:, 1, :], rZ[:, 3, :])

    mul(W[:, 1, 8:0:-2, :], zX[:, 1:5, :], rX[:, 2:6, :])
    link(v.tensor_copy(W[:, 3, 8:0:-2, :], zZ[:, 1:5, :]))
    mul(G[:, 0:4, :], zZ[:, 1:5, :], rZ[:, 2:6, :])
    mul(W[:, 0, 9:1:-2, :], G[:, 0:4, :], TZ[:, :, :])
    mul(G[:, 0:4, :], zX[:, 1:5, :], nrY[:, 2:6, :])
    mul(W[:, 2, 9:1:-2, :], G[:, 0:4, :], TZ[:, :, :])
    link(v.tensor_copy(W[:, 1, 0, :], zX[:, 4, :]))
    mul(W[:, 3, 0, :], zZ[:, 4, :], rX[:, 5, :])
    mul(W[:, 0, 1, :], zZ[:, 4, :], rY[:, 5, :])
    mul(W[:, 2, 1, :], zX[:, 4, :], rZ[:, 5, :])
    mul(W[:, 1:3, 10, :], XP[:, 0:2, 1, :], wide(rX[:, 2, :].unsqueeze(1), [P, 2, T16]))
    link(v.tensor_copy(W[:, 3, 10, :], xZ[:, 1, :]))
    mul(W[:, 0, 11, :], xZ[:, 1, :], rZ[:, 2, :])
    mul(W[:, 1, 11, :], xY[:, 1, :], rY[:, 2, :])
    mul(W[:, 2, 11, :], xX[:, 1, :], nrY[:, 2, :])

    def contract(q, n):
        mul(M[:, 0:2, 0:n, :], W[:, 1::-1, 0:n, :], wide(rX[:, q, :].unsqueeze(1).unsqueeze(1), [P, 2, n, T16]))
        add(U[:, 3:0:-2, 0:n, :], W[:, 0:2, 0:n, :], M[:, 0:2, 0:n, :])
        mul(M[:, 0:2, 0:n, :], W[:, 2:4, 0:n, :], wide(R[:, 1:3, q, :].unsqueeze(2), [P, 2, n, T16]))
        mul(M[:, 2:4, 0:n, :], W[:, 2:4, 0:n, :], wide(R[:, 2:4, q, :].unsqueeze(2), [P, 2, n, T16]))
        add(U[:, 0:3:2, 0:n, :], M[:, 0:4:2, 0:n, :], M[:, 1:4:2, 0:n, :])

    for q in (3, 2, 1):
        n = 4 + 2 * (3 - q)
        contract(q + 1, n)
        mul(W[:, :, 0:n, :], U[:, :, 0:n, :], wide(ZM[:, :, q, :].unsqueeze(2), [P, 4, n, T16]))
    contract(1, 12)
    mul(M[:, 0:2, :, :], U[:, 0:4:3, :, :], wide(rZ[:, 0, :].unsqueeze(1).unsqueeze(1), [P, 2, 12, T16]))
    add(E[:, 0:2, :, :], U[:, 3::-3, :, :], M[:, 0:2, :, :])
    mul(M[:, 0:2, :, :], U[:, 1:3, :, :], wide(R[:, 0:2, 0, :].unsqueeze(2), [P, 2, 12, T16]))
    add(E[:, 2, :, :], M[:, 0, :, :], M[:, 1, :, :])
    mul(M[:, 0:2, :, :], U[:, 1:3, :, :], wide(R[:, 1:5:3, 0, :].unsqueeze(2), [P, 2, 12, T16]))
    add(E[:, 3, :, :], M[:, 0, :, :], M[:, 1, :, :])
    E_I, E_Z, E_X, E_Y = (E[:, i, :, :] for i in range(4))
    X4, Y4, I4, Z4, P1, T1 = 0, 1, 2, 3, 10, 11

    def dot(o, pairs, g=0):
        for n, (a, b) in enumerate(pairs):
            mul(o if n == 0 else G[:, g, :], a, b)
            if n:
                add(o, o, G[:, g, :])

    mul(G[:, 0:4, :], E_X[:, 8:0:-2, :], wide(zX[:, 0, :].unsqueeze(1), [P, 4, T16]))
    mul(G[:, 4:8, :], E_Z[:, 9:1:-2, :], wide(zZ[:, 0, :].unsqueeze(1), [P, 4, T16]))
    add(OZ[:, 1:5, :], G[:, 0:4, :], G[:, 4:8, :])
    dot(OZ[:, 0, :], [(zZ[:, 5, :], E_I[:, Z4, :]), (zX[:, 5, :], E_X[:, X4, :])])
    dot(G[:, 1, :], [(zX[:, 0, :], E_X[:, Z4, :]), (zZ[:, 0, :], E_Z[:, I4, :])])
    mul(G[:, 2, :], zX[:, 0, :], E_I[:, X4, :])
    mul(G[:, 3, :], zZ[:, 0, :], E_Y[:, Y4, :])
    link(v.tensor_tensor(G[:, 2, :], G[:, 2, :], G[:, 3, :], ALU.subtract))
    dot(OZ[:, 5, :], [(zZ[:, 5, :], G[:, 1, :]), (zX[:, 5, :], G[:, 2, :])])

    mul(PP[:, 0:2, 0:3, :], XP[:, 0:2, 2:5, :], wide(rX[:, 3:6, :].unsqueeze(1), [P, 2, 3, T16]))
    link(v.tensor_copy(PP[:, 2, 0:3, :], xZ[:, 2:5, :]))
    link(v.tensor_copy(PP[:, 0:2, 3, :], XP[:, 0:2, 5, :]))
    link(v.memset(PP[:, 2, 3, :], 0.0))
    pA, pB, pD = G[:, 8:12, :], G[:, 12:16, :], G[:, 16:20, :]
    pC = PP[:, 0, :, :]
    t0, t1 = G[:, 0:4, :], G[:, 4:8, :]
    vI, vX, vY, vZ = (G[:, 20 + 4 * i:24 + 4 * i, :] for i in range(4))
    mul(pA, PP[:, 0, :, :], rX[:, 2:6, :])
    mul(t0, PP[:, 1, :, :], rY[:, 2:6, :])
    mul(t1, PP[:, 2, :, :], rZ[:, 2:6, :])
    add(pB, t0, t1)
    mul(t0, PP[:, 1, :, :], rZ[:, 2:6, :])
    mul(t1, PP[:, 2, :, :], nrY[:, 2:6, :])
    add(pD, t0, t1)
    mul(vI, xZ[:, 1:5, :], pB)
    mul(vZ, xZ[:, 1:5, :], pA)
    mul(t0, xX[:, 1:5, :], pC)
    mul(t1, nxY[:, 1:5, :], pD)
    add(vX, t0, t1)
    mul(t0, xY[:, 1:5, :], pC)
    mul(t1, xX[:, 1:5, :], pD)
    add(vY, t0, t1)
    mul(t0, vX, rX[:, 1:5, :])
    add(pA, vI, t0)
    mul(t0, vY, rY[:, 1:5, :])
    mul(t1, vZ, rZ[:, 1:5, :])
    add(pB, t0, t1)
    CZ = G[:, 36:40, :]
    link(v.tensor_copy(CZ[:, 0, :], rZ[:, 0, :]))
    for q in (1, 2, 3):
        mul(CZ[:, q, :], CZ[:, q - 1, :], rZ[:, q, :])
    mul(t0[:, 0:3, :], pB[:, 0:3, :], CZ[:, 0:3, :])
    add(OX[:, 1:4, :], pA[:, 0:3, :], t0[:, 0:3, :])
    s = [G[:, 40 + i, :] for i in range(8)]
    mul(s[0], pA[:, 3, :], rX[:, 1, :])
    mul(s[0], s[0], rX[:, 0, :])
    mul(s[1], rZ[:, 3, :], rZ[:, 2, :])
    mul(s[1], s[1], pB[:, 3, :])
    mul(s[1], s[1], nrY[:, 1, :])
    mul(s[1], s[1], rY[:, 0, :])
    add(OX[:, 4, :], s[0], s[1])
    mul(s[0], xY[:, 4, :], rY[:, 5, :])
    mul(s[0], s[0], rX[:, 4, :])
    mul(s[1], xZ[:, 4, :], rZ[:, 5, :])
    add(s[0], s[0], s[1])
    mul(s[1], xX[:, 4, :], nrY[:, 5, :])
    mul(s[1], s[1], rY[:, 4, :])
    mul(s[1], s[1], CZ[:, 3, :])
    add(s[0], s[0], s[1])
    mul(s[0], s[0], xZ[:, 5, :])
    add(OX[:, 4, :], OX[:, 4, :], s[0])
    zeta, zeta5 = s[2], s[3]
    mul(zeta, rZ[:, 4, :], rZ[:, 3, :])
    mul(zeta5, zeta, rZ[:, 5, :])
    dot(s[4], [(xY[:, 0, :], E_Y[:, T1, :]), (xZ[:, 0, :], E_Z[:, T1, :])])
    dot(OX[:, 0, :], [(xX[:, 0, :], E_X[:, P1, :]), (zeta5, s[4])])
    dot(s[4], [(xY[:, 0, :], E_Y[:, P1, :]), (xZ[:, 0, :], E_Z[:, P1, :])])
    mul(s[5], xX[:, 0, :], zeta5)
    mul(s[5], s[5], E_X[:, T1, :])
    add(s[4], s[4], s[5])
    mul(OX[:, 5, :], xZ[:, 5, :], s[4])
    mul(s[5], zeta, rY[:, 5, :])
    mul(s[4], s[5], E_I[:, T1, :])
    mul(s[4], s[4], xY[:, 5, :])
    mul(s[6], rX[:, 5, :], E_I[:, P1, :])
    mul(s[6], s[6], xX[:, 5, :])
    add(s[4], s[4], s[6])
    mul(s[4], s[4], xX[:, 0, :])
    add(OX[:, 5, :], OX[:, 5, :], s[4])
    mul(s[4], xY[:, 0, :], E_Z[:, P1, :])
    mul(s[6], xZ[:, 0, :], E_Y[:, P1, :])
    link(v.tensor_tensor(s[4], s[4], s[6], ALU.subtract))
    mul(s[4], s[4], nxY[:, 5, :])
    mul(s[4], s[4], rX[:, 5, :])
    add(OX[:, 5, :], OX[:, 5, :], s[4])
    mul(s[4], xY[:, 0, :], E_Z[:, T1, :])
    mul(s[6], xZ[:, 0, :], E_Y[:, T1, :])
    link(v.tensor_tensor(s[4], s[4], s[6], ALU.subtract))
    mul(s[4], s[4], xX[:, 5, :])
    mul(s[4], s[4], s[5])
    add(OX[:, 5, :], OX[:, 5, :], s[4])

    mul(OZ[:, :, :], OZ[:, :, :], cs[:, angle(2, 0), :])
    mul(OX[:, :, :], OX[:, :, :], sn[:, angle(2, 0), :])
    v.tensor_tensor(evp[:, :, 0:NQ].rearrange("p t q -> p q t"), OZ[:, :, :], OX[:, :, :],
                    ALU.subtract).then_inc(sem["ev_ready"], 1)
NH, HD, NC = 8, 24, 4
QD = HD // NC
NU = NC + 1
HG = 4
SROW = 3 * 32 + HD
BIAS_ROWS = 2
VBLK = 32
QSIGN = [[1, -1, -1, -1], [1, 1, -1, 1], [1, 1, 1, -1], [1, -1, 1, 1]]
VSIGN = [[1, 1, 1, 1], [1, -1, 1, -1], [1, -1, -1, 1], [1, 1, -1, -1]]
LSIGN = [[1, 1, 1, 1], [-1, 1, -1, 1], [-1, 1, 1, -1], [-1, -1, 1, 1]]
NQKV = 2 * NU * P + D
NMAX, NEXP = 3, 2
BANK_MAX, BANK_EXP, BANK_AV, BANK_MISC = 0, NMAX, NMAX + NEXP, 6
VSLOT = 4

LEAD_X, LEAD_U, LEAD_V = -12, -11, -6
LAG_MAX, LAG_EXP, LAG_AV = 8, 10, 11
LAG_PAIR, LAG_OT, LAG_PROJ = 13, 20, 22
STEPS = range(LEAD_X, NH * (B - 1) + LAG_PROJ + 1)


def head_at(s, lag):
    n = s - lag
    return (n // NH, n % NH) if 0 <= n < NH * B else None


def misc_items(s):
    items = []
    if (s - LAG_MAX) % NH == 0 and 0 <= (s - LAG_MAX) // NH < B:
        items.append(("max", (s - LAG_MAX) // NH))
    if (s - LEAD_X) % NH == 0 and 0 <= (s - LEAD_X) // NH < B:
        items.append(("x", (s - LEAD_X) // NH))
    for u in range(NU):
        if (s - LEAD_U - u) % NH == 0 and 0 <= (s - LEAD_U - u) // NH < B:
            items.append(("u", (s - LEAD_U - u) // NH, u))
    if (s - LEAD_V) % NH == 0 and 0 <= (s - LEAD_V) // NH < B:
        items.append(("v", (s - LEAD_V) // NH))
    for k in range(NH // 2):
        if (s - LAG_PAIR - 2 * k) % NH == 0 and 0 <= (s - LAG_PAIR - 2 * k) // NH < B:
            items.append(("pair", (s - LAG_PAIR - 2 * k) // NH, k))
    if (s - LAG_OT) % NH == 0 and 0 <= (s - LAG_OT) // NH < B:
        items.append(("ot", (s - LAG_OT) // NH))
    if (s - LAG_PROJ) % NH == 0 and 0 <= (s - LAG_PROJ) // NH < B:
        items.append(("proj", (s - LAG_PROJ) // NH))
    assert len(items) <= 2
    return items


def misc_uses():
    return {item: n for n, item in enumerate(item for s in STEPS for item in misc_items(s))}


def wait_misc_done(eng, sem, n):
    eng.wait_ge(sem[f"misc_free{n % 2}"], n // 2 + 1)


def attention_on_tensor(nc, eng, sem, buf, ps):
    use = misc_uses()
    W, xa, xb = buf["wqkv"], buf["xa"], buf["xb"]
    QK, VS, PT, OTs, ident = buf["QK"], buf["VS"], buf["PT"], buf["OTs"], buf["ident"]

    def do_misc(item):
        n, kind, b = use[item], item[0], item[1]
        misc = ps[:, BANK_MISC + n % 2, :]
        if n >= 2:
            wait_misc_done(eng, sem, n - 2)
        if kind == "x":
            eng.wait_ge(sem["xn_ready"], b + 1)
            for t in range(TPB):
                eng.transpose(misc[:, P * t:P * t + P], buf["xn"][:, b % 2, t, 0:DA], ident[:, :])
            for t in range(TPB):
                ins = eng.transpose(misc[0:DB, SEQ + P * t:SEQ + P * t + P], buf["xn"][:, b % 2, t, DA:D], ident[:, :])
        elif kind == "u":
            u = item[2]
            if u == 0:
                eng.wait_ge(sem["xs_half"], b + 1)
                wait_misc_done(eng, sem, use[("x", b)])
            for g in range(2):
                c = (2 * u + g) * P
                ins = five(eng, misc[:, SEQ * g:SEQ * g + SEQ], [W[:, s, c:c + P] for s in range(4)], xa, xb, slice(0, SEQ), True)
        elif kind == "v":
            for t in range(TPB):
                ins = five(eng, misc[:, D * t:D * t + D], [W[:, s, 2 * NU * P:NQKV] for s in range(4)], xa, xb,
                           slice(P * t, P * t + P), False)
        elif kind == "pair":
            k = item[2]
            eng.wait_ge(sem["av_out"], NH * b + 2 * k + 2)
            for hh in range(2):
                for t in range(TPB):
                    at = P * (2 * hh + t)
                    ins = eng.transpose(misc[:, at:at + P], OTs[:, (2 * k + hh) % 4, P * t:P * t + P], ident[:, :])
        elif kind == "max":
            eng.wait_ge(sem["mx_done"], 4 * NH * (b + 1))
            for t in range(TPB):
                ins = eng.transpose(misc[0:NC * NH, P * t:P * t + P], buf["mx"][:, b % 2, t, :], ident[:, :])
        elif kind == "ot":
            eng.wait_ge(sem["o_ready"], 4 * (b + 1))
            for t in range(TPB):
                eng.transpose(misc[:, P * t:P * t + P], buf["o"][:, t, 0:DA], ident[:, :])
            for t in range(TPB):
                ins = eng.transpose(misc[0:DB, SEQ + P * t:SEQ + P * t + P], buf["o"][:, t, DA:D], ident[:, :])
        elif kind == "proj":
            eng.wait_ge(sem["ot_half"], b + 1)
            wait_misc_done(eng, sem, use[("ot", b)])
            for t in range(TPB):
                out = misc[:, D * t:D * t + D]
                eng.matmul(out, buf["ot"][:, P * t:P * t + P], buf["wp"][:, 0, :], start=True, stop=False)
                ins = eng.matmul(out, buf["ot"][0:DB, SEQ + P * t:SEQ + P * t + P], buf["wp"][0:DB, 1, :],
                                 start=False, stop=True)
        ins.then_inc(sem["misc_full"], 1)

    def scores_for_max(b, h, k):
        t, cp = k // 2, k % 2
        n = 4 * (NH * b + h) + k
        if n >= NMAX:
            eng.wait_ge(sem["mx_done"], n - NMAX + 1)
        for c in (2 * cp, 2 * cp + 1):
            ins = eng.matmul(ps[:, BANK_MAX + n % NMAX, SEQ * (c % 2):SEQ * (c % 2) + SEQ],
                             QK[0:SROW, b % 2, c, h, P * t:P * t + P], QK[0:SROW, b % 2, NC, h, :],
                             start=True, stop=True)
        ins.then_inc(sem["p1_full"], 1)

    def scores_for_exp(b, h, k):
        t, cp = k // 2, k % 2
        n = 4 * (NH * b + h) + k
        if n >= NEXP:
            eng.wait_ge(sem["exp_done"], n - NEXP + 1)
        eng.matmul(ps[:, BANK_EXP + n % NEXP, :], QK[0:SROW + BIAS_ROWS, b % 2, NC, h, P * t:P * t + P],
                   QK[0:SROW + BIAS_ROWS, b % 2, 2 * cp:2 * cp + 2, h, :], start=True, stop=True).then_inc(sem["p2_full"], 1)

    def values(b, h):
        n = NH * b + h
        if h == 0:
            eng.wait_ge(sem["vs_half"], b + 1)
            wait_misc_done(eng, sem, use[("v", b)])
        eng.wait_ge(sem["exp_done"], 4 * (n + 1))
        if n:
            eng.wait_ge(sem["av_out"], n)
        for t in range(TPB):
            for c in range(NC):
                ins = eng.matmul(ps[VBLK * c:VBLK * c + VBLK, BANK_AV, 0:SEQ], VS[:, b % VSLOT, t, h, :, :].rearrange("p a e -> p (a e)"),
                                 PT[:, n % 2, t, c, :], start=t == 0, stop=t == TPB - 1)
        ins.then_inc(sem["av_full"], 1)

    eng.wait_ge(sem["wqkv_ready"], 1)
    eng.wait_ge(sem["wp_ready"], 1)
    eng.wait_ge(sem["vs_clear"], 1)
    for s in STEPS:
        m, x, v = head_at(s, 0), head_at(s, LAG_EXP), head_at(s, LAG_AV)
        items = misc_items(s)
        if m:
            if m[1] % 2 == 0:
                eng.wait_ge(sem[f"qk_in{m[0] % 2}{m[1] // 2}"], 96 * (m[0] // 2 + 1))
            scores_for_max(*m, 0)
            scores_for_max(*m, 1)
        if x:
            if x[1] == 0:
                eng.wait_ge(sem["nm_in"], 32 * (x[0] + 1))
            scores_for_exp(*x, 0)
            scores_for_exp(*x, 1)
        for item in items[:1]:
            do_misc(item)
        for k in (2, 3):
            if m:
                scores_for_max(*m, k)
            if x:
                scores_for_exp(*x, k)
            if k == 2 and v:
                values(*v)
        for item in items[1:]:
            do_misc(item)


def attention_on_scalar(nc, eng, sem, buf, ps):
    use = misc_uses()
    VS, PT, OTs, HL = buf["VS"], buf["PT"], buf["OTs"], buf["HL"]

    def do_misc(item):
        n, kind, b = use[item], item[0], item[1]
        misc = ps[:, BANK_MISC + n % 2, :]
        if kind in ("x", "u", "v", "ot"):
            eng.wait_ge(sem["misc_full"], n + 1)
        if kind == "x":
            if b:
                eng.wait_ge(sem["misc_full"], use[("v", b - 1)] + 1)
            eng.activation(buf["xa"][:, 0, :], misc[:, 0:SEQ], ACT.Copy).then_inc(sem["hi_ready"], 1)
            eng.activation(buf["xb"][0:DB, :], misc[0:DB, SEQ:2 * SEQ], ACT.Copy).then_inc(sem["hi_ready"], 1)
        elif kind == "u":
            u = item[2]
            if b >= 2 and u == 0:
                for j in range(HG):
                    eng.wait_ge(sem[f"qk_in{b % 2}{j}"], 96 * (b // 2))
            eng.activation(HL[:, b % 2, 0, u, :, :].rearrange("p g n -> p (g n)"), misc, ACT.Copy).then_inc(sem["hi_ready"], 1)
        elif kind == "v":
            if b >= VSLOT:
                eng.wait_ge(sem["av_full"], NH * (b - VSLOT + 1))
            for t in range(TPB):
                src = misc[:, D * t:D * t + D].rearrange("p (h a e) -> p h a e", h=NH, e=QD)
                eng.activation(VS[:, b % VSLOT, t, :, :, 0:QD], src, ACT.Copy)\
                   .then_inc(sem["vs_half"] if t == 0 else sem[f"misc_free{n % 2}"], 1)
        elif kind == "ot":
            eng.activation(buf["ot"][:, 0:SEQ], misc[:, 0:SEQ], ACT.Copy).then_inc(sem["ot_half"], 1)
            eng.activation(buf["ot"][0:DB, SEQ:2 * SEQ], misc[0:DB, SEQ:2 * SEQ], ACT.Copy).then_inc(sem[f"misc_free{n % 2}"], 1)

    def exponentials(b, h, k):
        t, cp = k // 2, k % 2
        m = NH * b + h
        n = 4 * m + k
        eng.wait_ge(sem["p2_full"], n + 1)
        if m >= 2 and k == 0:
            eng.wait_ge(sem["av_full"], m - 1)
        eng.activation(PT[:, m % 2, t, 2 * cp:2 * cp + 2, :].rearrange("p c n -> p (c n)"), ps[:, BANK_EXP + n % NEXP, :],
                       ACT.Exp, scale=float(HD) ** -0.5).then_inc(sem["exp_done"], 1)

    def copy_out(b, h):
        n = NH * b + h
        eng.wait_ge(sem["av_full"], n + 1)
        if n >= 4:
            m = n - 4
            eng.wait_ge(sem["misc_full"], use[("pair", m // NH, m % NH // 2)] + 1)
        eng.activation(OTs[:, h % 4, :], ps[:, BANK_AV, 0:SEQ], ACT.Copy).then_inc(sem["av_out"], 1)

    for s in STEPS:
        x, v = head_at(s, LAG_EXP), head_at(s, LAG_AV)
        items = misc_items(s)
        if x:
            exponentials(*x, 0)
        for item in items[:1]:
            do_misc(item)
        if x:
            exponentials(*x, 1)
            exponentials(*x, 2)
        if v:
            copy_out(*v)
        for item in items[1:]:
            do_misc(item)
        if x:
            exponentials(*x, 3)


def attention_on_vector(nc, eng, link, sem, buf, ps):
    use = misc_uses()
    H, HL = buf["H"], buf["HL"]
    hi_seen = [0]

    def hi(n=1):
        hi_seen[0] += n
        eng.wait_ge(sem["hi_ready"], hi_seen[0])

    def normalize(b):
        if b >= 2:
            eng.wait_ge(sem["misc_full"], use[("x", b - 2)] + 1)
        for t in range(TPB):
            k = TPB * b + t
            ins = eng.tensor_scalar(buf["xn"][:, b % 2, t, :], H[:, k, :], buf["rstd"][:, k:k + 1], buf["nmr"][:, k:k + 1],
                                    ALU.mult, ALU.add)
            if t < TPB - 1:
                link(ins)
            else:
                ins.then_inc(sem["xn_ready"], 1)

    def do_misc(item):
        n, kind, b = use[item], item[0], item[1]
        misc, free = ps[:, BANK_MISC + n % 2, :], sem[f"misc_free{n % 2}"]
        if kind == "x":
            hi(2)
            eng.tensor_tensor(buf["xa"][:, 1, :], misc[:, 0:SEQ], buf["xa"][:, 0, :].bitcast(F32), ALU.subtract).then_inc(sem["xs_half"], 1)
            eng.tensor_tensor(buf["xb"][DB:P, :], misc[0:DB, SEQ:2 * SEQ], buf["xb"][0:DB, :].bitcast(F32),
                              ALU.subtract).then_inc(free, 1)
        elif kind == "u":
            u = item[2]
            hi()
            halves = [HL[:, b % 2, k, u, :, :].rearrange("p g n -> p (g n)") for k in range(2)]
            eng.tensor_tensor(halves[1], misc, halves[0].bitcast(F32), ALU.subtract).then_inc(free, 1)
        elif kind == "pair":
            k = item[2]
            eng.wait_ge(sem["misc_full"], n + 1)
            G = misc.rearrange("p (g e) -> p g e", e=8)
            link(eng.reciprocal(buf["rec"][:, :], G[:, 0:64:NC, QD]))
            link(eng.tensor_tensor(buf["rs"][:, :, :, :], buf["rec"][:, :].rearrange("p (k c) -> p k c", c=NC).unsqueeze(3).broadcast_to([P, 4, NC, NC]),
                                   buf["vsign"][:, :, :].unsqueeze(1).broadcast_to([P, 4, NC, NC]), ALU.mult))
            TM = buf["TM"]
            eng.tensor_tensor(TM[:, :, :, :, :].rearrange("p c k a e -> p k c a e"),
                              G[:, :, 0:QD].rearrange("p (k c a) e -> p k c a e", c=NC, a=NC),
                              buf["rs"][:, :, :, :].unsqueeze(4).broadcast_to([P, 4, NC, NC, QD]), ALU.mult).then_inc(free, 1)
            wait_misc_done(eng, sem, n)
            T0, T1, T2, T3 = (TM[:, c, :, :, :] for c in range(NC))
            f = lambda a: a.rearrange("p k (x y) e -> p (k x) y e", y=2)
            link(eng.tensor_tensor(f(T0), f(T0), f(T1)[:, :, ::-1, :], ALU.add))
            g = lambda a: a.rearrange("p k (x y) e -> p k x (y e)", y=2)
            link(eng.tensor_tensor(g(T0), g(T0), g(T2)[:, :, ::-1, :], ALU.add))
            if b and k == 0:
                eng.wait_ge(sem["misc_full"], use[("ot", b - 1)] + 1)
            dst = buf["o"][:, :, 2 * HD * k:2 * HD * k + 2 * HD].rearrange("p t (h a e) -> p h t a e", h=2, a=NC)
            m = lambda a: a.rearrange("p (h t) a e -> p h t a e", h=2)
            eng.tensor_tensor(dst, m(T0), m(T3[:, :, ::-1, :]), ALU.add).then_inc(sem["o_ready"], 1)
            eng.wait_ge(sem["o_ready"], 4 * b + k + 1)
        elif kind == "max":
            eng.wait_ge(sem["misc_full"], n + 1)
            if b:
                eng.wait_ge(sem["nm_in"], 32 * b)
            M = NC * NH
            eng.tensor_scalar(buf["nm"][0:M, 0, :], misc[0:M, 0:SEQ], -1.0, None, ALU.mult).then_inc(sem["nm_ready"], 1)
            eng.wait_ge(sem["nm_ready"], b + 1)
            eng.scalar_tensor_tensor(buf["nm"][0:M, 1, :], misc[0:M, 0:SEQ], -1.0, buf["nm"][0:M, 0, :].bitcast(F32),
                                     ALU.mult, ALU.subtract).then_inc(free, 1)
        elif kind == "proj":
            eng.wait_ge(sem["misc_full"], n + 1)
            eng.wait_ge(sem["bp_added"], b + 1)
            dst = H[:, TPB * b:TPB * b + TPB, :]
            eng.tensor_tensor(dst, misc[:, 0:TPB * D].rearrange("p (t d) -> p t d", t=TPB), dst, ALU.add).then_inc(free, 1)
            wait_misc_done(eng, sem, n)
            moments(eng, link, buf, range(TPB * b, TPB * b + TPB))

    def maximum(b, h, k):
        t, cp = k // 2, k % 2
        n = 4 * (NH * b + h) + k
        if b >= 2 and h == 0 and k == 0:
            eng.wait_ge(sem["misc_full"], use[("max", b - 2)] + 1)
        eng.wait_ge(sem["p1_full"], n + 1)
        eng.reduce_max(buf["mx"][:, b % 2, t, :].rearrange("p (c h) -> p c h", h=NH)[:, 2 * cp:2 * cp + 2, h],
                       ps[:, BANK_MAX + n % NMAX, :].rearrange("p (c n) -> p c n", c=2), AX.X).then_inc(sem["mx_done"], 1)

    normalize(0)
    for s in STEPS:
        m = head_at(s, 0)
        items = misc_items(s)
        if m:
            for k in range(3):
                maximum(*m, k)
        for item in items[:1]:
            do_misc(item)
        if m:
            maximum(*m, 3)
        for item in items[1:]:
            do_misc(item)
        if (s - LEAD_X) % NH == NH - 2 and (s - LEAD_X) // NH + 1 < B:
            normalize((s - LEAD_X) // NH + 1)


def attention_on_sync(nc, eng, sem, buf):
    use = misc_uses()
    QK, HL, nm = buf["QK"], buf["HL"], buf["nm"]
    eng.wait_ge(sem["qk_clear"], 2)
    for s in STEPS:
        if ("max", (s - LAG_MAX) // NH) in misc_items(s):
            b = (s - LAG_MAX) // NH
            eng.wait_ge(sem["nm_ready"], b + 1)
            wait_misc_done(eng, sem, use[("max", b)])
            if b >= 2:
                eng.wait_ge(sem["p2_full"], 4 * NH * (b - 1))
            for k in range(2):
                eng.dma_start(QK[SROW + k:SROW + k + 1, b % 2, 0:NC, :, :].bitcast(F32),
                              nm[0:NC * NH, k, :].bitcast(F32)).then_inc(sem["nm_in"], 16)
        n = s - LAG_EXP + 2 * NH - 1
        b, j = n // NH, n % NH // 2
        if n % 2 == 0 and 0 <= b < B:
            wait_misc_done(eng, sem, use[("u", b, NU - 1)])
            wait_misc_done(eng, sem, use[("u", b, NU - 2)])
            if b >= 2:
                eng.wait_ge(sem["p2_full"], 4 * (NH * (b - 2) + 2 * j + 2))
            for blk, parts in ((0, [(0, 0, NU)]), (1, [(1, 0, NC), (0, NC, NU)]), (2, [(0, 0, NC), (1, NC, NU)]), (3, [(1, 0, NU)])):
                for half, u0, u1 in parts:
                    eng.dma_start(QK[32 * blk:32 * blk + HD, b % 2, u0:u1, 2 * j:2 * j + 2, :].rearrange("r u g n -> r u (g n)").bitcast(F32),
                                  HL[32 * j:32 * j + HD, b % 2, half, u0:u1, :, :].rearrange("r u g n -> r u (g n)").bitcast(F32)).then_inc(sem[f"qk_in{b % 2}{j}"], 16)
GT = 4
NG = NT // GT
GW = GT * P
SPLIT = (True, False, True)
HI_BASE = (0, 2 * NG, 3 * NG)


def transposed_on_vector(eng, link, sem, buf, ps, k):
    H, xn = buf["H"], buf[f"xn{k}"]
    for t in range(NT):
        eng.tensor_scalar(xn[:, t, :], H[:, t, :], buf["rstd"][:, t:t + 1], buf["nmr"][:, t:t + 1],
                          ALU.mult, ALU.add).then_inc(sem["xt_xn"], 1)
    if SPLIT[k]:
        xa, xb = buf[f"xa{k}"], buf[f"xb{k}"]
        for g in range(NG):
            cols, bank = slice(GW * g, GW * g + GW), 2 * (g % 2)
            eng.wait_ge(sem["xt_hi"], HI_BASE[k] + 2 * (g + 1))
            eng.tensor_tensor(xa[:, 1, cols], ps[:, bank, :], xa[:, 0, cols].bitcast(F32), ALU.subtract).then_inc(sem["xt_lo"], 1)
            eng.tensor_tensor(xb[DB:P, cols], ps[0:DB, bank + 1, :], xb[0:DB, cols].bitcast(F32), ALU.subtract).then_inc(sem["xt_free"], 1)


def transposed_on_tensor(eng, sem, buf, ps, k):
    for g in range(NG):
        n, bank = NG * k + g, 2 * (g % 2)
        eng.wait_ge(sem["xt_xn"], NT * k + GT * (g + 1))
        if n >= 2:
            eng.wait_ge(sem["xt_free"], n - 1)
        for t in range(GT):
            eng.transpose(ps[:, bank, P * t:P * t + P], buf[f"xn{k}"][:, GT * g + t, 0:DA], buf["ident"][:, :])
        for t in range(GT):
            ins = eng.transpose(ps[0:DB, bank + 1, P * t:P * t + P], buf[f"xn{k}"][:, GT * g + t, DA:D], buf["ident"][:, :])
        ins.then_inc(sem["xt_full"], 1)


def transposed_on_scalar(eng, sem, buf, ps, k):
    for g in range(NG):
        cols, bank = slice(GW * g, GW * g + GW), 2 * (g % 2)
        eng.wait_ge(sem["xt_full"], NG * k + g + 1)
        if SPLIT[k]:
            eng.activation(buf[f"xa{k}"][:, 0, cols], ps[:, bank, :], ACT.Copy).then_inc(sem["xt_hi"], 1)
            eng.activation(buf[f"xb{k}"][0:DB, cols], ps[0:DB, bank + 1, :], ACT.Copy).then_inc(sem["xt_hi"], 1)
        else:
            eng.activation(buf["xtA"][:, cols], ps[:, bank, :], ACT.Copy).then_inc(sem["xt_hi"], 1)
            eng.activation(buf["xtB"][:, cols], ps[0:DB, bank + 1, :], ACT.Copy).then_inc(sem["xt_free"], 1)


def x_ready(eng, sem, k, g):
    eng.wait_ge(sem["xt_free"], NG * k + g + 1)
    eng.wait_ge(sem["xt_hi"], HI_BASE[k] + (2 if SPLIT[k] else 1) * (g + 1))
    if SPLIT[k]:
        eng.wait_ge(sem["xt_lo"], NG * (k // 2) + g + 1)


def load_runs(eng, dst, src, sem):
    eng.dma_start(dst[:, 0, :], src[0:DA, :]).then_inc(sem, 16)
    for half in range(2):
        eng.dma_start(dst[DB * half:DB * half + DB, 1, :], src[DA:D, :]).then_inc(sem, 16)


HF = 768
MF = HF // P
NCLS, NA = 6, 5
NCT = B * NCLS
LEFT = 3


def classes_of(atom):
    return slice(2 * atom, 2 * atom + 2) if atom < LEFT else slice(atom - LEFT, NCLS, 2)


def ffn0_on_sync(eng, sem, buf, io):
    eng.wait_ge(sem["misc_full"], misc_uses()[("v", B - 1)] + 1)
    load_runs(eng, buf["w1f"], io["fc1"], sem["w1_in"])
    eng.dma_start(buf["w2"][:, :, :], io["fc2"].rearrange("(m p) d -> p m d", p=P)).then_inc(sem["w2_in"], 16)
    eng.wait_ge(sem["p2_full"], 4 * NH * (B - 1))
    eng.dma_start(buf["b1"][:, :], io["fc1_b"]).then_inc(sem["b1_in"], 16)
    eng.dma_start(buf["b2"][:, :], io["fc2_b"].partition_broadcast(P)).then_inc(sem["b2_in"], 16)
    eng.dma_start(buf["gp"][0:NCT, :, :], io["gate_pair"]).then_inc(sem["gate_in"], 16)
    eng.dma_start(buf["bal"][0:NCT, :], io["balance"]).then_inc(sem["gate_in"], 16)
    eng.dma_start(buf["aob"][0:NCT, :, :], io["atom_out_b"]).then_inc(sem["aob_in"], 16)
    eng.dma_start(buf["ain"][:, :, 0, :], io["atom_in"][:, 0:DA, :].rearrange("a p h -> p a h")).then_inc(sem["ain_in"], 16)
    eng.dma_start(buf["ain"][0:DB + 1, :, 1, :], io["atom_in"][:, DA:D + 1, :].rearrange("a p h -> p a h")).then_inc(sem["ain_in"], 16)
    eng.wait_ge(sem["p2_full"], 4 * NH * B)
    eng.dma_start(buf["aout"][:, :, :, :], io["atom_out"].rearrange("a (m p) d -> p a m d", p=P)).then_inc(sem["aout_in"], 16)
    wait_misc_done(eng, sem, len(misc_uses()) - 1)
    for b in range(B):
        eng.dma_start(buf["hc"][NCLS * b:NCLS * b + NCLS, :], buf["H"][0:NCLS, TPB * b, :]).then_inc(sem["hc_in"], 16)
    for b in range(B):
        eng.wait_ge(sem["xt_xn"], TPB * b + 1)
        eng.dma_start(buf["xc"][NCLS * b:NCLS * b + NCLS, :], buf["xn0"][0:NCLS, TPB * b, :]).then_inc(sem["xc_in"], 16)
    eng.wait_ge(sem["cls_done"], 1)
    for b in range(B):
        eng.wait_ge(sem["f0_add"], TPB * b + 1)
        eng.dma_start(buf["H"][0:NCLS, TPB * b, :], buf["hc"][NCLS * b:NCLS * b + NCLS, :]).then_inc(sem["h2_in"], 16)


def ffn0_on_gpsimd(eng, link, sem, buf):
    W, wf = buf["w1"], buf["w1f"]
    eng.wait_ge(sem["w1_in"], 48)
    link(eng.tensor_copy(W[:, 0:4:2, :], wf[:, :, :]))
    eng.tensor_tensor(W[:, 1:4:2, :], wf[:, :, :], W[:, 0:4:2, :].bitcast(F32), ALU.subtract).then_inc(sem["w1_ready"], 1)
    wait_misc_done(eng, sem, len(misc_uses()) - 1)
    eng.memset(buf["mh"][:, :, :, :], 0.0).then_inc(sem["mh_zero"], 1)
    eng.memset(buf["xct"][:, :, :], 1.0).then_inc(sem["xct_ones"], 1)
    eng.wait_ge(sem["b2_in"], 16)
    eng.wait_ge(sem["hc_in"], 16 * B)
    for t in range(0, NT, 2):
        eng.wait_ge(sem["xt_xn"], t + 2)
        tiles = buf["H"][:, t:t + 2, :]
        eng.tensor_tensor(tiles, tiles, buf["b2"][:, :].unsqueeze(1).broadcast_to([P, 2, D]), ALU.add).then_inc(sem["b2_added"], 1)


def ffn0_on_tensor(eng, sem, buf, ps):
    w1, w2, hid, mh, ident = buf["w1"], buf["w2"], buf["hid0"], buf["mh"], buf["ident"]
    xct = buf["xct"]
    transposed_on_tensor(eng, sem, buf, ps, 0)

    def hidden(g):
        x_ready(eng, sem, 0, g)
        for m in range(MF):
            n = MF * g + m
            if n >= 2:
                eng.wait_ge(sem["f0_act"], n - 1)
            five(eng, ps[:, 4 + n % 2, :], [w1[:, s, P * m:P * m + P] for s in range(4)], buf["xa0"], buf["xb0"],
                 slice(GW * g, GW * g + GW), True).then_inc(sem["f0_full"], 1)

    def down(g):
        eng.wait_ge(sem["f0_act"], MF * (g + 1))
        for t in range(GT):
            n = GT * g + t
            if n >= 2:
                eng.wait_ge(sem["f0_add"], n - 1)
            for m in range(MF):
                ins = eng.matmul(ps[:, 6 + n % 2, 0:D], hid[:, g % 2, m, P * t:P * t + P], w2[:, m, :],
                                 start=m == 0, stop=m == MF - 1)
            ins.then_inc(sem["f0_out"], 1)

    eng.wait_ge(sem["w1_ready"], 1)
    hidden(0)
    eng.wait_ge(sem["xc_in"], 16 * B)
    eng.wait_ge(sem["xt_free"], NG)
    eng.transpose(ps[:, 0, 0:NCT], buf["xc"][0:NCT, 0:DA], ident[0:NCT, 0:NCT])
    eng.transpose(ps[0:DB, 0, 64:64 + NCT], buf["xc"][0:NCT, DA:D], ident[0:NCT, 0:NCT]).then_inc(sem["xct_psum"], 1)
    hidden(1)
    eng.wait_ge(sem["xct_ready"], 2)
    eng.wait_ge(sem["ain_in"], 32)
    for a in range(NA):
        n = 2 if a < LEFT else 3
        if a >= 2:
            eng.wait_ge(sem["atom_act"], sum(2 if x < LEFT else 3 for x in range(a - 1)))
        xs = [xct[0:k, r, :].rearrange("k (b n) -> k b n", n=NCLS)[:, :, classes_of(a)] for r, k in ((0, P), (1, DB + 1))]
        for m in range(MF):
            out = ps[:, 1 + a % 2, 24 * m:24 * m + B * n].rearrange("p (b n) -> p b n", n=n)
            eng.matmul(out, buf["ain"][:, a, 0, P * m:P * m + P], xs[0], start=True, stop=False)
            ins = eng.matmul(out, buf["ain"][0:DB + 1, a, 1, P * m:P * m + P], xs[1], start=False, stop=True)
        ins.then_inc(sem["atom_full"], 1)
    eng.wait_ge(sem["w2_in"], 16)
    down(0)
    hidden(2)
    down(1)
    eng.wait_ge(sem["aout_in"], 16)
    eng.wait_ge(sem["atom_act"], 12)
    for r, atoms in ((0, (3, 4)), (1, (0, 1, 2))):
        for i, a in enumerate(atoms):
            for m in range(MF):
                ins = eng.matmul(ps[0:NCT, 3, D * r:D * r + D], mh[:, a, m, :], buf["aout"][:, a, m, :],
                                 start=i + m == 0, stop=i == len(atoms) - 1 and m == MF - 1)
    ins.then_inc(sem["cand_full"], 1)
    hidden(3)
    down(2)
    down(3)


def ffn0_on_scalar(eng, sem, buf, ps):
    transposed_on_scalar(eng, sem, buf, ps, 0)
    eng.wait_ge(sem["gate_sq"], 1)
    eng.activation(buf["gs"][0:NCT, 2:5], buf["gs"][0:NCT, 2:5], ACT.Sqrt).then_inc(sem["gate_root"], 1)
    eng.wait_ge(sem["gate_shift"], 1)
    eng.activation(buf["ge"][0:NCT, :], buf["gl"][0:NCT, :], ACT.Exp).then_inc(sem["gate_exp"], 1)
    eng.wait_ge(sem["b1_in"], 16)

    def gelus(g):
        for m in range(MF):
            n = MF * g + m
            eng.wait_ge(sem["f0_full"], n + 1)
            if g >= 2:
                eng.wait_ge(sem["f0_out"], GT * (g - 1))
            eng.activation(buf["hid0"][:, g % 2, m, :], ps[:, 4 + n % 2, :], ACT.Gelu, bias=buf["b1"][:, m:m + 1]).then_inc(sem["f0_act"], 1)

    gelus(0)
    eng.wait_ge(sem["xct_psum"], 1)
    eng.wait_ge(sem["xct_ones"], 1)
    eng.activation(buf["xct"][:, 0, :], ps[:, 0, 0:NCT], ACT.Copy).then_inc(sem["xct_ready"], 1)
    eng.activation(buf["xct"][0:DB, 1, :], ps[0:DB, 0, 64:64 + NCT], ACT.Copy).then_inc(sem["xct_ready"], 1)
    gelus(1)
    eng.wait_ge(sem["mh_zero"], 1)
    for a in range(NA):
        eng.wait_ge(sem["atom_full"], a + 1)
        first, n = (2 * a, 2) if a < LEFT else (a - LEFT, 3)
        for k in range(n):
            cls = first + (k if a < LEFT else 2 * k)
            dst = LEFT + cls % 2 if a < LEFT else cls // 2
            src = ps[:, 1 + a % 2, 0:24 * MF].rearrange("p (m j) -> p m j", j=24)[:, :, k:k + (B - 1) * n + 1:n]
            out = buf["mh"][:, dst, :, :].rearrange("p m (b c) -> p m b c", c=NCLS)[:, :, :, cls]
            eng.activation(out, src, ACT.Gelu).then_inc(sem["atom_act"], 1)
    gelus(2)
    gelus(3)


def ffn0_on_vector(eng, link, sem, buf, ps):
    wait_misc_done(eng, sem, len(misc_uses()) - 1)
    statistics_on_vector(eng, link, sem, buf, 1)
    transposed_on_vector(eng, link, sem, buf, ps, 0)
    xc, gp, gq, gs, gl, ge, gr = (buf[n] for n in ("xc", "gp", "gq", "gs", "gl", "ge", "gr"))
    C = slice(0, NCT)
    eng.wait_ge(sem["xc_in"], 16 * B)
    eng.wait_ge(sem["gate_in"], 32)
    link(eng.tensor_tensor(gq[C, 0:2, :], gp[C, :, :], xc[C, :].unsqueeze(1).broadcast_to([NCT, 2, D]), ALU.mult))
    link(eng.tensor_tensor(gq[C, 2:4, :], gp[C, :, :], gp[C, :, :], ALU.mult))
    link(eng.tensor_tensor(gq[C, 4, :], xc[C, :], xc[C, :], ALU.mult))
    eng.reduce_sum(gs[C, 0:5], gq[C, :, :], AX.X).then_inc(sem["gate_sq"], 1)
    eng.wait_ge(sem["gate_root"], 1)
    link(eng.tensor_scalar(gs[C, 2:5], gs[C, 2:5], 1e-12, None, ALU.max))
    link(eng.reciprocal(gs[C, 2:5], gs[C, 2:5]))
    link(eng.tensor_tensor(gl[C, :], gs[C, 0:2], gs[C, 2:4], ALU.mult))
    link(eng.scalar_tensor_tensor(gl[C, :], gl[C, :], gs[C, 4:5], buf["bal"][C, :], ALU.mult, ALU.add))
    link(eng.tensor_tensor(gr[C, 0:1], gl[C, 0:1], gl[C, 1:2], ALU.max))
    eng.tensor_scalar(gl[C, :], gl[C, :], gr[C, 0:1], None, ALU.subtract).then_inc(sem["gate_shift"], 1)
    eng.wait_ge(sem["gate_exp"], 1)
    link(eng.tensor_tensor(gr[C, 0:1], ge[C, 0:1], ge[C, 1:2], ALU.add))
    link(eng.reciprocal(gr[C, 0:1], gr[C, 0:1]))
    link(eng.tensor_scalar(ge[C, :], ge[C, :], gr[C, 0:1], None, ALU.mult))
    link(eng.tensor_tensor(gr[C, 1:2], ge[C, 0:1], ge[C, 1:2], ALU.is_ge))
    link(eng.tensor_tensor(gr[C, 2:3], ge[C, 0:1], ge[C, 1:2], ALU.max))
    link(eng.tensor_tensor(gr[C, 0:1], gr[C, 1:2], gr[C, 2:3], ALU.mult))
    link(eng.tensor_tensor(gr[C, 1:2], gr[C, 2:3], gr[C, 0:1], ALU.subtract))

    def adds(g):
        for t in range(GT):
            n = GT * g + t
            eng.wait_ge(sem["f0_out"], n + 1)
            eng.wait_ge(sem["b2_added"], n // 2 + 1)
            eng.tensor_tensor(buf["H"][:, n, :], ps[:, 6 + n % 2, 0:D], buf["H"][:, n, :], ALU.add).then_inc(sem["f0_add"], 1)
            if n % TPB:
                eng.wait_ge(sem["f0_add"], n + 1)
                moments(eng, link, buf, [n])

    adds(0)
    adds(1)
    eng.wait_ge(sem["cand_full"], 1)
    eng.wait_ge(sem["aob_in"], 16)
    eng.wait_ge(sem["hc_in"], 16 * B)
    cand = buf["cand"]
    link(eng.tensor_tensor(cand[C, :, :], ps[C, 3, 0:2 * D].rearrange("p (r d) -> p r d", r=2), buf["aob"][C, :, :], ALU.add))
    link(eng.scalar_tensor_tensor(buf["hc"][C, :], cand[C, 0, :], gr[C, 0:1], buf["hc"][C, :], ALU.mult, ALU.add))
    eng.scalar_tensor_tensor(buf["hc"][C, :], cand[C, 1, :], gr[C, 1:2], buf["hc"][C, :], ALU.mult, ALU.add).then_inc(sem["cls_done"], 1)
    adds(2)
    adds(3)


SCW = 3 * P


def attn1_on_tensor(eng, sem, buf, ps):
    A, Bm, xn, ident = buf["xtA"], buf["xtB"], buf["xn1"], buf["ident"]
    transposed_on_tensor(eng, sem, buf, ps, 1)

    def scores(b):
        x_ready(eng, sem, 1, b // 2)
        if b >= 2:
            eng.wait_ge(sem["a1_masked"], b - 1)
        for t, (at, w) in enumerate(((0, P), (P, 2 * P))):
            rows, cols = slice(SEQ * b + P * t, SEQ * b + P * t + P), slice(SEQ * b, SEQ * b + w)
            out = ps[:, 4 + b % 2, at:at + w]
            eng.matmul(out, A[:, rows], A[:, cols], start=True, stop=False)
            ins = eng.matmul(out, Bm[:, rows], Bm[:, cols], start=False, stop=True)
        ins.then_inc(sem["a1_scores"], 1)

    scores(0)
    for b in range(B):
        if b + 1 < B:
            scores(b + 1)
        eng.wait_ge(sem["a1_exp"], 2 * (b + 1))
        if b:
            eng.wait_ge(sem["a1_pt"], b)
        for k in range(3):
            ins = eng.transpose(ps[:, 6, P * k:P * k + P], buf["p1"][:, b % 2, P * k:P * k + P], ident[:, :])
        ins.then_inc(sem["a1_pt_psum"], 1)
        eng.wait_ge(sem["a1_pt"], b + 1)
        if b:
            eng.wait_ge(sem["a1_add"], 2 * b)
        pt = buf["pt1"][:, b % 2, :]
        eng.matmul(ps[:, 7, 0:D], pt[:, 0:P], xn[:, TPB * b, :], start=True, stop=True)
        eng.matmul(ps[:, 7, D:2 * D], pt[:, P:2 * P], xn[:, TPB * b, :], start=True, stop=False)
        eng.matmul(ps[:, 7, D:2 * D], pt[:, 2 * P:3 * P], xn[:, TPB * b + 1, :], start=False, stop=True).then_inc(sem["a1_av"], 1)


def attn1_on_scalar(eng, sem, buf, ps):
    transposed_on_scalar(eng, sem, buf, ps, 1)
    for b in range(B):
        eng.wait_ge(sem["a1_shift"], b + 1)
        if b >= 2:
            eng.wait_ge(sem["a1_pt_psum"], b - 1)
        for t, (at, w) in enumerate(((0, P), (P, 2 * P))):
            eng.activation(buf["p1"][:, b % 2, at:at + w], buf["sc1"][:, b % 2, at:at + w], ACT.Exp,
                           bias=buf["m1"][:, b % 2, t:t + 1], accum_out=buf["sum1"][:, b % 2, t:t + 1]).then_inc(sem["a1_exp"], 1)
        eng.wait_ge(sem["a1_pt_psum"], b + 1)
        if b >= 2:
            eng.wait_ge(sem["a1_av"], b - 1)
        eng.activation(buf["pt1"][:, b % 2, :], ps[:, 6, 0:SCW], ACT.Copy).then_inc(sem["a1_pt"], 1)


def attn1_on_vector(eng, link, sem, buf, ps):
    eng.wait_ge(sem["h2_in"], 16 * B)
    moments(eng, link, buf, range(0, NT, TPB))
    statistics_on_vector(eng, link, sem, buf, 2)
    transposed_on_vector(eng, link, sem, buf, ps, 1)
    eng.wait_ge(sem["mask_ready"], 2)

    def mask(b):
        eng.wait_ge(sem["a1_scores"], b + 1)
        if b >= 2:
            eng.wait_ge(sem["a1_exp"], 2 * (b - 1))
        eng.scalar_tensor_tensor(buf["sc1"][:, b % 2, :], ps[:, 4 + b % 2, 0:SCW], float(D) ** -0.5, buf["mask"][:, :],
                                 ALU.mult, ALU.add).then_inc(sem["a1_masked"], 1)
        eng.wait_ge(sem["a1_masked"], b + 1)
        link(eng.reduce_max(buf["m1"][:, b % 2, 0:1], buf["sc1"][:, b % 2, 0:P], AX.X))
        link(eng.reduce_max(buf["m1"][:, b % 2, 1:2], buf["sc1"][:, b % 2, P:SCW], AX.X))
        eng.tensor_scalar(buf["m1"][:, b % 2, :], buf["m1"][:, b % 2, :], -1.0, None, ALU.mult).then_inc(sem["a1_shift"], 1)

    mask(0)
    for b in range(B):
        if b + 1 < B:
            mask(b + 1)
        eng.wait_ge(sem["a1_exp"], 2 * (b + 1))
        if b:
            eng.wait_ge(sem["a1_add"], TPB * b)
        link(eng.reciprocal(buf["rec1"][:, :], buf["sum1"][:, b % 2, :]))
        eng.wait_ge(sem["a1_av"], b + 1)
        for t in range(TPB):
            h = buf["H"][:, TPB * b + t, :]
            eng.scalar_tensor_tensor(h, ps[:, 7, D * t:D * t + D], buf["rec1"][:, t:t + 1], h, ALU.mult, ALU.add).then_inc(sem["a1_add"], 1)
        eng.wait_ge(sem["a1_add"], TPB * (b + 1))
        moments(eng, link, buf, range(TPB * b, TPB * b + TPB))


NE, TOPK = 8, 2
HE, HS = D, HF
HALL = NE * HE + HS
MR, MA = NE * HE // P, HALL // P
RW = NE + 2
LOROW = 32
NGATE = NE + 1
WC = HF // 2
NWC = 2 * HALL // WC


def ffn1_on_sync(eng, sem, buf, io):
    eng.wait_ge(sem["f0_add"], NT)
    eng.wait_ge(sem["h2_in"], 16 * B)
    eng.dma_start(buf["wd"][:, :, :], io["w_down"].rearrange("(m p) d -> p m d", p=P)).then_inc(sem["wd_in"], 16)
    eng.dma_start(buf["sgb"][:, :], io["sg_b"].partition_broadcast(P)).then_inc(sem["sgb_in"], 16)
    load_runs(eng, buf["wrf"], io["router"], sem["wr_in"])
    for n in range(NWC):
        if n >= 2:
            eng.wait_ge(sem["wgu_ready"], n - 1)
        load_runs(eng, buf["wgf"][:, n % 2, :, :], io["w_gate_up"][:, WC * n:WC * n + WC], sem[f"wgu_in{n % 2}"])


def ffn1_on_gpsimd(eng, link, sem, buf, io):
    eng.wait_ge(sem["f0_add"], NT)
    eng.wait_ge(sem["h2_in"], 16 * B)
    eng.dma_start(buf["sel"][0:2 * LOROW, :, :], io["select"]).then_inc(sem["sel_in"], 16)
    eng.memset(buf["mask"][:, :], 0.0).then_inc(sem["mask_zero"], 1)
    eng.wait_ge(sem["mask_zero"], 1)
    for k in (0, 2):
        tile = buf["mask"][:, P * k:P * k + P]
        eng.affine_select(out=tile, in_=tile, compare_op=ALU.is_ge, fill=-1e9, base=0, pattern=[[-1, P]],
                          channel_multiplier=1).then_inc(sem["mask_ready"], 1)
    eng.memset(buf["gt"][:, :].bitcast(F32), 0.0).then_inc(sem["gt_zero"], 1)
    eng.wait_ge(sem["wr_in"], 48)
    link(eng.tensor_copy(buf["wr"][:, 0:4:2, :], buf["wrf"][:, :, :]))
    eng.tensor_tensor(buf["wr"][:, 1:4:2, :], buf["wrf"][:, :, :], buf["wr"][:, 0:4:2, :].bitcast(F32), ALU.subtract).then_inc(sem["wr_ready"], 1)
    for n in range(NWC):
        eng.wait_ge(sem[f"wgu_in{n % 2}"], 48 * (n // 2 + 1))
        cols, wf, W = slice(WC * n, WC * n + WC), buf["wgf"][:, n % 2, :, :], buf["wgu"]
        link(eng.tensor_copy(W[:, 0:4:2, cols], wf))
        eng.tensor_tensor(W[:, 1:4:2, cols], wf, W[:, 0:4:2, cols].bitcast(F32), ALU.subtract).then_inc(sem["wgu_ready"], 1)
    for n in range(NG * MA):
        g, m = n // MA, n % MA
        eng.wait_ge(sem["f1_prod"], n + 1)
        eng.wait_ge(sem["f1_gb"], gb_count(g, m))
        if n >= NHID:
            eng.wait_ge(sem["f1_used"], n - NHID + 1)
        gb = buf["gb"][:, m % 2, :] if m < MR else buf["gbs"][:, :]
        eng.tensor_tensor(buf["hid1"][:, n % NHID, :], buf["prod"][:, n % 2, :], gb, ALU.mult).then_inc(sem["f1_hid"], 1)


def gb_count(g, m):
    return (MR + 1) * g + min(m, MR) + 1


NHID = 4
DOWN_LAG = 3


def ffn1_on_tensor(eng, sem, buf, ps):
    W, wd, hid, ident = buf["wgu"], buf["wd"], buf["hid1"], buf["ident"]
    transposed_on_tensor(eng, sem, buf, ps, 2)
    eng.wait_ge(sem["wr_ready"], 1)
    for g in range(NG):
        x_ready(eng, sem, 2, g)
        five(eng, ps[0:RW, 4 + g, :], [buf["wr"][:, s, :] for s in range(4)], buf["xa2"], buf["xb2"],
             slice(GW * g, GW * g + GW), True).then_inc(sem["router_t"], 1)

    def gate_up(g, m):
        n = MA * g + m
        cols = slice(GW * g, GW * g + GW)
        if n >= 2:
            eng.wait_ge(sem["f1_silu"], n - 1)
        five(eng, ps[:, n % 2, :], [W[:, s, P * m:P * m + P] for s in range(4)], buf["xa2"], buf["xb2"], cols, True)\
            .then_inc(sem["f1_gate"], 1)
        if n >= 2:
            eng.wait_ge(sem["f1_prod"], n - 1)
        five(eng, ps[:, 2 + n % 2, :], [W[:, s, HALL + P * m:HALL + P * m + P] for s in range(4)], buf["xa2"], buf["xb2"], cols, True)\
            .then_inc(sem["f1_up"], 1)

    def router_logits():
        eng.wait_ge(sem["router_lt"], NG)
        for t in range(NT):
            ins = eng.transpose(ps[:, 4, RW * t:RW * t + RW], buf["lt"][0:RW, P * t:P * t + P], ident[0:RW, 0:RW])
        ins.then_inc(sem["router_psum"], 1)

    def gates():
        eng.wait_ge(sem["gates_ready"], 1)
        for t in range(NT):
            if t % GT == 0 and t >= 2 * GT:
                eng.wait_ge(sem["gt_done"], t // GT - 1)
            ins = eng.transpose(ps[0:NGATE, 6 + t // GT % 2, P * (t % GT):P * (t % GT) + P], buf["ga"][:, t, :], ident[:, :])
            if t % GT == GT - 1:
                ins.then_inc(sem["gt_psum"], 1)
        eng.wait_ge(sem["gt_done"], NG)
        eng.wait_ge(sem["sel_in"], 16)

    def spread(g, m):
        k = (MR + 1) * g + m
        if k >= 2:
            eng.wait_ge(sem["f1_gb"], k - 1)
        eng.matmul(ps[:, 4 + k % 2, :], buf["sel"][0:2 * LOROW, m, :], buf["gt"][0:2 * LOROW, GW * g:GW * g + GW],
                   start=True, stop=True).then_inc(sem["f1_spread"], 1)

    def down(n):
        g, m = n // MA, n % MA
        eng.wait_ge(sem["f1_hid"], n + 1)
        if m == 0 and g:
            eng.wait_ge(sem["f1_add"], GT * g)
        if m == 0:
            for k in range(2):
                eng.matmul(ps[:, 6 + k, 0:2 * D], buf["gt"][2 * LOROW:3 * LOROW, 0:P], buf["gt"][2 * LOROW:3 * LOROW, 0:2 * D],
                           start=True, stop=False)
        for t in range(GT):
            out, cols = ps[:, 6 + t // 2, D * (t % 2):D * (t % 2) + D], slice(P * t, P * t + P)
            ins = eng.matmul(out, hid[:, n % NHID, cols], wd[:, m, :], start=False, stop=m == MA - 1 and t % 2 == 1)
        ins.then_inc(sem["f1_used"], 1)

    for n in range(NG * MA + DOWN_LAG):
        g, m = n // MA, n % MA
        if g < NG:
            if g == 0:
                eng.wait_ge(sem["wgu_ready"], (HALL + P * m + P - 1) // WC + 1)
            gate_up(g, m)
            if n == 0:
                router_logits()
            elif n == 1:
                gates()
                spread(0, 0)
                spread(0, 1)
            elif m <= MR:
                spread(g, m)
        if n == DOWN_LAG:
            eng.wait_ge(sem["wd_in"], 16)
        if n >= DOWN_LAG:
            down(n - DOWN_LAG)


def ffn1_on_scalar(eng, sem, buf, ps):
    transposed_on_scalar(eng, sem, buf, ps, 2)
    for g in range(NG):
        eng.wait_ge(sem["router_t"], g + 1)
        eng.activation(buf["lt"][0:RW, GW * g:GW * g + GW], ps[0:RW, 4 + g, :], ACT.Copy).then_inc(sem["router_lt"], 1)
    eng.wait_ge(sem["router_shift"], 1)
    eng.activation(buf["rl"][:, :, :], buf["rl"][:, :, :], ACT.Exp).then_inc(sem["router_exp"], 1)
    for k in range(NG):
        rows = slice(0, NGATE)
        cols = slice(GW * k, GW * k + GW)
        eng.wait_ge(sem["gt_zero"], 1)
        eng.wait_ge(sem["gt_psum"], k + 1)
        eng.activation(buf["gt"][rows, cols], ps[rows, 6 + k % 2, :], ACT.Copy).then_inc(sem["gt_hi"], 1)
    for n in range(NG * MA):
        g, m = n // MA, n % MA
        eng.wait_ge(sem["f1_gate"], n + 1)
        if n >= 2:
            eng.wait_ge(sem["f1_prod"], n - 1)
        eng.activation(buf["sg"][:, n % 2, :], ps[:, n % 2, :], ACT.Silu).then_inc(sem["f1_silu"], 1)
        if m <= MR:
            k = (MR + 1) * g + m
            eng.wait_ge(sem["f1_spread"], k + 1)
            last = n - 2 if m < MR else MA * g - 1
            if last >= 0:
                eng.wait_ge(sem["f1_hid"], last + 1)
            dst = buf["gb"][:, m % 2, :] if m < MR else buf["gbs"][:, :]
            eng.activation(dst, ps[:, 4 + k % 2, :], ACT.Copy).then_inc(sem["f1_gb"], 1)


def ffn1_on_vector(eng, link, sem, buf, ps):
    statistics_on_vector(eng, link, sem, buf, 3)
    transposed_on_vector(eng, link, sem, buf, ps, 2)
    rl, mx, ga, cmp, rk = (buf[n] for n in ("rl", "rmx", "ga", "cmp", "rk"))
    eng.wait_ge(sem["router_psum"], 1)
    eng.wait_ge(sem["sgb_in"], 16)
    R = ps[:, 4, 0:NT * RW].rearrange("p (t r) -> p t r", r=RW)
    link(eng.reduce_max(mx[:, :], R[:, :, 0:NE], AX.X))
    link(eng.tensor_tensor(rl[:, :, 0:NE], R[:, :, 0:NE], mx[:, :].unsqueeze(2).broadcast_to([P, NT, NE]), ALU.subtract))
    eng.tensor_scalar(rl[:, :, NE], R[:, :, NE], buf["sgb"][:, 0:1], -1.0, ALU.add, ALU.mult).then_inc(sem["router_shift"], 1)
    eng.wait_ge(sem["router_exp"], 1)
    link(eng.tensor_scalar(mx[:, :], rl[:, :, NE], 1.0, None, ALU.add))
    link(eng.reciprocal(ga[:, :, NE], mx[:, :]))
    for e in range(NE):
        q = rl[:, :, e:e + 1].broadcast_to([P, NT, NE])
        link(eng.tensor_tensor(cmp[:, :, e, :], rl[:, :, 0:NE], q, ALU.is_gt))
    for e in range(1, NE):
        q = rl[:, :, e:e + 1].broadcast_to([P, NT, e])
        link(eng.tensor_tensor(cmp[:, :, e, 0:e], rl[:, :, 0:e], q, ALU.is_ge))
    link(eng.reduce_sum(rk[:, :, :], cmp[:, :, :, :], AX.X))
    link(eng.tensor_scalar(rk[:, :, :], rk[:, :, :], float(TOPK), None, ALU.is_lt))
    link(eng.tensor_tensor(rk[:, :, :], rk[:, :, :], rl[:, :, 0:NE], ALU.mult))
    link(eng.reduce_sum(mx[:, :], rk[:, :, :], AX.X))
    link(eng.reciprocal(mx[:, :], mx[:, :]))
    link(eng.tensor_scalar(buf["oma"][:, :], ga[:, :, NE], -1.0, 1.0, ALU.mult, ALU.add))
    link(eng.tensor_tensor(mx[:, :], mx[:, :], buf["oma"][:, :], ALU.mult))
    eng.tensor_tensor(ga[:, :, 0:NE], rk[:, :, :], mx[:, :].unsqueeze(2).broadcast_to([P, NT, NE]), ALU.mult).then_inc(sem["gates_ready"], 1)

    def product(n):
        eng.wait_ge(sem["f1_up"], n + 1)
        eng.wait_ge(sem["f1_silu"], n + 1)
        if n >= 2:
            eng.wait_ge(sem["f1_hid"], n - 1)
        eng.tensor_tensor(buf["prod"][:, n % 2, :], ps[:, 2 + n % 2, :], buf["sg"][:, n % 2, :], ALU.mult).then_inc(sem["f1_prod"], 1)

    for k in range(NG):
        eng.wait_ge(sem["gt_hi"], k + 1)
        rows, cols = slice(0, NGATE), slice(GW * k, GW * k + GW)
        eng.tensor_tensor(buf["gt"][LOROW:LOROW + NGATE, cols], ps[rows, 6 + k % 2, :], buf["gt"][rows, cols].bitcast(F32),
                          ALU.subtract).then_inc(sem["gt_done"], 1)
    for n in range(NG * MA + DOWN_LAG):
        if n < NG * MA:
            product(n)
        if (n + 1 - DOWN_LAG) % MA == 0 and n >= MA:
            g = (n + 1 - DOWN_LAG) // MA - 1
            eng.wait_ge(sem["f1_used"], MA * (g + 1))
            for t in range(0, GT, 2):
                h = buf["H"][:, GT * g + t:GT * g + t + 2, :]
                eng.tensor_tensor(h, ps[:, 6 + t // 2, 0:2 * D].rearrange("p (t d) -> p t d", t=2), h, ALU.add).then_inc(sem["f1_add"], 2)
SEMS = ["ids_in", "theta_in", "angles_ready", "trig_ready", "ev_ready", "ident_zero", "ident_ready", "pw_zero", "pw_in",
        "evt_psum", "evt_ready", "emb_psum", "h_ready", "dve_step", "pool_step", "out_sent",
        "var_ready", "std_ready", "wqkv_in", "wqkv_ready", "wp_in", "wp_ready", "bp_in", "bp_added", "vsign_in",
        "vs_clear", "qk_clear", "xn_ready", "misc_full", "misc_free0", "misc_free1", "qk_in00", "qk_in01", "qk_in02", "qk_in03", "qk_in10", "qk_in11", "qk_in12", "qk_in13", "hi_ready", "xs_half", "vs_half", "ot_half",
        "p1_full", "mx_done", "nm_ready", "nm_in", "p2_full", "exp_done", "av_full", "av_out", "o_ready",
        "xt_xn", "xt_full", "xt_hi", "xt_lo", "xt_free",
        "w1_in", "w1_ready", "b1_in", "w2_in", "b2_in", "b2_added", "gate_in", "aob_in", "ain_in", "aout_in", "hc_in", "xc_in",
        "mh_zero", "xct_ones", "xct_psum", "xct_ready", "atom_full", "atom_act", "cand_full", "cls_done", "h2_in",
        "gate_sq", "gate_root", "gate_shift", "gate_exp", "f0_full", "f0_act", "f0_out", "f0_add",
        "mask_zero", "mask_ready", "a1_scores", "a1_masked", "a1_shift", "a1_exp", "a1_pt_psum", "a1_pt", "a1_av", "a1_add",
        "wd_in", "sel_in", "sgb_in", "wr_in", "wr_ready", "wgu_in0", "wgu_in1", "wgu_ready", "gt_zero", "router_psum",
        "router_shift", "router_exp", "gates_ready", "gt_psum", "gt_hi", "gt_done", "f1_gate", "f1_up", "f1_silu",
        "f1_spread", "f1_gb", "f1_prod", "f1_hid", "f1_used", "router_t", "router_lt",  "f1_add"]


def embedding_on_tensor(eng, sem, buf, ps):
    evt, pw, ident = buf["evt"], buf["pw"], buf["ident"]
    eng.wait_ge(sem["ident_ready"], 1)
    eng.wait_ge(sem["ev_ready"], 1)
    for c in range(4):
        eng.transpose(ps[:, 0, P * c:P * c + P], buf["evp"][:, 4 * c:4 * c + 4, :].rearrange("p t e -> p (t e)"),
                      ident[:, :]).then_inc(sem["evt_psum"], 1)
    eng.wait_ge(sem["pw_in"], 64)
    for c in range(4):
        eng.wait_ge(sem["evt_ready"], c + 1)
        for k in range(2):
            if c >= 2:
                eng.wait_ge(sem["h_ready"], 2 * c + k - 3)
            eng.matmul(ps[:, 1 + (2 * c + k) % 4, 0:2 * D], evt[:, c, :],
                       pw[:, 2 * k:2 * k + 2, :].rearrange("p t d -> p (t d)"), start=True, stop=True).then_inc(sem["emb_psum"], 1)


def embedding_on_scalar(eng, sem, buf, ps):
    eng.wait_ge(sem["angles_ready"], 1)
    eng.activation(buf["sn"][:, :, :], buf["red"][:, 0, :, :], ACT.Sin).then_inc(sem["trig_ready"], 1)
    eng.activation(buf["cs"][:, :, :], buf["red"][:, 1, :, :], ACT.Sin).then_inc(sem["trig_ready"], 1)
    for c in range(4):
        eng.wait_ge(sem["evt_psum"], 4)
        eng.activation(buf["evt"][:, c, :], ps[:, 0, P * c:P * c + P], ACT.Copy).then_inc(sem["evt_ready"], 1)
    for i in range(8):
        eng.wait_ge(sem["emb_psum"], i + 1)
        eng.activation(buf["H"][:, 2 * i:2 * i + 2, :].rearrange("p t d -> p (t d)"), ps[:, 1 + i % 4, 0:2 * D],
                       ACT.Copy).then_inc(sem["h_ready"], 1)


def program(nc, io, out):
    ctx = ExitStack()
    with ctx:
        def alloc(scope, buf, name, shape, dt=F32):
            buf[name] = scope.enter_context(nc.sbuf_tensor(name, shape, dt))

        sem = {n: ctx.enter_context(nc.semaphore(n)) for n in SEMS}
        buf = {}
        for name, shape, dt in (("H", [P, NT, D], F32), ("ident", [P, P], F32), ("st", [P, NT, 6], F32),
                                ("mv", [P, NT, 2], F32), ("rstd", [P, NT], F32), ("nmr", [P, NT], F32),
                                ):
            alloc(ctx, buf, name, shape, dt)
        first = ctx.enter_context(ExitStack())
        for name, shape, dt in (("QK", [P, 2, NU, NH, SEQ], F32R), ("VS", [P, VSLOT, TPB, NH, NC, VBLK // NC], F32),
                                ("wqkv", [P, 4, NQKV], F32R), ("wp", [P, 2, D], F32), ("wps", [P, 2, D], F32),
                                ("bp", [P, D], F32), ("vsign", [P, NC, NC], F32)):
            alloc(first, buf, name, shape, dt)
        with ExitStack() as scope:
            for name, shape in (("theta", [P, NT, NANG]), ("red", [P, 2, NANG, NT]), ("sn", [P, NANG, NT]),
                                ("cs", [P, NANG, NT]), ("R", [P, 5, NQ, NT]), ("ZM", [P, 4, NQ, NT]),
                                ("XP", [P, 4, NQ, NT]), ("W", [P, 4, 12, NT]), ("U", [P, 4, 12, NT]),
                                ("M", [P, 4, 12, NT]), ("E", [P, 4, 12, NT]), ("PP", [P, 3, 4, NT]),
                                ("TZ", [P, 4, NT]), ("G", [P, 48, NT]), ("OZ", [P, NQ, NT]), ("OX", [P, NQ, NT]),
                                ("evp", [P, NT, EVW]), ("evt", [P, 4, P]), ("pw", [P, 4, D]),
                                ("wf", [P, 2, NQKV]), ("wsg", [P, 2, NQKV])):
                alloc(scope, buf, name, shape)
            alloc(scope, buf, "ids", [P, NT], I32)
        with ExitStack() as scope:
            for name, shape, dt in (("HL", [P, 2, 2, NU, 2, SEQ], F32R), ("PT", [P, 2, TPB, NC, SEQ], F32),
                                    ("OTs", [P, 4, SEQ], F32), ("o", [P, TPB, D], F32), ("ot", [P, 2 * SEQ], F32),
                                    ("TM", [P, NC, 4, NC, QD], F32), ("rec", [P, 16], F32), ("rs", [P, 4, NC, NC], F32),
                                    ("nm", [P, 2, SEQ], F32R), ("mx", [P, 2, TPB, NC * NH], F32),
                                    ("xn", [P, 2, TPB, D], F32), ("xa", [P, 2, SEQ], F32R), ("xb", [P, SEQ], F32R)):
                alloc(scope, buf, name, shape, dt)
        first.close()
        with ExitStack() as scope:
            for place, size, group in (
                    ("first operand stack", NU * NH * SEQ,
                     (("ain", [P, NA, 2, HF], F32), ("b1", [P, MF], F32), ("b2", [P, D], F32), ("bal", [P, 2], F32),
                      ("gp", [P, 2, D], F32), ("aob", [P, 2, D], F32))),
                    ("second operand stack and values", NU * NH * SEQ + VSLOT * TPB * NH * VBLK,
                     (("aout", [P, NA, MF, D], F32), ("hid0", [P, 2, MF, GW], F32))),
                    ("weights", 4 * NQKV, (("w1f", [P, 2, HF], F32), ("w1", [P, 4, HF], F32R), ("w2", [P, MF, D], F32))),
                    ("the others", None,
                     (("xn0", [P, NT, D], F32), ("xa0", [P, 2, NT * P], F32R), ("xb0", [P, NT * P], F32R), ("hc", [P, D], F32),
                      ("xc", [P, D], F32), ("xct", [P, 2, NCT], F32), ("mh", [P, NA, MF, NCT], F32), ("gq", [P, 5, D], F32),
                      ("gs", [P, 5], F32), ("gl", [P, 2], F32), ("ge", [P, 2], F32), ("gr", [P, 3], F32), ("cand", [P, 2, D], F32)))):
                for name, shape, dt in group:
                    alloc(scope, buf, name, shape, dt)
                if size:
                    rest = size - sum(math.prod(shape[1:]) for _, shape, _ in group)
                    alloc(scope, buf, "behind " + place, [P, rest])
        for name, shape, dt in (("wgu", [P, 4, 2 * HALL], F32R), ("wd", [P, MA, D], F32), ("sel", [P, MR + 1, P], F32R),
                                ("wgf", [P, 2, 2, WC], F32), ("wrf", [P, 2, RW], F32), ("wr", [P, 4, RW], F32R),
                                ("sgb", [P, 1], F32), ("mask", [P, SCW], F32), ("gt", [P, NT * P], F32R)):
            alloc(ctx, buf, name, shape, dt)
        with ExitStack() as scope:
            for name, shape, dt in (("xn1", [P, NT, D], F32), ("xtA", [P, NT * P], F32), ("xtB", [DB, NT * P], F32),
                                    ("sc1", [P, 2, SCW], F32), ("p1", [P, 2, SCW], F32), ("pt1", [P, 2, SCW], F32),
                                    ("m1", [P, 2, TPB], F32), ("sum1", [P, 2, TPB], F32), ("rec1", [P, TPB], F32)):
                alloc(scope, buf, name, shape, dt)
        with ExitStack() as scope:
            for name, shape, dt in (("xn2", [P, NT, D], F32), ("hid1", [P, NHID, GW], F32), ("xa2", [P, 2, NT * P], F32R),
                                    ("xb2", [P, NT * P], F32R), ("sgp", [P, 2, 2, GW], F32), ("gb", [P, 2, GW], F32),
                                    ("gbs", [P, GW], F32), ("rl", [P, NT, NGATE], F32), ("ga", [P, NT, NGATE], F32),
                                    ("rmx", [P, NT], F32), ("oma", [P, NT], F32), ("rk", [P, NT, NE], F32),
                                    ("cmp", [P, NT, NE, NE], F32)):
                alloc(scope, buf, name, shape, dt)
        buf["sg"], buf["prod"] = buf["sgp"][:, 0, :, :], buf["sgp"][:, 1, :, :]
        buf["lt"] = buf["sgp"][:, :, :, :].rearrange("p a s n -> p (a s n)")
        ps = ctx.enter_context(nc.psum_tensor("ps", [P, 8, NBANK], F32))
        block = ctx.enter_context(nc.Block())

        @block.sync
        def _(eng):
            eng.dma_start(buf["ids"][:, :], io["ids"]).then_inc(sem["ids_in"], 16)
            for dst, name in ((buf["wf"], "wqkv"), (buf["wsg"], "wqkv_sign")):
                eng.dma_start(dst[:, 0, :], io[name][0:DA, :]).then_inc(sem["wqkv_in"], 16)
                for half in range(2):
                    eng.dma_start(dst[DB * half:DB * half + DB, 1, :], io[name][DA:D, :]).then_inc(sem["wqkv_in"], 16)
            for dst, name in ((buf["wp"], "wp"), (buf["wps"], "wp_sign")):
                eng.dma_start(dst[:, 0, :], io[name][0:DA, :]).then_inc(sem["wp_in"], 16)
                eng.dma_start(dst[0:DB, 1, :], io[name][DA:D, :]).then_inc(sem["wp_in"], 16)
            eng.dma_start(buf["bp"][:, :], io["bp"].partition_broadcast(P)).then_inc(sem["bp_in"], 16)
            eng.dma_start(buf["vsign"][:, :, :], io["vsign"].partition_broadcast(P)).then_inc(sem["vsign_in"], 16)
            eng.wait_ge(sem["pw_zero"], 1)
            for j in range(4):
                eng.dma_start(buf["pw"][EVW * j:EVW * j + NQ + 1, j, :], io["post"]).then_inc(sem["pw_in"], 16)
            attention_on_sync(nc, eng, sem, buf)
            ffn0_on_sync(eng, sem, buf, io)
            ffn1_on_sync(eng, sem, buf, io)
            eng.wait_ge(sem["f1_add"], NT)
            eng.dma_start(out.rearrange("a (h p) d -> p (a h) d", p=P), buf["H"][:, :, :]).then_inc(sem["out_sent"], 16)
            eng.wait_ge(sem["out_sent"], 16)

        @block.gpsimd
        def _(eng):
            link = Chain(eng, sem["pool_step"])
            eng.memset(buf["pw"][:, :, :], 0.0).then_inc(sem["pw_zero"], 1)
            eng.memset(buf["ident"][:, :], 0.0).then_inc(sem["ident_zero"], 1)
            eng.wait_ge(sem["ids_in"], 16)
            for t in range(NT):
                eng.indirect_dma_start(buf["theta"][:, t, :], None, io["qp"],
                                       bass.IndirectOffsetOnAxis(ap=buf["ids"][:, t:t + 1], axis=0)).then_inc(sem["theta_in"], 16)
            eng.wait_ge(sem["ident_zero"], 1)
            eng.affine_select(out=buf["ident"][:, :], in_=buf["ident"][:, :], compare_op=ALU.not_equal, fill=1.0, base=0,
                              pattern=[[-1, P]], channel_multiplier=1).then_inc(sem["ident_ready"], 1)
            W, wf = buf["wqkv"], buf["wf"]
            eng.wait_ge(sem["wqkv_in"], 96)
            link(eng.tensor_tensor(wf[:, :, :], wf[:, :, :], buf["wsg"][:, :, :], ALU.mult))
            link(eng.tensor_copy(W[:, 0:4:2, :], wf[:, :, :]))
            eng.tensor_tensor(W[:, 1:4:2, :], wf[:, :, :], W[:, 0:4:2, :].bitcast(F32), ALU.subtract).then_inc(sem["wqkv_ready"], 1)
            eng.wait_ge(sem["wp_in"], 64)
            link(eng.tensor_tensor(buf["wp"][:, 0, :], buf["wp"][:, 0, :], buf["wps"][:, 0, :], ALU.mult))
            eng.tensor_tensor(buf["wp"][0:DB, 1, :], buf["wp"][0:DB, 1, :], buf["wps"][0:DB, 1, :], ALU.mult).then_inc(sem["wp_ready"], 1)
            for s in range(2):
                link(eng.memset(buf["QK"][:, s, :, :, :].rearrange("p u h n -> p (u h n)").bitcast(F32), 0.0))
                eng.memset(buf["QK"][96:P, s, NC, :, :].rearrange("p h n -> p (h n)").bitcast(F32), 1.0).then_inc(sem["qk_clear"], 1)
                eng.wait_ge(sem["qk_clear"], s + 1)
            VS = buf["VS"][:, :, :, :, :, :].rearrange("p s t h a e -> p (s t h a) e")
            link(eng.memset(VS, 0.0))
            eng.memset(VS[:, ::NC, QD:QD + 1], 1.0)\
               .then_inc(sem["vs_clear"], 1)
            eng.wait_ge(sem["bp_in"], 16)
            for b in range(B):
                eng.wait_ge(sem["xn_ready"], b + 1)
                tiles = buf["H"][:, TPB * b:TPB * b + TPB, :]
                eng.tensor_tensor(tiles, tiles, buf["bp"][:, :].unsqueeze(1).broadcast_to([P, TPB, D]), ALU.add).then_inc(sem["bp_added"], 1)
            ffn0_on_gpsimd(eng, link, sem, buf)
            ffn1_on_gpsimd(eng, link, sem, buf, io)

        @block.scalar
        def _(eng):
            embedding_on_scalar(eng, sem, buf, ps)
            root_on_scalar(eng, sem, buf, 0)
            eng.wait_ge(sem["vs_clear"], 1)
            attention_on_scalar(nc, eng, sem, buf, ps)
            root_on_scalar(eng, sem, buf, 1)
            ffn0_on_scalar(eng, sem, buf, ps)
            root_on_scalar(eng, sem, buf, 2)
            attn1_on_scalar(eng, sem, buf, ps)
            root_on_scalar(eng, sem, buf, 3)
            ffn1_on_scalar(eng, sem, buf, ps)

        @block.vector
        def _(eng):
            link = Chain(eng, sem["dve_step"])
            circuit_on_vector(eng, link, sem, buf)
            eng.wait_ge(sem["h_ready"], 8)
            moments(eng, link, buf, range(NT))
            statistics_on_vector(eng, link, sem, buf, 0)
            eng.wait_ge(sem["vsign_in"], 16)
            attention_on_vector(nc, eng, link, sem, buf, ps)
            ffn0_on_vector(eng, link, sem, buf, ps)
            attn1_on_vector(eng, link, sem, buf, ps)
            eng.wait_ge(sem["a1_add"], NT)
            ffn1_on_vector(eng, link, sem, buf, ps)

        @block.tensor
        def _(eng):
            embedding_on_tensor(eng, sem, buf, ps)
            eng.wait_ge(sem["h_ready"], 8)
            attention_on_tensor(nc, eng, sem, buf, ps)
            ffn0_on_tensor(eng, sem, buf, ps)
            attn1_on_tensor(eng, sem, buf, ps)
            ffn1_on_tensor(eng, sem, buf, ps)


def quaternion_layout(parts):
    return np.concatenate([np.concatenate([parts[r ^ c] for c in range(NC)], 1) for r in range(NC)], 0)


def arrange(inputs):
    a = {}
    get = lambda n: np.asarray(inputs[n])
    a["ids"] = get("x").reshape(NT, P).T
    a["qp"] = get("L0_tok_quantum_params").transpose(0, 1, 3, 2).reshape(VOCAB, NANG)
    a["post"] = np.concatenate([get("L0_tok_post_w").T, get("L0_tok_post_b")[None]], 0)
    full = quaternion_layout([get(f"L0_attn_wqkv_{c}") for c in "rijk"])
    sign = np.repeat(np.repeat(np.array(LSIGN, np.float32), D // NC, 0), 3 * D // NC, 1)
    w = np.zeros((D, NQKV), np.float32)
    s = np.zeros((D, NQKV), np.float32)
    for u in range(NU):
        for h in range(NH):
            for comp in range(NC):
                src = (0 if u < NC else D) + h * HD + ((u ^ comp) if u < NC else comp) * QD
                dst = (2 * u + h % 2) * P + 32 * (h // 2) + comp * QD
                w[:, dst:dst + QD] = full[:, src:src + QD]
                s[:, dst:dst + QD] = sign[:, src:src + QD] * (QSIGN[u][comp] if u < NC else 1)
    w[:, 2 * NU * P:] = full[:, 2 * D:]
    s[:, 2 * NU * P:] = sign[:, 2 * D:]
    a["wqkv"], a["wqkv_sign"] = w, s
    a["wp"] = quaternion_layout([get(f"L0_attn_wp_{c}") for c in "rijk"])
    a["wp_sign"] = np.repeat(np.repeat(np.array(LSIGN, np.float32), D // NC, 0), D // NC, 1)
    a["bp"] = get("L0_attn_bp")
    a["vsign"] = np.array(VSIGN, np.float32)
    left, right = [n // 2 for n in range(NCLS)], [LEFT + n % 2 for n in range(NCLS)]
    a["fc1"], a["fc1_b"] = get("L0_ffn_fc1_w").T, get("L0_ffn_fc1_b").reshape(MF, P).T
    a["fc2"], a["fc2_b"] = get("L0_ffn_fc2_w").T, get("L0_ffn_fc2_b")
    a["gate_pair"] = np.concatenate([get("L0_ffn_gate_pair")] * B, 0)
    a["balance"] = np.concatenate([get("L0_ffn_balance_bias")] * B, 0)
    ob = get("L0_ffn_atom_out_b")
    a["atom_out_b"] = np.concatenate([np.stack([ob[right], ob[left]], 1)] * B, 0)
    a["atom_in"] = np.concatenate([get("L0_ffn_atom_in_w").transpose(0, 2, 1), get("L0_ffn_atom_in_b")[:, None]], 1)
    a["atom_out"] = get("L0_ffn_atom_out_w").transpose(0, 2, 1)
    flat = lambda n: get(n).transpose(1, 0, 2).reshape(D, NE * HE)
    a["w_gate_up"] = np.concatenate([flat("L1_ffn_w_gate"), get("L1_ffn_ws_gate"), flat("L1_ffn_w_up"), get("L1_ffn_ws_up")], 1)
    a["w_down"] = np.concatenate([get("L1_ffn_w_down").reshape(NE * HE, D), get("L1_ffn_ws_down")], 0)
    a["router"] = np.concatenate([get("L1_ffn_router_w"), get("L1_ffn_sg_w"), np.zeros((D, 1), np.float32)], 1)
    a["sg_b"] = get("L1_ffn_sg_b")
    select = np.zeros((2 * LOROW, MR + 1, P), np.float32)
    for m in range(MR + 1):
        for p in range(P):
            e = min((P * m + p) // HE, NE)
            select[e, m, p] = select[LOROW + e, m, p] = 1
    a["select"] = select
    return {n: np.ascontiguousarray(x) for n, x in a.items()}


def kernel(**inputs):
    import concourse.bacc as _bacc
    from concourse import mybir as _mybir
    from concourse.bass_utils import run_bass_kernel_spmd as _run
    arrays = arrange(inputs)
    nc = _bacc.Bacc("TRN2", target_bir_lowering=False, num_devices=1)
    io = {n: nc.dram_tensor("in_" + n, a.shape, _mybir.dt.from_np(a.dtype), kind="ExternalInput").ap() for n, a in arrays.items()}
    o = nc.dram_tensor("out0", (B, SEQ, D), _mybir.dt.float32, kind="ExternalOutput").ap()
    program(nc, io, o)
    r = _run(nc, [{"in_" + n: a for n, a in arrays.items()}], core_ids=[0])
    return r.results[0]["out0"]
```

```python
import math
from contextlib import ExitStack

import numpy as np
import concourse.bass as bass
from concourse import mybir
from concourse.alu_op_type import AluOpType as ALU

F32 = mybir.dt.float32
F32R = mybir.dt.float32r
I32 = mybir.dt.int32
ACT = mybir.ActivationFunctionType
AX = mybir.AxisListType

P = 128
B, SEQ, D = 8, 256, 192
TPB = SEQ // P
NT = B * TPB
DA, DB = P, D - P
NQ, NL = 6, 3
NANG = NL * 2 * NQ
VOCAB = 8000
EPS = 1e-5
TWO_PI = 2.0 * math.pi
PI_SAFE = 3.1415925
ROUND = 1.5 * 2.0 ** 23
TWO_PI_HI = 6.28125
TWO_PI_LO = TWO_PI - TWO_PI_HI
EVW = 32
NBANK = 512


def angle(layer, rz, q0=0, n=NQ):
    at = (2 * layer + rz) * NQ + q0
    return slice(at, at + n)


class Chain:

    def __init__(self, eng, sem):
        self.eng, self.sem, self.n = eng, sem, 0

    def __call__(self, ins):
        self.n += 1
        ins.then_inc(self.sem, 1)
        self.eng.wait_ge(self.sem, self.n)

    def go(self, ins):
        self.n += 1
        ins.then_inc(self.sem, 1)
        return self.n

    def after(self, n):
        self.eng.wait_ge(self.sem, n)


def moments(eng, link, buf, tiles):
    for t in tiles:
        n = link.go(eng.bn_stats(buf["st"][:, t, :], buf["H"][:, t, :]))
    for i, t in enumerate(tiles):
        link.after(n - len(tiles) + 1 + i)
        m = link.go(eng.bn_aggr(buf["mv"][:, t, :], buf["st"][:, t, :]))
    link.after(m)


def statistics_on_vector(eng, link, sem, buf, stage):
    mv, rstd, nmr = buf["mv"], buf["rstd"], buf["nmr"]
    eng.tensor_scalar(rstd[:, :], mv[:, :, 1], EPS, None, ALU.add).then_inc(sem["var_ready"], 1)
    eng.wait_ge(sem["std_ready"], stage + 1)
    link(eng.reciprocal(rstd[:, :], rstd[:, :]))
    link(eng.scalar_tensor_tensor(nmr[:, :], mv[:, :, 0], -1.0, rstd[:, :], ALU.mult, ALU.mult))


def root_on_scalar(eng, sem, buf, stage):
    eng.wait_ge(sem["var_ready"], stage + 1)
    eng.activation(buf["rstd"][:, :], buf["rstd"][:, :], ACT.Sqrt).then_inc(sem["std_ready"], 1)


def five(eng, out, w, xa, xb, cols, stationary_is_weight):
    pairs = [(w[0], xa[:, 0, cols]), (w[1], xa[:, 0, cols]), (w[0], xa[:, 1, cols]), (w[2], xb[:, cols]), (w[3], xb[:, cols])]
    for n, (ww, xx) in enumerate(pairs):
        a, b = (ww, xx) if stationary_is_weight else (xx, ww)
        ins = eng.matmul(out, a, b, start=n == 0, stop=n == 4)
    return ins


def circuit_on_vector(eng, link, sem, buf):
    v = eng
    T16 = NT
    theta, red, sn, cs = buf["theta"], buf["red"], buf["sn"], buf["cs"]
    R, ZM, XP, W, U, M = buf["R"], buf["ZM"], buf["XP"], buf["W"], buf["U"], buf["M"]
    E, PP, TZ, G, OZ, OX, evp = buf["E"], buf["PP"], buf["TZ"], buf["G"], buf["OZ"], buf["OX"], buf["evp"]

    def then(ins, wait):
        (link if wait else link.go)(ins)

    def mul(o, a, b, wait=True):
        then(v.tensor_tensor(o, a, b, ALU.mult), wait)

    def add(o, a, b, wait=True):
        then(v.tensor_tensor(o, a, b, ALU.add), wait)

    def sub(o, a, b, wait=True):
        then(v.tensor_tensor(o, a, b, ALU.subtract), wait)

    def copy(o, a, wait=True):
        then(v.tensor_copy(o, a), wait)

    def neg(o, a, wait=True):
        then(v.tensor_scalar(o, a, -1.0, None, ALU.mult), wait)

    def wide(a, shape):
        return a.broadcast_to(shape)

    link(v.memset(W[:, :, :, :], 0.0))
    link(v.memset(evp[:, :, :], 0.0))
    link(v.memset(evp[:, :, NQ:NQ + 1], 1.0))
    v_theta = theta[:, :, :]
    v.wait_ge(sem["theta_in"], 16 * NT)
    link(v.tensor_scalar(red[:, 1, :, :].rearrange("p c t -> p t c"), v_theta, 1.0 / TWO_PI, ROUND, ALU.mult, ALU.add))
    link(v.tensor_scalar(red[:, 1, :, :], red[:, 1, :, :], -ROUND, None, ALU.add))
    link(v.scalar_tensor_tensor(red[:, 0, :, :].rearrange("p c t -> p t c"), red[:, 1, :, :].rearrange("p c t -> p t c"),
                                -TWO_PI_HI, v_theta, ALU.mult, ALU.add))
    link(v.scalar_tensor_tensor(red[:, 0, :, :], red[:, 1, :, :], -TWO_PI_LO, red[:, 0, :, :], ALU.mult, ALU.add))
    link(v.tensor_scalar(red[:, 0, :, :], red[:, 0, :, :], PI_SAFE, -PI_SAFE, ALU.min, ALU.max))
    link(v.scalar_tensor_tensor(red[:, 1, :, :], red[:, 0, :, :], -1.0, red[:, 0, :, :], ALU.mult, ALU.min))
    v.tensor_scalar(red[:, 1, :, :], red[:, 1, :, :], math.pi / 2, None, ALU.add).then_inc(sem["angles_ready"], 1)

    v.wait_ge(sem["trig_ready"], 2)
    mul(R[:, 0, :, :], sn[:, angle(0, 0), :], cs[:, angle(0, 1), :], False)
    mul(R[:, 1, :, :], sn[:, angle(0, 0), :], sn[:, angle(0, 1), :], False)
    link(v.tensor_copy(R[:, 2, :, :], cs[:, angle(0, 0), :]))
    neg(R[:, 3, :, :], R[:, 1, :, :], False)
    neg(R[:, 4, :, :], R[:, 0, :, :], False)
    rX, rY, rZ, nrY, nrX = (R[:, i, :, :] for i in range(5))
    copy(ZM[:, 0, :, :], cs[:, angle(1, 0), :], False)
    neg(ZM[:, 1, :, :], sn[:, angle(1, 0), :], False)
    neg(ZM[:, 2, :, :], sn[:, angle(1, 0), :], False)
    copy(ZM[:, 3, :, :], cs[:, angle(1, 0), :], False)
    zZ, zX = ZM[:, 0, :, :], ZM[:, 1, :, :]
    mul(XP[:, 0, :, :], cs[:, angle(1, 1), :], cs[:, angle(1, 0), :], False)
    neg(XP[:, 1, :, :], sn[:, angle(1, 1), :], False)
    mul(XP[:, 2, :, :], cs[:, angle(1, 1), :], sn[:, angle(1, 0), :], False)
    xX, xY, xZ, nxY = (XP[:, i, :, :] for i in range(4))

    v.tensor_copy(XP[:, 3, :, :], sn[:, angle(1, 1), :]).then_inc(sem["planes_ready"], 1)
    v.wait_ge(sem["planes_ready"], 1)
    link(v.memset(TZ[:, 3, :], 1.0))
    link(v.tensor_copy(TZ[:, 2, :], rZ[:, 5, :]))
    mul(TZ[:, 1, :], TZ[:, 2, :], rZ[:, 4, :])
    mul(TZ[:, 0, :], TZ[:, 1, :], rZ[:, 3, :])

    mul(W[:, 1, 8:0:-2, :], zX[:, 1:5, :], rX[:, 2:6, :], False)
    copy(W[:, 3, 8:0:-2, :], zZ[:, 1:5, :], False)
    mul(G[:, 0:4, :], zZ[:, 1:5, :], rZ[:, 2:6, :])
    mul(W[:, 0, 9:1:-2, :], G[:, 0:4, :], TZ[:, :, :])
    mul(G[:, 0:4, :], zX[:, 1:5, :], nrY[:, 2:6, :])
    mul(W[:, 2, 9:1:-2, :], G[:, 0:4, :], TZ[:, :, :])
    copy(W[:, 1, 0, :], zX[:, 4, :], False)
    mul(W[:, 3, 0, :], zZ[:, 4, :], rX[:, 5, :], False)
    mul(W[:, 0, 1, :], zZ[:, 4, :], rY[:, 5, :], False)
    mul(W[:, 2, 1, :], zX[:, 4, :], rZ[:, 5, :], False)
    mul(W[:, 1:3, 10, :], XP[:, 0:2, 1, :], wide(rX[:, 2, :].unsqueeze(1), [P, 2, T16]), False)
    copy(W[:, 3, 10, :], xZ[:, 1, :], False)
    mul(W[:, 0, 11, :], xZ[:, 1, :], rZ[:, 2, :], False)
    mul(W[:, 1, 11, :], xY[:, 1, :], rY[:, 2, :], False)
    mul(W[:, 2, 11, :], xX[:, 1, :], nrY[:, 2, :])

    def contract(q, n):
        mul(M[:, 4:6, 0:n, :], W[:, 1::-1, 0:n, :], wide(rX[:, q, :].unsqueeze(1).unsqueeze(1), [P, 2, n, T16]), False)
        mul(M[:, 0:2, 0:n, :], W[:, 2:4, 0:n, :], wide(R[:, 1:3, q, :].unsqueeze(2), [P, 2, n, T16]), False)
        mul(M[:, 2:4, 0:n, :], W[:, 2:4, 0:n, :], wide(R[:, 2:4, q, :].unsqueeze(2), [P, 2, n, T16]))
        add(U[:, 3:0:-2, 0:n, :], W[:, 0:2, 0:n, :], M[:, 4:6, 0:n, :], False)
        add(U[:, 0:3:2, 0:n, :], M[:, 0:4:2, 0:n, :], M[:, 1:4:2, 0:n, :])

    for q in (3, 2, 1):
        n = 4 + 2 * (3 - q)
        contract(q + 1, n)
        mul(W[:, :, 0:n, :], U[:, :, 0:n, :], wide(ZM[:, :, q, :].unsqueeze(2), [P, 4, n, T16]))
    contract(1, 12)
    mul(M[:, 0:2, :, :], U[:, 0:4:3, :, :], wide(rZ[:, 0, :].unsqueeze(1).unsqueeze(1), [P, 2, 12, T16]), False)
    mul(M[:, 2:4, :, :], U[:, 1:3, :, :], wide(R[:, 0:2, 0, :].unsqueeze(2), [P, 2, 12, T16]), False)
    mul(M[:, 4:6, :, :], U[:, 1:3, :, :], wide(R[:, 1:5:3, 0, :].unsqueeze(2), [P, 2, 12, T16]))
    add(E[:, 0:2, :, :], U[:, 3::-3, :, :], M[:, 0:2, :, :], False)
    add(E[:, 2:4, :, :], M[:, 2:6:2, :, :], M[:, 3:6:2, :, :])
    E_I, E_Z, E_X, E_Y = (E[:, i, :, :] for i in range(4))
    X4, Y4, I4, Z4, P1, T1 = 0, 1, 2, 3, 10, 11

    def dot(o, a0, b0, a1, b1, g):
        mul(o, a0, b0, False)
        mul(G[:, g, :], a1, b1)
        add(o, o, G[:, g, :])

    mul(G[:, 0:4, :], E_X[:, 8:0:-2, :], wide(zX[:, 0, :].unsqueeze(1), [P, 4, T16]), False)
    mul(G[:, 4:8, :], E_Z[:, 9:1:-2, :], wide(zZ[:, 0, :].unsqueeze(1), [P, 4, T16]))
    add(OZ[:, 1:5, :], G[:, 0:4, :], G[:, 4:8, :])
    mul(OZ[:, 0, :], zZ[:, 5, :], E_I[:, Z4, :], False)
    mul(G[:, 0, :], zX[:, 5, :], E_X[:, X4, :], False)
    mul(G[:, 1, :], zX[:, 0, :], E_X[:, Z4, :], False)
    mul(G[:, 4, :], zZ[:, 0, :], E_Z[:, I4, :], False)
    mul(G[:, 2, :], zX[:, 0, :], E_I[:, X4, :], False)
    mul(G[:, 3, :], zZ[:, 0, :], E_Y[:, Y4, :])
    add(OZ[:, 0, :], OZ[:, 0, :], G[:, 0, :], False)
    add(G[:, 1, :], G[:, 1, :], G[:, 4, :], False)
    sub(G[:, 2, :], G[:, 2, :], G[:, 3, :])
    dot(OZ[:, 5, :], zZ[:, 5, :], G[:, 1, :], zX[:, 5, :], G[:, 2, :], 0)

    PT1 = slice(P1, T1 + 1)
    two = lambda a: wide(a.unsqueeze(1), [P, 2, T16])
    pairs = [G[:, 8 + 2 * i:10 + 2 * i, :] for i in range(4)]
    YY, ZZ, YZ, ZY = pairs
    zeta, zeta5, zetaY, first, x5, eP, eT, last = (G[:, 16 + i, :] for i in range(8))
    mul(YY, two(xY[:, 0, :]), E_Y[:, PT1, :], False)
    mul(ZZ, two(xZ[:, 0, :]), E_Z[:, PT1, :], False)
    mul(YZ, two(xY[:, 0, :]), E_Z[:, PT1, :], False)
    mul(ZY, two(xZ[:, 0, :]), E_Y[:, PT1, :], False)
    mul(OX[:, 0, :], xX[:, 0, :], E_X[:, P1, :], False)
    mul(x5, rX[:, 5, :], E_I[:, P1, :], False)
    mul(zeta, rZ[:, 4, :], rZ[:, 3, :])
    add(YY, YY, ZZ, False)
    sub(YZ, YZ, ZY, False)
    mul(zeta5, zeta, rZ[:, 5, :], False)
    mul(zetaY, zeta, rY[:, 5, :], False)
    mul(x5, x5, xX[:, 5, :])
    mul(first, zeta5, YY[:, 1, :], False)
    mul(last, xX[:, 0, :], zeta5, False)
    mul(zeta, zetaY, E_I[:, T1, :], False)
    mul(eP, YZ[:, 0, :], nxY[:, 5, :], False)
    mul(eT, YZ[:, 1, :], xX[:, 5, :])
    add(OX[:, 0, :], OX[:, 0, :], first, False)
    mul(last, last, E_X[:, T1, :], False)
    mul(zeta, zeta, xY[:, 5, :], False)
    mul(eP, eP, rX[:, 5, :], False)
    mul(eT, eT, zetaY)
    add(last, YY[:, 0, :], last, False)
    add(zeta, zeta, x5, False)
    add(eP, eP, eT)
    mul(OX[:, 5, :], xZ[:, 5, :], last, False)
    mul(zeta, zeta, xX[:, 0, :])
    add(OX[:, 5, :], OX[:, 5, :], zeta)
    add(OX[:, 5, :], OX[:, 5, :], eP)

    mul(OZ[:, :, :], OZ[:, :, :], cs[:, angle(2, 0), :])
    v.wait_ge(sem["strings_ready"], 1)
    mul(OX[:, :, :], OX[:, :, :], sn[:, angle(2, 0), :])
    v.tensor_tensor(evp[:, :, 0:NQ].rearrange("p t q -> p q t"), OZ[:, :, :], OX[:, :, :],
                    ALU.subtract).then_inc(sem["ev_ready"], 1)


def neighbour_strings_on_gpsimd(eng, link, sem, buf):
    v, T16 = eng, NT
    R, XP, PP, G, OX = (buf[n] for n in ("R", "XP", "PP", "GX", "OX"))
    rX, rY, rZ, nrY, nrX = (R[:, i, :, :] for i in range(5))
    xX, xY, xZ, nxY = (XP[:, i, :, :] for i in range(4))

    def then(ins, wait):
        (link if wait else link.go)(ins)

    def mul(o, a, b, wait=True):
        then(v.tensor_tensor(o, a, b, ALU.mult), wait)

    def add(o, a, b, wait=True):
        then(v.tensor_tensor(o, a, b, ALU.add), wait)

    def sub(o, a, b, wait=True):
        then(v.tensor_tensor(o, a, b, ALU.subtract), wait)

    def copy(o, a, wait=True):
        then(v.tensor_copy(o, a), wait)

    def wide(a, shape):
        return a.broadcast_to(shape)

    v.wait_ge(sem["planes_ready"], 1)
    mul(PP[:, 0:2, 0:3, :], XP[:, 0:2, 2:5, :], wide(rX[:, 3:6, :].unsqueeze(1), [P, 2, 3, T16]))
    copy(PP[:, 2, 0:3, :], xZ[:, 2:5, :], False)
    copy(PP[:, 0:2, 3, :], XP[:, 0:2, 5, :], False)
    link(v.memset(PP[:, 2, 3, :], 0.0))
    pA, pB, pD = G[:, 8:12, :], G[:, 12:16, :], G[:, 16:20, :]
    pC = PP[:, 0, :, :]
    t0, t1 = G[:, 0:4, :], G[:, 4:8, :]
    vI, vX, vY, vZ = (G[:, 20 + 4 * i:24 + 4 * i, :] for i in range(4))
    mul(pA, PP[:, 0, :, :], rX[:, 2:6, :])
    mul(t0, PP[:, 1, :, :], rY[:, 2:6, :])
    mul(t1, PP[:, 2, :, :], rZ[:, 2:6, :])
    add(pB, t0, t1)
    mul(t0, PP[:, 1, :, :], rZ[:, 2:6, :])
    mul(t1, PP[:, 2, :, :], nrY[:, 2:6, :])
    add(pD, t0, t1)
    mul(vI, xZ[:, 1:5, :], pB)
    mul(vZ, xZ[:, 1:5, :], pA)
    mul(t0, xX[:, 1:5, :], pC)
    mul(t1, nxY[:, 1:5, :], pD)
    add(vX, t0, t1)
    mul(t0, xY[:, 1:5, :], pC)
    mul(t1, xX[:, 1:5, :], pD)
    add(vY, t0, t1)
    mul(t0, vX, rX[:, 1:5, :])
    add(pA, vI, t0)
    mul(t0, vY, rY[:, 1:5, :])
    mul(t1, vZ, rZ[:, 1:5, :])
    add(pB, t0, t1)
    CZ = G[:, 36:40, :]
    link(v.tensor_copy(CZ[:, 0, :], rZ[:, 0, :]))
    for q in (1, 2, 3):
        mul(CZ[:, q, :], CZ[:, q - 1, :], rZ[:, q, :])
    mul(t0[:, 0:3, :], pB[:, 0:3, :], CZ[:, 0:3, :])
    add(OX[:, 1:4, :], pA[:, 0:3, :], t0[:, 0:3, :])
    s = [G[:, 40 + i, :] for i in range(8)]
    mul(s[0], pA[:, 3, :], rX[:, 1, :])
    mul(s[0], s[0], rX[:, 0, :])
    mul(s[1], rZ[:, 3, :], rZ[:, 2, :])
    mul(s[1], s[1], pB[:, 3, :])
    mul(s[1], s[1], nrY[:, 1, :])
    mul(s[1], s[1], rY[:, 0, :])
    add(OX[:, 4, :], s[0], s[1])
    mul(s[0], xY[:, 4, :], rY[:, 5, :])
    mul(s[0], s[0], rX[:, 4, :])
    mul(s[1], xZ[:, 4, :], rZ[:, 5, :])
    add(s[0], s[0], s[1])
    mul(s[1], xX[:, 4, :], nrY[:, 5, :])
    mul(s[1], s[1], rY[:, 4, :])
    mul(s[1], s[1], CZ[:, 3, :])
    add(s[0], s[0], s[1])
    mul(s[0], s[0], xZ[:, 5, :])
    v.tensor_tensor(OX[:, 4, :], OX[:, 4, :], s[0], ALU.add).then_inc(sem["strings_ready"], 1)
NH, HD, NC = 8, 24, 4
QD = HD // NC
NU = NC + 1
HG = 4
SROW = 3 * 32 + HD
BIAS_ROWS = 2
VBLK = 32
QSIGN = [[1, -1, -1, -1], [1, 1, -1, 1], [1, 1, 1, -1], [1, -1, 1, 1]]
VSIGN = [[1, 1, 1, 1], [1, -1, 1, -1], [1, -1, -1, 1], [1, 1, -1, -1]]
LSIGN = [[1, 1, 1, 1], [-1, 1, -1, 1], [-1, 1, 1, -1], [-1, -1, 1, 1]]
NQKV = 2 * NU * P + D
NMAX, NEXP = 3, 2
BANK_MAX, BANK_EXP, BANK_AV, BANK_MISC = 0, NMAX, NMAX + NEXP, 6
VSLOT = 4

LEAD_X, LEAD_U, LEAD_V = -12, -11, -6
LAG_MAX, LAG_EXP, LAG_AV = 8, 10, 11
LAG_PAIR, LAG_OT, LAG_PROJ = 13, 20, 22
HIS = 2 + NU
STEPS = range(LEAD_X, NH * (B - 1) + LAG_PROJ + 1)


def head_at(s, lag):
    n = s - lag
    return (n // NH, n % NH) if 0 <= n < NH * B else None


def misc_items(s):
    items = []
    if (s - LAG_MAX) % NH == 0 and 0 <= (s - LAG_MAX) // NH < B:
        items.append(("max", (s - LAG_MAX) // NH))
    if (s - LEAD_X) % NH == 0 and 0 <= (s - LEAD_X) // NH < B:
        items.append(("x", (s - LEAD_X) // NH))
    for u in range(NU):
        if (s - LEAD_U - u) % NH == 0 and 0 <= (s - LEAD_U - u) // NH < B:
            items.append(("u", (s - LEAD_U - u) // NH, u))
    if (s - LEAD_V) % NH == 0 and 0 <= (s - LEAD_V) // NH < B:
        items.append(("v", (s - LEAD_V) // NH))
    for k in range(NH // 2):
        if (s - LAG_PAIR - 2 * k) % NH == 0 and 0 <= (s - LAG_PAIR - 2 * k) // NH < B:
            items.append(("pair", (s - LAG_PAIR - 2 * k) // NH, k))
    if (s - LAG_OT) % NH == 0 and 0 <= (s - LAG_OT) // NH < B:
        items.append(("ot", (s - LAG_OT) // NH))
    if (s - LAG_PROJ) % NH == 0 and 0 <= (s - LAG_PROJ) // NH < B:
        items.append(("proj", (s - LAG_PROJ) // NH))
    assert len(items) <= 2
    return items


def misc_uses():
    return {item: n for n, item in enumerate(item for s in STEPS for item in misc_items(s))}


def wait_misc_done(eng, sem, n):
    eng.wait_ge(sem[f"misc_free{n % 2}"], n // 2 + 1)


def attention_on_tensor(nc, eng, sem, buf, ps):
    use = misc_uses()
    W, xa, xb = buf["wqkv"], buf["xa"], buf["xb"]
    QK, VS, PT, OTs, ident = buf["QK"], buf["VS"], buf["PT"], buf["OTs"], buf["ident"]

    def do_misc(item):
        n, kind, b = use[item], item[0], item[1]
        misc = ps[:, BANK_MISC + n % 2, :]
        if n >= 2:
            wait_misc_done(eng, sem, n - 2)
        if kind == "x":
            eng.wait_ge(sem["xn_ready"], b + 1)
            for t in range(TPB):
                eng.transpose(misc[:, P * t:P * t + P], buf["xn"][:, b % 2, t, 0:DA], ident[:, :])
            for t in range(TPB):
                ins = eng.transpose(misc[0:DB, SEQ + P * t:SEQ + P * t + P], buf["xn"][:, b % 2, t, DA:D], ident[:, :])
        elif kind == "u":
            u = item[2]
            if u == 0:
                eng.wait_ge(sem["xs_half"], b + 1)
                wait_misc_done(eng, sem, use[("x", b)])
            for g in range(2):
                c = (2 * u + g) * P
                ins = five(eng, misc[:, SEQ * g:SEQ * g + SEQ], [W[:, s, c:c + P] for s in range(4)], xa, xb, slice(0, SEQ), True)
        elif kind == "v":
            for t in range(TPB):
                ins = five(eng, misc[:, D * t:D * t + D], [W[:, s, 2 * NU * P:NQKV] for s in range(4)], xa, xb,
                           slice(P * t, P * t + P), False)
        elif kind == "pair":
            k = item[2]
            eng.wait_ge(sem["av_out"], NH * b + 2 * k + 2)
            for hh in range(2):
                for t in range(TPB):
                    at = P * (2 * hh + t)
                    ins = eng.transpose(misc[:, at:at + P], OTs[:, (2 * k + hh) % 4, P * t:P * t + P], ident[:, :])
        elif kind == "max":
            eng.wait_ge(sem["mx_done"], 4 * NH * (b + 1))
            for t in range(TPB):
                ins = eng.transpose(misc[0:NC * NH, P * t:P * t + P], buf["mx"][:, b % 2, t, :], ident[:, :])
        elif kind == "ot":
            eng.wait_ge(sem["o_ready"], 4 * (b + 1))
            for t in range(TPB):
                eng.transpose(misc[:, P * t:P * t + P], buf["o"][:, t, 0:DA], ident[:, :])
            for t in range(TPB):
                ins = eng.transpose(misc[0:DB, SEQ + P * t:SEQ + P * t + P], buf["o"][:, t, DA:D], ident[:, :])
        elif kind == "proj":
            eng.wait_ge(sem["ot_half"], b + 1)
            wait_misc_done(eng, sem, use[("ot", b)])
            for t in range(TPB):
                out = misc[:, D * t:D * t + D]
                eng.matmul(out, buf["ot"][:, P * t:P * t + P], buf["wp"][:, 0, :], start=True, stop=False)
                ins = eng.matmul(out, buf["ot"][0:DB, SEQ + P * t:SEQ + P * t + P], buf["wp"][0:DB, 1, :],
                                 start=False, stop=True)
        ins.then_inc(sem["misc_full"], 1)

    def scores_for_max(b, h, k):
        t, cp = k // 2, k % 2
        n = 4 * (NH * b + h) + k
        if n >= NMAX:
            eng.wait_ge(sem["mx_done"], n - NMAX + 1)
        for c in (2 * cp, 2 * cp + 1):
            ins = eng.matmul(ps[:, BANK_MAX + n % NMAX, SEQ * (c % 2):SEQ * (c % 2) + SEQ],
                             QK[0:SROW, b % 2, c, h, P * t:P * t + P], QK[0:SROW, b % 2, NC, h, :],
                             start=True, stop=True)
        ins.then_inc(sem["p1_full"], 1)

    def scores_for_exp(b, h, k):
        t, cp = k // 2, k % 2
        n = 4 * (NH * b + h) + k
        if n >= NEXP:
            eng.wait_ge(sem["exp_done"], n - NEXP + 1)
        eng.matmul(ps[:, BANK_EXP + n % NEXP, :], QK[0:SROW + BIAS_ROWS, b % 2, NC, h, P * t:P * t + P],
                   QK[0:SROW + BIAS_ROWS, b % 2, 2 * cp:2 * cp + 2, h, :], start=True, stop=True).then_inc(sem["p2_full"], 1)

    def values(b, h):
        n = NH * b + h
        if h == 0:
            eng.wait_ge(sem["vs_half"], b + 1)
            wait_misc_done(eng, sem, use[("v", b)])
        eng.wait_ge(sem["exp_done"], 4 * (n + 1))
        if n:
            eng.wait_ge(sem["av_out"], n)
        for t in range(TPB):
            for c in range(NC):
                ins = eng.matmul(ps[VBLK * c:VBLK * c + VBLK, BANK_AV, 0:SEQ], VS[:, b % VSLOT, t, h, :, :].rearrange("p a e -> p (a e)"),
                                 PT[:, n % 2, t, c, :], start=t == 0, stop=t == TPB - 1)
        ins.then_inc(sem["av_full"], 1)

    eng.wait_ge(sem["wqkv_ready"], 1)
    eng.wait_ge(sem["wp_ready"], 1)
    eng.wait_ge(sem["vs_clear"], 1)
    for s in STEPS:
        m, x, v = head_at(s, 0), head_at(s, LAG_EXP), head_at(s, LAG_AV)
        items = misc_items(s)
        if m:
            if m[1] % 2 == 0:
                eng.wait_ge(sem[f"qk_in{m[0] % 2}{m[1] // 2}"], 96 * (m[0] // 2 + 1))
            scores_for_max(*m, 0)
            scores_for_max(*m, 1)
        if x:
            if x[1] == 0:
                eng.wait_ge(sem["nm_in"], 32 * (x[0] + 1))
            scores_for_exp(*x, 0)
            scores_for_exp(*x, 1)
        for item in items[:1]:
            do_misc(item)
        for k in (2, 3):
            if m:
                scores_for_max(*m, k)
            if x:
                scores_for_exp(*x, k)
            if k == 2 and v:
                values(*v)
        for item in items[1:]:
            do_misc(item)


def attention_on_scalar(nc, eng, sem, buf, ps):
    use = misc_uses()
    VS, PT, OTs, HL = buf["VS"], buf["PT"], buf["OTs"], buf["HL"]

    def do_misc(item):
        n, kind, b = use[item], item[0], item[1]
        misc = ps[:, BANK_MISC + n % 2, :]
        if kind in ("x", "u", "v", "ot"):
            eng.wait_ge(sem["misc_full"], n + 1)
        if kind == "x":
            if b:
                eng.wait_ge(sem["misc_full"], use[("v", b - 1)] + 1)
            eng.activation(buf["xa"][:, 0, :], misc[:, 0:SEQ], ACT.Copy).then_inc(sem["hi_ready"], 1)
            eng.activation(buf["xb"][0:DB, :], misc[0:DB, SEQ:2 * SEQ], ACT.Copy).then_inc(sem["hi_ready"], 1)
        elif kind == "u":
            u = item[2]
            if b >= 2 and u == 0:
                for j in range(HG):
                    eng.wait_ge(sem[f"qk_in{b % 2}{j}"], 96 * (b // 2))
            eng.activation(HL[:, b % 2, 0, u, :, :].rearrange("p g n -> p (g n)"), misc, ACT.Copy).then_inc(sem["hi_ready"], 1)
            k = NU * b + u
            if k >= 2:
                eng.wait_ge(sem["lo_ready"], k - 1)
            eng.activation(buf["uf"][:, k % 2, :], misc, ACT.Copy).then_inc(sem[f"misc_free{n % 2}"], 1)
        elif kind == "v":
            if b >= VSLOT:
                eng.wait_ge(sem["av_full"], NH * (b - VSLOT + 1))
            for t in range(TPB):
                src = misc[:, D * t:D * t + D].rearrange("p (h a e) -> p h a e", h=NH, e=QD)
                eng.activation(VS[:, b % VSLOT, t, :, :, 0:QD], src, ACT.Copy)\
                   .then_inc(sem["vs_half"] if t == 0 else sem[f"misc_free{n % 2}"], 1)
        elif kind == "ot":
            eng.activation(buf["ot"][:, 0:SEQ], misc[:, 0:SEQ], ACT.Copy).then_inc(sem["ot_half"], 1)
            eng.activation(buf["ot"][0:DB, SEQ:2 * SEQ], misc[0:DB, SEQ:2 * SEQ], ACT.Copy).then_inc(sem[f"misc_free{n % 2}"], 1)

    def exponentials(b, h, k):
        t, cp = k // 2, k % 2
        m = NH * b + h
        n = 4 * m + k
        eng.wait_ge(sem["p2_full"], n + 1)
        if m >= 2 and k == 0:
            eng.wait_ge(sem["av_full"], m - 1)
        eng.activation(PT[:, m % 2, t, 2 * cp:2 * cp + 2, :].rearrange("p c n -> p (c n)"), ps[:, BANK_EXP + n % NEXP, :],
                       ACT.Exp, scale=float(HD) ** -0.5).then_inc(sem["exp_done"], 1)

    def copy_out(b, h):
        n = NH * b + h
        eng.wait_ge(sem["av_full"], n + 1)
        if n >= 4:
            m = n - 4
            eng.wait_ge(sem["misc_full"], use[("pair", m // NH, m % NH // 2)] + 1)
        eng.activation(OTs[:, h % 4, :], ps[:, BANK_AV, 0:SEQ], ACT.Copy).then_inc(sem["av_out"], 1)

    for s in STEPS:
        x, v = head_at(s, LAG_EXP), head_at(s, LAG_AV)
        items = misc_items(s)
        if x:
            exponentials(*x, 0)
            exponentials(*x, 1)
        for item in items[:1]:
            do_misc(item)
        if x:
            exponentials(*x, 2)
        if v:
            copy_out(*v)
        if x:
            exponentials(*x, 3)
        for item in items[1:]:
            do_misc(item)


def attention_on_vector(nc, eng, link, sem, buf, ps):
    use = misc_uses()
    H = buf["H"]

    def normalize(b):
        if b >= 2:
            eng.wait_ge(sem["misc_full"], use[("x", b - 2)] + 1)
        for t in range(TPB):
            k = TPB * b + t
            ins = eng.tensor_scalar(buf["xn"][:, b % 2, t, :], H[:, k, :], buf["rstd"][:, k:k + 1], buf["nmr"][:, k:k + 1],
                                    ALU.mult, ALU.add)
            if t < TPB - 1:
                link(ins)
            else:
                ins.then_inc(sem["xn_ready"], 1)

    def do_misc(item):
        n, kind, b = use[item], item[0], item[1]
        misc, free = ps[:, BANK_MISC + n % 2, :], sem[f"misc_free{n % 2}"]
        if kind == "x":
            eng.wait_ge(sem["hi_ready"], HIS * b + 2)
            eng.tensor_tensor(buf["xa"][:, 1, :], misc[:, 0:SEQ], buf["xa"][:, 0, :].bitcast(F32), ALU.subtract).then_inc(sem["xs_half"], 1)
            eng.tensor_tensor(buf["xb"][DB:P, :], misc[0:DB, SEQ:2 * SEQ], buf["xb"][0:DB, :].bitcast(F32),
                              ALU.subtract).then_inc(free, 1)
        elif kind == "pair":
            k = item[2]
            eng.wait_ge(sem["misc_full"], n + 1)
            G = misc.rearrange("p (g e) -> p g e", e=8)
            link(eng.reciprocal(buf["rec"][:, :], G[:, 0:64:NC, QD]))
            link(eng.tensor_tensor(buf["rs"][:, :, :, :], buf["rec"][:, :].rearrange("p (k c) -> p k c", c=NC).unsqueeze(3).broadcast_to([P, 4, NC, NC]),
                                   buf["vsign"][:, :, :].unsqueeze(1).broadcast_to([P, 4, NC, NC]), ALU.mult))
            TM = buf["TM"]
            eng.tensor_tensor(TM[:, :, :, :, :].rearrange("p c k a e -> p k c a e"),
                              G[:, :, 0:QD].rearrange("p (k c a) e -> p k c a e", c=NC, a=NC),
                              buf["rs"][:, :, :, :].unsqueeze(4).broadcast_to([P, 4, NC, NC, QD]), ALU.mult).then_inc(free, 1)
        elif kind == "max":
            eng.wait_ge(sem["misc_full"], n + 1)
            if b:
                eng.wait_ge(sem["nm_in"], 32 * b)
            M = NC * NH
            eng.tensor_scalar(buf["nm"][0:M, 0, :], misc[0:M, 0:SEQ], -1.0, None, ALU.mult).then_inc(sem["nm_ready"], 1)
            eng.wait_ge(sem["nm_ready"], b + 1)
            eng.scalar_tensor_tensor(buf["nm"][0:M, 1, :], misc[0:M, 0:SEQ], -1.0, buf["nm"][0:M, 0, :].bitcast(F32),
                                     ALU.mult, ALU.subtract).then_inc(free, 1)
        elif kind == "proj":
            eng.wait_ge(sem["misc_full"], n + 1)
            eng.wait_ge(sem["bp_added"], b + 1)
            dst = H[:, TPB * b:TPB * b + TPB, :]
            eng.tensor_tensor(dst, misc[:, 0:TPB * D].rearrange("p (t d) -> p t d", t=TPB), dst, ALU.add).then_inc(free, 1)
            wait_misc_done(eng, sem, n)
            moments(eng, link, buf, range(TPB * b, TPB * b + TPB))

    def sum_pair(b, k):
        TM = buf["TM"]
        wait_misc_done(eng, sem, use[("pair", b, k)])
        T0, T1, T2, T3 = (TM[:, c, :, :, :] for c in range(NC))
        f = lambda a: a.rearrange("p k (x y) e -> p (k x) y e", y=2)
        link(eng.tensor_tensor(f(T0), f(T0), f(T1)[:, :, ::-1, :], ALU.add))
        g = lambda a: a.rearrange("p k (x y) e -> p k x (y e)", y=2)
        link(eng.tensor_tensor(g(T0), g(T0), g(T2)[:, :, ::-1, :], ALU.add))
        if b and k == 0:
            eng.wait_ge(sem["misc_full"], use[("ot", b - 1)] + 1)
        dst = buf["o"][:, :, 2 * HD * k:2 * HD * k + 2 * HD].rearrange("p t (h a e) -> p h t a e", h=2, a=NC)
        m = lambda a: a.rearrange("p (h t) a e -> p h t a e", h=2)
        eng.tensor_tensor(dst, m(T0), m(T3[:, :, ::-1, :]), ALU.add).then_inc(sem["o_ready"], 1)
        eng.wait_ge(sem["o_ready"], 4 * b + k + 1)

    def maximum(b, h, k):
        t, cp = k // 2, k % 2
        n = 4 * (NH * b + h) + k
        if b >= 2 and h == 0 and k == 0:
            eng.wait_ge(sem["misc_full"], use[("max", b - 2)] + 1)
        eng.wait_ge(sem["p1_full"], n + 1)
        eng.reduce_max(buf["mx"][:, b % 2, t, :].rearrange("p (c h) -> p c h", h=NH)[:, 2 * cp:2 * cp + 2, h],
                       ps[:, BANK_MAX + n % NMAX, :].rearrange("p (c n) -> p c n", c=2), AX.X).then_inc(sem["mx_done"], 1)

    normalize(0)
    for s in STEPS:
        m = head_at(s, 0)
        items = misc_items(s)
        if m:
            maximum(*m, 0)
            maximum(*m, 1)
            maximum(*m, 2)
        for item in items[:1]:
            do_misc(item)
        if m:
            maximum(*m, 3)
        for item in items[1:]:
            do_misc(item)
        for item in items:
            if item[0] == "pair":
                sum_pair(*item[1:])
        if (s - LEAD_X) % NH == NH - 2 and (s - LEAD_X) // NH + 1 < B:
            normalize((s - LEAD_X) // NH + 1)


def attention_on_gpsimd(eng, sem, buf):
    use, HL = misc_uses(), buf["HL"]
    for b in range(B):
        for u in range(NU):
            wait_misc_done(eng, sem, use[("u", b, u)])
            halves = [HL[:, b % 2, k, u, :, :].rearrange("p g n -> p (g n)") for k in range(2)]
            eng.tensor_tensor(halves[1], buf["uf"][:, (NU * b + u) % 2, :], halves[0].bitcast(F32), ALU.subtract).then_inc(sem["lo_ready"], 1)
        eng.wait_ge(sem["xn_ready"], b + 1)
        tiles = buf["H"][:, TPB * b:TPB * b + TPB, :]
        eng.tensor_tensor(tiles, tiles, buf["bp"][:, :].unsqueeze(1).broadcast_to([P, TPB, D]), ALU.add).then_inc(sem["bp_added"], 1)


def attention_on_sync(nc, eng, sem, buf):
    use = misc_uses()
    QK, HL, nm = buf["QK"], buf["HL"], buf["nm"]
    for s in STEPS:
        if ("max", (s - LAG_MAX) // NH) in misc_items(s):
            b = (s - LAG_MAX) // NH
            eng.wait_ge(sem["nm_ready"], b + 1)
            wait_misc_done(eng, sem, use[("max", b)])
            if b >= 2:
                eng.wait_ge(sem["p2_full"], 4 * NH * (b - 1))
            for k in range(2):
                eng.dma_start(QK[SROW + k:SROW + k + 1, b % 2, 0:NC, :, :].bitcast(F32),
                              nm[0:NC * NH, k, :].bitcast(F32)).then_inc(sem["nm_in"], 16)
        n = s - LAG_EXP + 2 * NH - 1
        b, j = n // NH, n % NH // 2
        if n % 2 == 0 and 0 <= b < B:
            if b < 2:
                eng.wait_ge(sem[f"qk_clear{b}"], 1)
            eng.wait_ge(sem["lo_ready"], NU * (b + 1))
            if b >= 2:
                eng.wait_ge(sem["p2_full"], 4 * (NH * (b - 2) + 2 * j + 2))
            for blk, parts in ((0, [(0, 0, NU)]), (1, [(1, 0, NC), (0, NC, NU)]), (2, [(0, 0, NC), (1, NC, NU)]), (3, [(1, 0, NU)])):
                for half, u0, u1 in parts:
                    eng.dma_start(QK[32 * blk:32 * blk + HD, b % 2, u0:u1, 2 * j:2 * j + 2, :].rearrange("r u g n -> r u (g n)").bitcast(F32),
                                  HL[32 * j:32 * j + HD, b % 2, half, u0:u1, :, :].rearrange("r u g n -> r u (g n)").bitcast(F32))\
                       .then_inc(sem[f"qk_in{b % 2}{j}"], 16)
GT = 4
NG = NT // GT
GW = GT * P
SPLIT = (True, False, True)
HI_BASE = (0, 2 * NG, 3 * NG)


def transposed_on_vector(eng, link, sem, buf, ps, k):
    H, xn = buf["H"], buf[f"xn{k}"]
    for t in range(NT):
        eng.tensor_scalar(xn[:, t, :], H[:, t, :], buf["rstd"][:, t:t + 1], buf["nmr"][:, t:t + 1],
                          ALU.mult, ALU.add).then_inc(sem["xt_xn"], 1)
    if SPLIT[k]:
        xa, xb = buf[f"xa{k}"], buf[f"xb{k}"]
        for g in range(NG):
            cols, bank = slice(GW * g, GW * g + GW), 2 * (g % 2)
            eng.wait_ge(sem["xt_hi"], HI_BASE[k] + 2 * (g + 1))
            eng.tensor_tensor(xa[:, 1, cols], ps[:, bank, :], xa[:, 0, cols].bitcast(F32), ALU.subtract).then_inc(sem["xt_lo"], 1)
            eng.tensor_tensor(xb[DB:P, cols], ps[0:DB, bank + 1, :], xb[0:DB, cols].bitcast(F32), ALU.subtract).then_inc(sem["xt_free"], 1)


def transposed_on_tensor(eng, sem, buf, ps, k):
    for g in range(NG):
        n, bank = NG * k + g, 2 * (g % 2)
        eng.wait_ge(sem["xt_xn"], NT * k + GT * (g + 1))
        if n >= 2:
            eng.wait_ge(sem["xt_free"], n - 1)
        for t in range(GT):
            eng.transpose(ps[:, bank, P * t:P * t + P], buf[f"xn{k}"][:, GT * g + t, 0:DA], buf["ident"][:, :])
        for t in range(GT):
            ins = eng.transpose(ps[0:DB, bank + 1, P * t:P * t + P], buf[f"xn{k}"][:, GT * g + t, DA:D], buf["ident"][:, :])
        ins.then_inc(sem["xt_full"], 1)


def transposed_on_scalar(eng, sem, buf, ps, k):
    for g in range(NG):
        cols, bank = slice(GW * g, GW * g + GW), 2 * (g % 2)
        eng.wait_ge(sem["xt_full"], NG * k + g + 1)
        if SPLIT[k]:
            eng.activation(buf[f"xa{k}"][:, 0, cols], ps[:, bank, :], ACT.Copy).then_inc(sem["xt_hi"], 1)
            eng.activation(buf[f"xb{k}"][0:DB, cols], ps[0:DB, bank + 1, :], ACT.Copy).then_inc(sem["xt_hi"], 1)
        else:
            eng.activation(buf["xtA"][:, cols], ps[:, bank, :], ACT.Copy).then_inc(sem["xt_hi"], 1)
            eng.activation(buf["xtB"][:, cols], ps[0:DB, bank + 1, :], ACT.Copy).then_inc(sem["xt_free"], 1)


def x_ready(eng, sem, k, g):
    eng.wait_ge(sem["xt_free"], NG * k + g + 1)
    eng.wait_ge(sem["xt_hi"], HI_BASE[k] + (2 if SPLIT[k] else 1) * (g + 1))
    if SPLIT[k]:
        eng.wait_ge(sem["xt_lo"], NG * (k // 2) + g + 1)


def load_runs(eng, dst, src, sem):
    eng.dma_start(dst[:, 0, :], src[0:DA, :]).then_inc(sem, 16)
    for half in range(2):
        eng.dma_start(dst[DB * half:DB * half + DB, 1, :], src[DA:D, :]).then_inc(sem, 16)


HF = 768
MF = HF // P
NCLS, NA = 6, 5
NCT = B * NCLS
LEFT = 3


CPA = 4
TPA = CPA * B
HH = HF // 2
FIRST = (0, 1, 2, 0, 2)


def served(atom):
    classes = (2 * atom, 2 * atom + 1) if atom < LEFT else range(atom - LEFT, NCLS, 2)
    return [(c, NCLS // 2 * (c % 2) + c // 2 - FIRST[atom], LEFT + c % 2 if atom < LEFT else c // 2) for c in classes]


def ffn0_on_sync(eng, sem, buf, io):
    eng.wait_ge(sem["misc_full"], misc_uses()[("v", B - 1)] + 1)
    load_runs(eng, buf["w1f"], io["fc1"], sem["w1_in"])
    eng.dma_start(buf["w2"][:, :, :], io["fc2"].rearrange("(m p) d -> p m d", p=P)).then_inc(sem["w2_in"], 16)
    eng.wait_ge(sem["p2_full"], 4 * NH * (B - 1))
    eng.dma_start(buf["b1"][:, :], io["fc1_b"]).then_inc(sem["b1_in"], 16)
    eng.dma_start(buf["b2"][:, :], io["fc2_b"].partition_broadcast(P)).then_inc(sem["b2_in"], 16)
    eng.dma_start(buf["gp"][0:NCT, :, :], io["gate_pair"]).then_inc(sem["gate_in"], 16)
    eng.dma_start(buf["bal"][0:NCT, :], io["balance"]).then_inc(sem["gate_in"], 16)
    eng.dma_start(buf["aob"][0:NCT, :, :], io["atom_out_b"]).then_inc(sem["aob_in"], 16)
    eng.dma_start(buf["ain"][:, :, 0, :], io["atom_in"][:, 0:DA, :].rearrange("a p h -> p a h")).then_inc(sem["ain_in"], 16)
    eng.dma_start(buf["ain"][0:DB + 1, :, 1, :], io["atom_in"][:, DA:D + 1, :].rearrange("a p h -> p a h")).then_inc(sem["ain_in"], 16)
    eng.wait_ge(sem["p2_full"], 4 * NH * B)
    eng.dma_start(buf["aout"][:, :, :, :], io["atom_out"].rearrange("a (m p) d -> p a m d", p=P)).then_inc(sem["aout_in"], 16)
    wait_misc_done(eng, sem, len(misc_uses()) - 1)
    for b in range(B):
        eng.dma_start(buf["hc"][NCLS * b:NCLS * b + NCLS, :], buf["H"][0:NCLS, TPB * b, :]).then_inc(sem["hc_in"], 16)
    for b in range(B):
        eng.wait_ge(sem["xt_xn"], TPB * b + 1)
        eng.dma_start(buf["xc"][NCLS * b:NCLS * b + NCLS, :], buf["xn0"][0:NCLS, TPB * b, :]).then_inc(sem["xc_in"], 16)
    eng.wait_ge(sem["cls_done"], 1)
    for b in range(B):
        eng.wait_ge(sem["f0_add"], TPB * b + 1)
        eng.dma_start(buf["H"][0:NCLS, TPB * b, :], buf["hc"][NCLS * b:NCLS * b + NCLS, :]).then_inc(sem["h2_in"], 16)


def ffn0_on_gpsimd(eng, link, sem, buf):
    W, wf = buf["w1"], buf["w1f"]
    eng.wait_ge(sem["w1_in"], 48)
    link(eng.tensor_copy(W[:, 0:4:2, :], wf[:, :, :]))
    eng.tensor_tensor(W[:, 1:4:2, :], wf[:, :, :], W[:, 0:4:2, :].bitcast(F32), ALU.subtract).then_inc(sem["w1_ready"], 1)
    wait_misc_done(eng, sem, len(misc_uses()) - 1)
    eng.memset(buf["mh"][:, :, :, :], 0.0).then_inc(sem["mh_zero"], 1)
    eng.memset(buf["xct"][:, :, :], 1.0).then_inc(sem["xct_ones"], 1)
    eng.wait_ge(sem["b2_in"], 16)
    eng.wait_ge(sem["hc_in"], 16 * B)
    for t in range(0, NT, 2):
        eng.wait_ge(sem["xt_xn"], t + 2)
        tiles = buf["H"][:, t:t + 2, :]
        eng.tensor_tensor(tiles, tiles, buf["b2"][:, :].unsqueeze(1).broadcast_to([P, 2, D]), ALU.add).then_inc(sem["b2_added"], 1)


def ffn0_on_tensor(eng, sem, buf, ps):
    w1, w2, hid, mh, ident = buf["w1"], buf["w2"], buf["hid0"], buf["mh"], buf["ident"]
    xct = buf["xct"]
    transposed_on_tensor(eng, sem, buf, ps, 0)

    def hidden(g):
        x_ready(eng, sem, 0, g)
        for m in range(MF):
            n = MF * g + m
            if n >= 2:
                eng.wait_ge(sem["f0_act"], n - 1)
            five(eng, ps[:, 4 + n % 2, :], [w1[:, s, P * m:P * m + P] for s in range(4)], buf["xa0"], buf["xb0"],
                 slice(GW * g, GW * g + GW), True).then_inc(sem["f0_full"], 1)

    def down(g):
        eng.wait_ge(sem["f0_act"], MF * (g + 1))
        for t in range(GT):
            n = GT * g + t
            if n >= 2:
                eng.wait_ge(sem["f0_add"], n - 1)
            for m in range(MF):
                ins = eng.matmul(ps[:, 6 + n % 2, 0:D], hid[:, g % 2, m, P * t:P * t + P], w2[:, m, :],
                                 start=m == 0, stop=m == MF - 1)
            ins.then_inc(sem["f0_out"], 1)

    eng.wait_ge(sem["w1_ready"], 1)
    hidden(0)
    eng.wait_ge(sem["xc_in"], 16 * B)
    eng.wait_ge(sem["xt_free"], NG)
    eng.transpose(ps[:, 0, 0:NCT], buf["xc"][0:NCT, 0:DA], ident[0:NCT, 0:NCT])
    eng.transpose(ps[0:DB, 0, 64:64 + NCT], buf["xc"][0:NCT, DA:D], ident[0:NCT, 0:NCT]).then_inc(sem["xct_psum"], 1)
    hidden(1)
    eng.wait_ge(sem["xct_ready"], 2)
    eng.wait_ge(sem["ain_in"], 32)
    for atoms, banks in (((0, 1, 2, 3), (1, 2)), ((4,), (3, 0))):
        for half, bank in enumerate(banks):
            for part, k in ((0, P), (1, DB + 1)):
                for q, a in enumerate(atoms):
                    x = xct[0:k, part, B * FIRST[a]:B * FIRST[a] + TPA]
                    ins = eng.matmul(ps[TPA * q:TPA * q + TPA, bank, 0:HH], x, buf["ain"][0:k, a, part, HH * half:HH * half + HH],
                                     start=part == 0, stop=part == 1)
        ins.then_inc(sem["atom_full"], 1)
    eng.wait_ge(sem["w2_in"], 16)
    down(0)
    eng.wait_ge(sem["atom_act"], NA)
    for m in range(MF):
        eng.transpose(ps[:, 1 + m // 4, P * (m % 4):P * (m % 4) + P], buf["gh"][:, 0, P * m:P * m + P], ident[:, :])
        ins = eng.transpose(ps[:, 2, 2 * P + TPA * m:2 * P + TPA * m + TPA], buf["gh"][0:TPA, 1, P * m:P * m + P], ident[0:TPA, 0:TPA])
    ins.then_inc(sem["atom_t"], 1)
    hidden(2)
    down(1)
    eng.wait_ge(sem["aout_in"], 16)
    eng.wait_ge(sem["atom_done"], 1)
    for r, atoms in ((0, (3, 4)), (1, (0, 1, 2))):
        for i, a in enumerate(atoms):
            for m in range(MF):
                ins = eng.matmul(ps[0:NCT, 3, D * r:D * r + D], mh[:, a, m, :], buf["aout"][:, a, m, :],
                                 start=i + m == 0, stop=i == len(atoms) - 1 and m == MF - 1)
    ins.then_inc(sem["cand_full"], 1)
    hidden(3)
    down(2)
    down(3)


def ffn0_on_scalar(eng, sem, buf, ps):
    transposed_on_scalar(eng, sem, buf, ps, 0)
    eng.wait_ge(sem["b1_in"], 16)

    def gelus(g):
        for m in range(MF):
            n = MF * g + m
            eng.wait_ge(sem["f0_full"], n + 1)
            if g >= 2:
                eng.wait_ge(sem["f0_out"], GT * (g - 1))
            eng.activation(buf["hid0"][:, g % 2, m, :], ps[:, 4 + n % 2, :], ACT.Gelu, bias=buf["b1"][:, m:m + 1]).then_inc(sem["f0_act"], 1)

    by_class = lambda a, order: a.rearrange(f"k {order} -> k q h b", b=B, q=2)
    gelus(0)
    eng.wait_ge(sem["xct_psum"], 1)
    eng.wait_ge(sem["xct_ones"], 1)
    eng.activation(by_class(buf["xct"][:, 0, :], "(q h b)"), by_class(ps[:, 0, 0:NCT], "(b h q)"), ACT.Copy).then_inc(sem["xct_ready"], 1)
    eng.activation(by_class(buf["xct"][0:DB, 1, :], "(q h b)"), by_class(ps[0:DB, 0, 64:64 + NCT], "(b h q)"), ACT.Copy).then_inc(sem["xct_ready"], 1)
    gelus(1)
    for a in range(NA):
        eng.wait_ge(sem["atom_full"], 1 + a // 4)
        q = TPA * (a % 4)
        for half, bank in enumerate((1, 2) if a < 4 else (3, 0)):
            ins = eng.activation(buf["gh"][q:q + TPA, a // 4, HH * half:HH * half + HH], ps[q:q + TPA, bank, 0:HH], ACT.Gelu)
        ins.then_inc(sem["atom_act"], 1)
    gelus(2)
    eng.wait_ge(sem["gate_sq"], 1)
    eng.activation(buf["gs"][0:NCT, 2:5], buf["gs"][0:NCT, 2:5], ACT.Sqrt).then_inc(sem["gate_root"], 1)
    eng.wait_ge(sem["gate_shift"], 1)
    eng.activation(buf["ge"][0:NCT, :], buf["gl"][0:NCT, :], ACT.Exp).then_inc(sem["gate_exp"], 1)
    gelus(3)


def ffn0_on_vector(eng, link, sem, buf, ps):
    wait_misc_done(eng, sem, len(misc_uses()) - 1)
    statistics_on_vector(eng, link, sem, buf, 1)
    transposed_on_vector(eng, link, sem, buf, ps, 0)
    xc, gp, gq, gs, gl, ge, gr = (buf[n] for n in ("xc", "gp", "gq", "gs", "gl", "ge", "gr"))
    C = slice(0, NCT)
    eng.wait_ge(sem["xc_in"], 16 * B)
    eng.wait_ge(sem["gate_in"], 32)
    link(eng.tensor_tensor(gq[C, 0:2, :], gp[C, :, :], xc[C, :].unsqueeze(1).broadcast_to([NCT, 2, D]), ALU.mult))
    link(eng.tensor_tensor(gq[C, 2:4, :], gp[C, :, :], gp[C, :, :], ALU.mult))
    link(eng.tensor_tensor(gq[C, 4, :], xc[C, :], xc[C, :], ALU.mult))
    eng.reduce_sum(gs[C, 0:5], gq[C, :, :], AX.X).then_inc(sem["gate_sq"], 1)

    def adds(g):
        for t in range(GT):
            n = GT * g + t
            eng.wait_ge(sem["f0_out"], n + 1)
            eng.wait_ge(sem["b2_added"], n // 2 + 1)
            eng.tensor_tensor(buf["H"][:, n, :], ps[:, 6 + n % 2, 0:D], buf["H"][:, n, :], ALU.add).then_inc(sem["f0_add"], 1)
            if n % TPB:
                eng.wait_ge(sem["f0_add"], n + 1)
                moments(eng, link, buf, [n])

    adds(0)
    eng.wait_ge(sem["atom_t"], 1)
    eng.wait_ge(sem["mh_zero"], 1)
    for a in range(NA):
        for cls, i, dst in served(a):
            out = buf["mh"][:, dst, :, :].rearrange("p m (b c) -> p m b c", c=NCLS)[:, :, :, cls]
            if a < 4:
                parts = [(0, 4, 1, P, 0), (4, MF, 2, P, 0)]
            else:
                parts = [(0, MF, 2, TPA, 2 * P // TPA)]
            for m0, m1, bank, step, row in parts:
                at = TPA * a % P + B * i
                src = ps[:, bank, :].rearrange("p (m j) -> p m j", j=step)[:, row:row + m1 - m0, at:at + B]
                last = eng.tensor_copy(out[:, m0:m1], src)
                if (a, cls) != (NA - 1, NCLS - 1):
                    link.go(last)
    last.then_inc(sem["atom_done"], 1)
    eng.wait_ge(sem["gate_root"], 1)
    link(eng.tensor_scalar(gs[C, 2:5], gs[C, 2:5], 1e-12, None, ALU.max))
    link(eng.reciprocal(gs[C, 2:5], gs[C, 2:5]))
    link(eng.tensor_tensor(gl[C, :], gs[C, 0:2], gs[C, 2:4], ALU.mult))
    link(eng.scalar_tensor_tensor(gl[C, :], gl[C, :], gs[C, 4:5], buf["bal"][C, :], ALU.mult, ALU.add))
    link(eng.tensor_tensor(gr[C, 0:1], gl[C, 0:1], gl[C, 1:2], ALU.max))
    eng.tensor_scalar(gl[C, :], gl[C, :], gr[C, 0:1], None, ALU.subtract).then_inc(sem["gate_shift"], 1)
    eng.wait_ge(sem["gate_exp"], 1)
    link(eng.tensor_tensor(gr[C, 0:1], ge[C, 0:1], ge[C, 1:2], ALU.add))
    link(eng.reciprocal(gr[C, 0:1], gr[C, 0:1]))
    link(eng.tensor_scalar(ge[C, :], ge[C, :], gr[C, 0:1], None, ALU.mult))
    link(eng.tensor_tensor(gr[C, 1:2], ge[C, 0:1], ge[C, 1:2], ALU.is_ge))
    link(eng.tensor_tensor(gr[C, 2:3], ge[C, 0:1], ge[C, 1:2], ALU.max))
    link(eng.tensor_tensor(gr[C, 0:1], gr[C, 1:2], gr[C, 2:3], ALU.mult))
    link(eng.tensor_tensor(gr[C, 1:2], gr[C, 2:3], gr[C, 0:1], ALU.subtract))
    adds(1)
    eng.wait_ge(sem["cand_full"], 1)
    eng.wait_ge(sem["aob_in"], 16)
    eng.wait_ge(sem["hc_in"], 16 * B)
    cand = buf["cand"]
    link(eng.tensor_tensor(cand[C, :, :], ps[C, 3, 0:2 * D].rearrange("p (r d) -> p r d", r=2), buf["aob"][C, :, :], ALU.add))
    link(eng.scalar_tensor_tensor(buf["hc"][C, :], cand[C, 0, :], gr[C, 0:1], buf["hc"][C, :], ALU.mult, ALU.add))
    eng.scalar_tensor_tensor(buf["hc"][C, :], cand[C, 1, :], gr[C, 1:2], buf["hc"][C, :], ALU.mult, ALU.add).then_inc(sem["cls_done"], 1)
    adds(2)
    adds(3)


SCW = 3 * P


def attn1_on_tensor(eng, sem, buf, ps):
    A, Bm, xn, ident = buf["xtA"], buf["xtB"], buf["xn1"], buf["ident"]
    transposed_on_tensor(eng, sem, buf, ps, 1)

    def scores(b):
        x_ready(eng, sem, 1, b // 2)
        if b >= 2:
            eng.wait_ge(sem["a1_masked"], b - 1)
        for t, (at, w) in enumerate(((0, P), (P, 2 * P))):
            rows, cols = slice(SEQ * b + P * t, SEQ * b + P * t + P), slice(SEQ * b, SEQ * b + w)
            out = ps[:, 4 + b % 2, at:at + w]
            eng.matmul(out, A[:, rows], A[:, cols], start=True, stop=False)
            ins = eng.matmul(out, Bm[:, rows], Bm[:, cols], start=False, stop=True)
        ins.then_inc(sem["a1_scores"], 1)

    scores(0)
    for b in range(B + 1):
        if b + 1 < B:
            scores(b + 1)
        if b < B:
            eng.wait_ge(sem["a1_exp"], 2 * (b + 1))
            if b:
                eng.wait_ge(sem["a1_pt"], b)
            for k in range(3):
                ins = eng.transpose(ps[:, 6, P * k:P * k + P], buf["p1"][:, b % 2, P * k:P * k + P], ident[:, :])
            ins.then_inc(sem["a1_pt_psum"], 1)
        if b:
            c = b - 1
            eng.wait_ge(sem["a1_pt"], c + 1)
            if c:
                eng.wait_ge(sem["a1_add"], 2 * c)
            pt = buf["pt1"][:, c % 2, :]
            eng.matmul(ps[:, 7, 0:D], pt[:, 0:P], xn[:, TPB * c, :], start=True, stop=True)
            eng.matmul(ps[:, 7, D:2 * D], pt[:, P:2 * P], xn[:, TPB * c, :], start=True, stop=False)
            eng.matmul(ps[:, 7, D:2 * D], pt[:, 2 * P:3 * P], xn[:, TPB * c + 1, :], start=False, stop=True).then_inc(sem["a1_av"], 1)


def attn1_on_scalar(eng, sem, buf, ps):
    transposed_on_scalar(eng, sem, buf, ps, 1)
    for b in range(B):
        eng.wait_ge(sem["a1_shift"], b + 1)
        if b >= 2:
            eng.wait_ge(sem["a1_pt_psum"], b - 1)
        for t, (at, w) in enumerate(((0, P), (P, 2 * P))):
            eng.activation(buf["p1"][:, b % 2, at:at + w], buf["sc1"][:, b % 2, at:at + w], ACT.Exp,
                           bias=buf["m1"][:, b % 2, t:t + 1], accum_out=buf["sum1"][:, b % 3, t:t + 1]).then_inc(sem["a1_exp"], 1)
        eng.wait_ge(sem["a1_pt_psum"], b + 1)
        if b >= 2:
            eng.wait_ge(sem["a1_av"], b - 1)
        eng.activation(buf["pt1"][:, b % 2, :], ps[:, 6, 0:SCW], ACT.Copy).then_inc(sem["a1_pt"], 1)


def attn1_on_vector(eng, link, sem, buf, ps):
    eng.wait_ge(sem["h2_in"], 16 * B)
    moments(eng, link, buf, range(0, NT, TPB))
    statistics_on_vector(eng, link, sem, buf, 2)
    transposed_on_vector(eng, link, sem, buf, ps, 1)
    eng.wait_ge(sem["mask_ready"], 2)

    def mask(b):
        eng.wait_ge(sem["a1_scores"], b + 1)
        if b >= 2:
            eng.wait_ge(sem["a1_exp"], 2 * (b - 1))
        eng.scalar_tensor_tensor(buf["sc1"][:, b % 2, :], ps[:, 4 + b % 2, 0:SCW], float(D) ** -0.5, buf["mask"][:, :],
                                 ALU.mult, ALU.add).then_inc(sem["a1_masked"], 1)
        eng.wait_ge(sem["a1_masked"], b + 1)
        link(eng.reduce_max(buf["m1"][:, b % 2, 0:1], buf["sc1"][:, b % 2, 0:P], AX.X))
        link(eng.reduce_max(buf["m1"][:, b % 2, 1:2], buf["sc1"][:, b % 2, P:SCW], AX.X))
        eng.tensor_scalar(buf["m1"][:, b % 2, :], buf["m1"][:, b % 2, :], -1.0, None, ALU.mult).then_inc(sem["a1_shift"], 1)

    mask(0)
    for b in range(B + 1):
        if b + 1 < B:
            mask(b + 1)
        if b:
            c = b - 1
            eng.wait_ge(sem["a1_exp"], 2 * (c + 1))
            if c:
                eng.wait_ge(sem["a1_add"], TPB * c)
            link(eng.reciprocal(buf["rec1"][:, :], buf["sum1"][:, c % 3, :]))
            eng.wait_ge(sem["a1_av"], c + 1)
            for t in range(TPB):
                h = buf["H"][:, TPB * c + t, :]
                eng.scalar_tensor_tensor(h, ps[:, 7, D * t:D * t + D], buf["rec1"][:, t:t + 1], h, ALU.mult, ALU.add).then_inc(sem["a1_add"], 1)
            eng.wait_ge(sem["a1_add"], TPB * (c + 1))
            moments(eng, link, buf, range(TPB * c, TPB * c + TPB))


NE, TOPK = 8, 2
HE, HS = D, HF
HALL = NE * HE + HS
MR, MA = NE * HE // P, HALL // P
RW = NE + 2
LOROW = 32
NGATE = NE + 1
WC = HF // 2
NWC = 2 * HALL // WC


def chunk(n):
    at = n % 2 * HALL + n // 2 * WC
    return slice(at, at + WC)


def ffn1_on_sync(eng, sem, buf, io):
    eng.wait_ge(sem["f0_add"], NT)
    eng.wait_ge(sem["h2_in"], 16 * B)
    eng.dma_start(buf["wd"][:, :, :], io["w_down"].rearrange("(m p) d -> p m d", p=P)).then_inc(sem["wd_in"], 16)
    eng.dma_start(buf["sgb"][:, :], io["sg_b"].partition_broadcast(P)).then_inc(sem["sgb_in"], 16)
    load_runs(eng, buf["wrf"], io["router"], sem["wr_in"])
    for n in range(NWC):
        if n >= 2:
            eng.wait_ge(sem["wgu_ready"], n - 1)
        load_runs(eng, buf["wgf"][:, n % 2, :, :], io["w_gate_up"][:, chunk(n)], sem[f"wgu_in{n % 2}"])


def ffn1_on_gpsimd(eng, link, sem, buf, io):
    eng.wait_ge(sem["f0_add"], NT)
    eng.wait_ge(sem["h2_in"], 16 * B)
    eng.dma_start(buf["sel"][0:2 * LOROW, :, :], io["select"]).then_inc(sem["sel_in"], 16)
    eng.memset(buf["mask"][:, :], 0.0).then_inc(sem["mask_zero"], 1)
    eng.wait_ge(sem["mask_zero"], 1)
    for k in (0, 2):
        tile = buf["mask"][:, P * k:P * k + P]
        eng.affine_select(out=tile, in_=tile, compare_op=ALU.is_ge, fill=-1e9, base=0, pattern=[[-1, P]],
                          channel_multiplier=1).then_inc(sem["mask_ready"], 1)
    eng.memset(buf["gt"][:, :].bitcast(F32), 0.0).then_inc(sem["gt_zero"], 1)
    eng.wait_ge(sem["wr_in"], 48)
    link(eng.tensor_copy(buf["wr"][:, 0:4:2, :], buf["wrf"][:, :, :]))
    eng.tensor_tensor(buf["wr"][:, 1:4:2, :], buf["wrf"][:, :, :], buf["wr"][:, 0:4:2, :].bitcast(F32), ALU.subtract).then_inc(sem["wr_ready"], 1)
    for n in range(NWC):
        eng.wait_ge(sem[f"wgu_in{n % 2}"], 48 * (n // 2 + 1))
        cols, wf, W = chunk(n), buf["wgf"][:, n % 2, :, :], buf["wgu"]
        link(eng.tensor_copy(W[:, 0:4:2, cols], wf))
        eng.tensor_tensor(W[:, 1:4:2, cols], wf, W[:, 0:4:2, cols].bitcast(F32), ALU.subtract).then_inc(sem["wgu_ready"], 1)
    for n in range(NG * MA):
        g, m = n // MA, n % MA
        eng.wait_ge(sem["f1_prod"], n + 1)
        eng.wait_ge(sem["f1_gb"], gb_count(g, m))
        if n >= NHID:
            eng.wait_ge(sem["f1_used"], n - NHID + 1)
        gb = buf["gb"][:, m % 2, :] if m < MR else buf["gbs"][:, :]
        eng.tensor_tensor(buf["hid1"][:, n % NHID, :], buf["prod"][:, n % NPROD, :], gb, ALU.mult).then_inc(sem["f1_hid"], 1)


def gb_count(g, m):
    return (MR + 1) * g + min(m, MR) + 1


NHID = 4
NPROD = 6
EARLY = 4
SPREAD_LAG = 2
DOWN_LAG = SPREAD_LAG + 3


def ffn1_on_tensor(eng, sem, buf, ps):
    W, wd, hid, ident = buf["wgu"], buf["wd"], buf["hid1"], buf["ident"]
    eng.wait_ge(sem["wr_ready"], 1)
    transposed_on_tensor(eng, sem, buf, ps, 2)
    for g in range(NG):
        x_ready(eng, sem, 2, g)
        five(eng, ps[0:RW, 4 + g, :], [buf["wr"][:, s, :] for s in range(4)], buf["xa2"], buf["xb2"],
             slice(GW * g, GW * g + GW), True).then_inc(sem["router_t"], 1)

    def gate_up(g, m):
        n = MA * g + m
        cols = slice(GW * g, GW * g + GW)
        if n >= 2:
            eng.wait_ge(sem["f1_silu"], n - 1)
        five(eng, ps[:, n % 2, :], [W[:, s, P * m:P * m + P] for s in range(4)], buf["xa2"], buf["xb2"], cols, True)\
            .then_inc(sem["f1_gate"], 1)
        if n >= 2:
            eng.wait_ge(sem["f1_prod"], n - 1)
        five(eng, ps[:, 2 + n % 2, :], [W[:, s, HALL + P * m:HALL + P * m + P] for s in range(4)], buf["xa2"], buf["xb2"], cols, True)\
            .then_inc(sem["f1_up"], 1)

    def router_logits():
        eng.wait_ge(sem["router_lt"], NG)
        for t in range(NT):
            ins = eng.transpose(ps[:, 4, RW * t:RW * t + RW], buf["lt"][0:RW, P * t:P * t + P], ident[0:RW, 0:RW])
        ins.then_inc(sem["router_psum"], 1)

    def gates():
        eng.wait_ge(sem["gates_ready"], 1)
        for t in range(NT):
            ins = eng.transpose(ps[0:NGATE, 4 + t // GT, P * (t % GT):P * (t % GT) + P], buf["ga"][:, t, :], ident[:, :])
            if t % GT == GT - 1:
                ins.then_inc(sem["gt_psum"], 1)
        eng.wait_ge(sem["sel_in"], 16)

    def spread(g, m):
        k = (MR + 1) * g + m
        if k < 2:
            eng.wait_ge(sem["gt_done"], k + 1)
        else:
            eng.wait_ge(sem["f1_gb"], k - 1)
        eng.matmul(ps[:, 4 + k % 2, :], buf["sel"][0:2 * LOROW, m, :], buf["gt"][0:2 * LOROW, GW * g:GW * g + GW],
                   start=True, stop=True).then_inc(sem["f1_spread"], 1)

    def down(n):
        g, m = n // MA, n % MA
        eng.wait_ge(sem["f1_hid"], n + 1)
        if m == 0 and g:
            eng.wait_ge(sem["f1_add"], GT * g)
        if m == 0:
            for k in range(2):
                eng.matmul(ps[:, 6 + k, 0:2 * D], buf["gt"][2 * LOROW:3 * LOROW, 0:P], buf["gt"][2 * LOROW:3 * LOROW, 0:2 * D],
                           start=True, stop=False)
        for t in range(GT):
            out, cols = ps[:, 6 + t // 2, D * (t % 2):D * (t % 2) + D], slice(P * t, P * t + P)
            ins = eng.matmul(out, hid[:, n % NHID, cols], wd[:, m, :], start=False, stop=m == MA - 1 and t % 2 == 1)
        ins.then_inc(sem["f1_used"], 1)

    for n in range(NG * MA + DOWN_LAG):
        g, m = n // MA, n % MA
        if g < NG:
            if g == 0:
                eng.wait_ge(sem["wgu_ready"], 2 * ((P * m + P - 1) // WC + 1))
            gate_up(g, m)
        if n == 0:
            router_logits()
        if n == EARLY - 1:
            gates()
            eng.wait_ge(sem["wd_in"], 16)
        if n == DOWN_LAG:
            eng.wait_ge(sem["gt_done"], NG)
        if n >= EARLY - 1:
            for k in range(EARLY - SPREAD_LAG) if n == EARLY - 1 else (n - SPREAD_LAG,):
                if k < NG * MA and k % MA <= MR:
                    spread(k // MA, k % MA)
        if n >= DOWN_LAG:
            down(n - DOWN_LAG)


def ffn1_on_scalar(eng, sem, buf, ps):
    transposed_on_scalar(eng, sem, buf, ps, 2)
    for g in range(NG):
        eng.wait_ge(sem["router_t"], g + 1)
        eng.activation(buf["lt"][0:RW, GW * g:GW * g + GW], ps[0:RW, 4 + g, :], ACT.Copy).then_inc(sem["router_lt"], 1)
    eng.wait_ge(sem["router_shift"], 1)
    eng.activation(buf["rl"][:, :, :], buf["rl"][:, :, :], ACT.Exp).then_inc(sem["router_exp"], 1)

    def silu(n):
        eng.wait_ge(sem["f1_gate"], n + 1)
        if n >= 2:
            eng.wait_ge(sem["f1_prod"], n - 1)
        eng.activation(buf["sg"][:, n % 2, :], ps[:, n % 2, :], ACT.Silu).then_inc(sem["f1_silu"], 1)

    for n in range(EARLY):
        silu(n)
    for k in range(NG):
        rows = slice(0, NGATE)
        cols = slice(GW * k, GW * k + GW)
        eng.wait_ge(sem["gt_zero"], 1)
        eng.wait_ge(sem["gt_psum"], k + 1)
        eng.activation(buf["gt"][rows, cols], ps[rows, 4 + k, :], ACT.Copy).then_inc(sem["gt_hi"], 1)
    for n in range(EARLY - 1, NG * MA + SPREAD_LAG):
        if EARLY <= n < NG * MA:
            silu(n)
        for j in range(EARLY - SPREAD_LAG) if n == EARLY - 1 else (n - SPREAD_LAG,):
            g, m = j // MA, j % MA
            if m <= MR:
                k = (MR + 1) * g + m
                eng.wait_ge(sem["f1_spread"], k + 1)
                last = j - 2 if m < MR else MA * g - 1
                if last >= 0:
                    eng.wait_ge(sem["f1_hid"], last + 1)
                dst = buf["gb"][:, m % 2, :] if m < MR else buf["gbs"][:, :]
                eng.activation(dst, ps[:, 4 + k % 2, :], ACT.Copy).then_inc(sem["f1_gb"], 1)


def ffn1_on_vector(eng, link, sem, buf, ps):
    statistics_on_vector(eng, link, sem, buf, 3)
    transposed_on_vector(eng, link, sem, buf, ps, 2)
    rl, mx, ga, cmp, rk = (buf[n] for n in ("rl", "rmx", "ga", "cmp", "rk"))
    def product(n):
        eng.wait_ge(sem["f1_up"], n + 1)
        eng.wait_ge(sem["f1_silu"], n + 1)
        if n >= NPROD:
            eng.wait_ge(sem["f1_hid"], n - NPROD + 1)
        eng.tensor_tensor(buf["prod"][:, n % NPROD, :], ps[:, 2 + n % 2, :], buf["sg"][:, n % 2, :], ALU.mult).then_inc(sem["f1_prod"], 1)

    eng.wait_ge(sem["router_psum"], 1)
    eng.wait_ge(sem["sgb_in"], 16)
    R = ps[:, 4, 0:NT * RW].rearrange("p (t r) -> p t r", r=RW)
    link(eng.reduce_max(mx[:, :], R[:, :, 0:NE], AX.X))
    link(eng.tensor_tensor(rl[:, :, 0:NE], R[:, :, 0:NE], mx[:, :].unsqueeze(2).broadcast_to([P, NT, NE]), ALU.subtract))
    eng.tensor_scalar(rl[:, :, NE], R[:, :, NE], buf["sgb"][:, 0:1], -1.0, ALU.add, ALU.mult).then_inc(sem["router_shift"], 1)
    eng.wait_ge(sem["router_exp"], 1)
    link(eng.tensor_scalar(mx[:, :], rl[:, :, NE], 1.0, None, ALU.add))
    link(eng.reciprocal(ga[:, :, NE], mx[:, :]))
    for e in range(NE):
        q = rl[:, :, e:e + 1]
        compared = link.go(eng.tensor_tensor(cmp[:, :, e, e:NE], rl[:, :, e:NE], q.broadcast_to([P, NT, NE - e]), ALU.is_gt))
        if e:
            compared = link.go(eng.tensor_tensor(cmp[:, :, e, 0:e], rl[:, :, 0:e], q.broadcast_to([P, NT, e]), ALU.is_ge))
        if e % 2:
            product(e // 2)
    link.after(compared)
    link(eng.reduce_sum(rk[:, :, :], cmp[:, :, :, :], AX.X))
    for n in range(NE // 2, EARLY):
        product(n)
    link(eng.tensor_scalar(rk[:, :, :], rk[:, :, :], float(TOPK), None, ALU.is_lt))
    link(eng.tensor_tensor(rk[:, :, :], rk[:, :, :], rl[:, :, 0:NE], ALU.mult))
    link(eng.reduce_sum(mx[:, :], rk[:, :, :], AX.X))
    link(eng.reciprocal(mx[:, :], mx[:, :]))
    link(eng.tensor_scalar(buf["oma"][:, :], ga[:, :, NE], -1.0, 1.0, ALU.mult, ALU.add))
    link(eng.tensor_tensor(mx[:, :], mx[:, :], buf["oma"][:, :], ALU.mult))
    eng.tensor_tensor(ga[:, :, 0:NE], rk[:, :, :], mx[:, :].unsqueeze(2).broadcast_to([P, NT, NE]), ALU.mult).then_inc(sem["gates_ready"], 1)

    for k in range(NG):
        eng.wait_ge(sem["gt_hi"], k + 1)
        rows, cols = slice(0, NGATE), slice(GW * k, GW * k + GW)
        eng.tensor_tensor(buf["gt"][LOROW:LOROW + NGATE, cols], ps[rows, 4 + k, :], buf["gt"][rows, cols].bitcast(F32),
                          ALU.subtract).then_inc(sem["gt_done"], 1)
    for n in range(EARLY, NG * MA + DOWN_LAG):
        if n < NG * MA:
            product(n)
        if (n + 1 - DOWN_LAG) % MA == 0 and n >= MA:
            g = (n + 1 - DOWN_LAG) // MA - 1
            eng.wait_ge(sem["f1_used"], MA * (g + 1))
            for t in range(0, GT, 2):
                h = buf["H"][:, GT * g + t:GT * g + t + 2, :]
                eng.tensor_tensor(h, ps[:, 6 + t // 2, 0:2 * D].rearrange("p (t d) -> p t d", t=2), h, ALU.add).then_inc(sem["f1_add"], 2)
SEMS = ["ids_in", "theta_in", "angles_ready", "trig_ready", "planes_ready", "strings_ready", "ev_ready", "ident_zero", "ident_ready", "pw_zero", "pw_in",
        "evt_psum", "evt_ready", "emb_psum", "h_ready", "dve_step", "pool_step", "out_sent",
        "var_ready", "std_ready", "wqkv_in", "wqkv_ready", "wqkv_signed", "wqkv_hi", "wp_in", "wp_ready", "bp_in", "bp_added", "vsign_in",
        "vs_clear", "qk_clear0", "qk_clear1", "xn_ready", "misc_full", "misc_free0", "misc_free1", "qk_in00", "qk_in01", "qk_in02", "qk_in03", "qk_in10", "qk_in11", "qk_in12", "qk_in13", "hi_ready", "lo_ready", "xs_half", "vs_half", "ot_half",
        "p1_full", "mx_done", "nm_ready", "nm_in", "p2_full", "exp_done", "av_full", "av_out", "o_ready",
        "xt_xn", "xt_full", "xt_hi", "xt_lo", "xt_free",
        "w1_in", "w1_ready", "b1_in", "w2_in", "b2_in", "b2_added", "gate_in", "aob_in", "ain_in", "aout_in", "hc_in", "xc_in",
        "mh_zero", "xct_ones", "xct_psum", "xct_ready", "atom_full", "atom_act", "atom_t", "atom_done", "cand_full", "cls_done", "h2_in",
        "gate_sq", "gate_root", "gate_shift", "gate_exp", "f0_full", "f0_act", "f0_out", "f0_add",
        "mask_zero", "mask_ready", "a1_scores", "a1_masked", "a1_shift", "a1_exp", "a1_pt_psum", "a1_pt", "a1_av", "a1_add",
        "wd_in", "sel_in", "sgb_in", "wr_in", "wr_ready", "wgu_in0", "wgu_in1", "wgu_ready", "gt_zero", "router_psum",
        "router_shift", "router_exp", "gates_ready", "gt_psum", "gt_hi", "gt_done", "f1_gate", "f1_up", "f1_silu",
        "f1_spread", "f1_gb", "f1_prod", "f1_hid", "f1_used", "router_t", "router_lt",  "f1_add"]


def clear_operands(eng, link, sem, buf, slot):
    link(eng.memset(buf["QK"][:, slot, :, :, :].rearrange("p u h n -> p (u h n)").bitcast(F32), 0.0))
    eng.memset(buf["QK"][96:P, slot, NC, :, :].rearrange("p h n -> p (h n)").bitcast(F32), 1.0).then_inc(sem[f"qk_clear{slot}"], 1)
    eng.wait_ge(sem[f"qk_clear{slot}"], 1)


def embedding_on_tensor(eng, sem, buf, ps):
    evt, pw, ident = buf["evt"], buf["pw"], buf["ident"]
    eng.wait_ge(sem["ident_ready"], 1)
    eng.wait_ge(sem["ev_ready"], 1)
    for c in range(4):
        eng.transpose(ps[:, 0, P * c:P * c + P], buf["evp"][:, 4 * c:4 * c + 4, :].rearrange("p t e -> p (t e)"),
                      ident[:, :]).then_inc(sem["evt_psum"], 1)
    eng.wait_ge(sem["pw_in"], 64)
    for c in range(4):
        eng.wait_ge(sem["evt_ready"], c + 1)
        for k in range(2):
            if c >= 2:
                eng.wait_ge(sem["h_ready"], 2 * c + k - 3)
            eng.matmul(ps[:, 1 + (2 * c + k) % 4, 0:2 * D], evt[:, c, :],
                       pw[:, 2 * k:2 * k + 2, :].rearrange("p t d -> p (t d)"), start=True, stop=True).then_inc(sem["emb_psum"], 1)


def embedding_on_scalar(eng, sem, buf, ps):
    eng.wait_ge(sem["angles_ready"], 1)
    eng.activation(buf["sn"][:, :, :], buf["red"][:, 0, :, :], ACT.Sin).then_inc(sem["trig_ready"], 1)
    eng.activation(buf["cs"][:, :, :], buf["red"][:, 1, :, :], ACT.Sin).then_inc(sem["trig_ready"], 1)
    eng.wait_ge(sem["wqkv_signed"], 1)
    eng.activation(buf["wqkv"][:, 0:4:2, :], buf["wf"][:, :, :], ACT.Copy).then_inc(sem["wqkv_hi"], 1)
    for c in range(4):
        eng.wait_ge(sem["evt_psum"], 4)
        eng.activation(buf["evt"][:, c, :], ps[:, 0, P * c:P * c + P], ACT.Copy).then_inc(sem["evt_ready"], 1)
    for i in range(8):
        eng.wait_ge(sem["emb_psum"], i + 1)
        eng.activation(buf["H"][:, 2 * i:2 * i + 2, :].rearrange("p t d -> p (t d)"), ps[:, 1 + i % 4, 0:2 * D],
                       ACT.Copy).then_inc(sem["h_ready"], 1)


def program(nc, io, out):
    ctx = ExitStack()
    with ctx:
        def alloc(scope, buf, name, shape, dt=F32):
            buf[name] = scope.enter_context(nc.sbuf_tensor(name, shape, dt))

        sem = {n: ctx.enter_context(nc.semaphore(n)) for n in SEMS}
        buf = {}
        for name, shape, dt in (("H", [P, NT, D], F32), ("ident", [P, P], F32), ("st", [P, NT, 6], F32),
                                ("mv", [P, NT, 2], F32), ("rstd", [P, NT], F32), ("nmr", [P, NT], F32),
                                ):
            alloc(ctx, buf, name, shape, dt)
        first = ctx.enter_context(ExitStack())
        for name, shape, dt in (("QK", [P, 2, NU, NH, SEQ], F32R), ("VS", [P, VSLOT, TPB, NH, NC, VBLK // NC], F32),
                                ("wqkv", [P, 4, NQKV], F32R), ("wp", [P, 2, D], F32), ("wps", [P, 2, D], F32),
                                ("bp", [P, D], F32), ("vsign", [P, NC, NC], F32)):
            alloc(first, buf, name, shape, dt)
        with ExitStack() as scope:
            for name, shape in (("theta", [P, NT, NANG]), ("red", [P, 2, NANG, NT]), ("sn", [P, NANG, NT]),
                                ("cs", [P, NANG, NT]), ("R", [P, 5, NQ, NT]), ("ZM", [P, 4, NQ, NT]),
                                ("XP", [P, 4, NQ, NT]), ("W", [P, 4, 12, NT]), ("U", [P, 4, 12, NT]),
                                ("M", [P, 6, 12, NT]), ("E", [P, 4, 12, NT]), ("PP", [P, 3, 4, NT]),
                                ("TZ", [P, 4, NT]), ("G", [P, 48, NT]), ("GX", [P, 48, NT]), ("OZ", [P, NQ, NT]), ("OX", [P, NQ, NT]),
                                ("evp", [P, NT, EVW]), ("evt", [P, 4, P]), ("pw", [P, 4, D]),
                                ("wf", [P, 2, NQKV]), ("wsg", [P, 2, NQKV])):
                alloc(scope, buf, name, shape)
            alloc(scope, buf, "ids", [P, NT], I32)
        with ExitStack() as scope:
            for name, shape, dt in (("HL", [P, 2, 2, NU, 2, SEQ], F32R), ("uf", [P, 2, 2 * SEQ], F32), ("PT", [P, 2, TPB, NC, SEQ], F32),
                                    ("OTs", [P, 4, SEQ], F32), ("o", [P, TPB, D], F32), ("ot", [P, 2 * SEQ], F32),
                                    ("TM", [P, NC, 4, NC, QD], F32), ("rec", [P, 16], F32), ("rs", [P, 4, NC, NC], F32),
                                    ("nm", [P, 2, SEQ], F32R), ("mx", [P, 2, TPB, NC * NH], F32),
                                    ("xn", [P, 2, TPB, D], F32), ("xa", [P, 2, SEQ], F32R), ("xb", [P, SEQ], F32R)):
                alloc(scope, buf, name, shape, dt)
        first.close()
        with ExitStack() as scope:
            for place, size, group in (
                    ("first operand stack", NU * NH * SEQ,
                     (("ain", [P, NA, 2, HF], F32), ("b1", [P, MF], F32), ("b2", [P, D], F32), ("bal", [P, 2], F32),
                      ("gp", [P, 2, D], F32), ("aob", [P, 2, D], F32))),
                    ("second operand stack and values", NU * NH * SEQ + VSLOT * TPB * NH * VBLK,
                     (("aout", [P, NA, MF, D], F32), ("hid0", [P, 2, MF, GW], F32))),
                    ("weights", 4 * NQKV, (("w1f", [P, 2, HF], F32), ("w1", [P, 4, HF], F32R), ("w2", [P, MF, D], F32))),
                    ("the others", None,
                     (("xn0", [P, NT, D], F32), ("xa0", [P, 2, NT * P], F32R), ("xb0", [P, NT * P], F32R), ("hc", [P, D], F32),
                      ("xc", [P, D], F32), ("xct", [P, 2, NCT], F32), ("mh", [P, NA, MF, NCT], F32), ("gh", [P, 2, HF], F32), ("gq", [P, 5, D], F32),
                      ("gs", [P, 5], F32), ("gl", [P, 2], F32), ("ge", [P, 2], F32), ("gr", [P, 3], F32), ("cand", [P, 2, D], F32)))):
                for name, shape, dt in group:
                    alloc(scope, buf, name, shape, dt)
                if size:
                    rest = size - sum(math.prod(shape[1:]) for _, shape, _ in group)
                    alloc(scope, buf, "behind " + place, [P, rest])
        for name, shape, dt in (("wgu", [P, 4, 2 * HALL], F32R), ("wd", [P, MA, D], F32), ("sel", [P, MR + 1, P], F32R),
                                ("wgf", [P, 2, 2, WC], F32), ("wrf", [P, 2, RW], F32), ("wr", [P, 4, RW], F32R),
                                ("sgb", [P, 1], F32), ("mask", [P, SCW], F32), ("gt", [P, NT * P], F32R)):
            alloc(ctx, buf, name, shape, dt)
        with ExitStack() as scope:
            for name, shape, dt in (("xn1", [P, NT, D], F32), ("xtA", [P, NT * P], F32), ("xtB", [DB, NT * P], F32),
                                    ("sc1", [P, 2, SCW], F32), ("p1", [P, 2, SCW], F32), ("pt1", [P, 2, SCW], F32),
                                    ("m1", [P, 2, TPB], F32), ("sum1", [P, 3, TPB], F32), ("rec1", [P, TPB], F32)):
                alloc(scope, buf, name, shape, dt)
        with ExitStack() as scope:
            for name, shape, dt in (("xn2", [P, NT, D], F32), ("hid1", [P, NHID, GW], F32), ("xa2", [P, 2, NT * P], F32R),
                                    ("xb2", [P, NT * P], F32R), ("sg", [P, 2, GW], F32), ("prod", [P, NPROD, GW], F32), ("lt", [P, NT * P], F32), ("gb", [P, 2, GW], F32),
                                    ("gbs", [P, GW], F32), ("rl", [P, NT, NGATE], F32), ("ga", [P, NT, NGATE], F32),
                                    ("rmx", [P, NT], F32), ("oma", [P, NT], F32), ("rk", [P, NT, NE], F32),
                                    ("cmp", [P, NT, NE, NE], F32)):
                alloc(scope, buf, name, shape, dt)
        ps = ctx.enter_context(nc.psum_tensor("ps", [P, 8, NBANK], F32))
        block = ctx.enter_context(nc.Block())

        @block.sync
        def _(eng):
            eng.dma_start(buf["ids"][:, :], io["ids"]).then_inc(sem["ids_in"], 16)
            for dst, name in ((buf["wf"], "wqkv"), (buf["wsg"], "wqkv_sign")):
                eng.dma_start(dst[:, 0, :], io[name][0:DA, :]).then_inc(sem["wqkv_in"], 16)
                for half in range(2):
                    eng.dma_start(dst[DB * half:DB * half + DB, 1, :], io[name][DA:D, :]).then_inc(sem["wqkv_in"], 16)
            for dst, name in ((buf["wp"], "wp"), (buf["wps"], "wp_sign")):
                eng.dma_start(dst[:, 0, :], io[name][0:DA, :]).then_inc(sem["wp_in"], 16)
                eng.dma_start(dst[0:DB, 1, :], io[name][DA:D, :]).then_inc(sem["wp_in"], 16)
            eng.dma_start(buf["bp"][:, :], io["bp"].partition_broadcast(P)).then_inc(sem["bp_in"], 16)
            eng.dma_start(buf["vsign"][:, :, :], io["vsign"].partition_broadcast(P)).then_inc(sem["vsign_in"], 16)
            eng.wait_ge(sem["pw_zero"], 1)
            for j in range(4):
                eng.dma_start(buf["pw"][EVW * j:EVW * j + NQ + 1, j, :], io["post"]).then_inc(sem["pw_in"], 16)
            attention_on_sync(nc, eng, sem, buf)
            ffn0_on_sync(eng, sem, buf, io)
            ffn1_on_sync(eng, sem, buf, io)
            eng.wait_ge(sem["f1_add"], NT)
            eng.dma_start(out.rearrange("a (h p) d -> p (a h) d", p=P), buf["H"][:, :, :]).then_inc(sem["out_sent"], 16)
            eng.wait_ge(sem["out_sent"], 16)

        @block.gpsimd
        def _(eng):
            link = Chain(eng, sem["pool_step"])
            eng.memset(buf["pw"][:, :, :], 0.0).then_inc(sem["pw_zero"], 1)
            eng.memset(buf["ident"][:, :], 0.0).then_inc(sem["ident_zero"], 1)
            eng.wait_ge(sem["ids_in"], 16)
            for t in range(NT):
                eng.indirect_dma_start(buf["theta"][:, t, :], None, io["qp"],
                                       bass.IndirectOffsetOnAxis(ap=buf["ids"][:, t:t + 1], axis=0)).then_inc(sem["theta_in"], 16)
            eng.wait_ge(sem["ident_zero"], 1)
            eng.affine_select(out=buf["ident"][:, :], in_=buf["ident"][:, :], compare_op=ALU.not_equal, fill=1.0, base=0,
                              pattern=[[-1, P]], channel_multiplier=1).then_inc(sem["ident_ready"], 1)
            W, wf = buf["wqkv"], buf["wf"]
            eng.wait_ge(sem["wqkv_in"], 96)
            eng.tensor_tensor(wf[:, :, :], wf[:, :, :], buf["wsg"][:, :, :], ALU.mult).then_inc(sem["wqkv_signed"], 1)
            eng.wait_ge(sem["wqkv_signed"], 1)
            neighbour_strings_on_gpsimd(eng, link, sem, buf)
            eng.wait_ge(sem["wqkv_hi"], 1)
            eng.tensor_tensor(W[:, 1:4:2, :], wf[:, :, :], W[:, 0:4:2, :].bitcast(F32), ALU.subtract).then_inc(sem["wqkv_ready"], 1)
            eng.wait_ge(sem["strings_ready"], 1)
            eng.wait_ge(sem["wqkv_ready"], 1)
            eng.wait_ge(sem["wp_in"], 64)
            link(eng.tensor_tensor(buf["wp"][:, 0, :], buf["wp"][:, 0, :], buf["wps"][:, 0, :], ALU.mult))
            eng.tensor_tensor(buf["wp"][0:DB, 1, :], buf["wp"][0:DB, 1, :], buf["wps"][0:DB, 1, :], ALU.mult).then_inc(sem["wp_ready"], 1)
            eng.wait_ge(sem["wp_ready"], 1)
            clear_operands(eng, link, sem, buf, 1)
            VS = buf["VS"][:, :, :, :, :, :].rearrange("p s t h a e -> p (s t h a) e")
            link(eng.memset(VS, 0.0))
            eng.memset(VS[:, ::NC, QD:QD + 1], 1.0)\
               .then_inc(sem["vs_clear"], 1)
            eng.wait_ge(sem["bp_in"], 16)
            attention_on_gpsimd(eng, sem, buf)
            ffn0_on_gpsimd(eng, link, sem, buf)
            ffn1_on_gpsimd(eng, link, sem, buf, io)

        @block.scalar
        def _(eng):
            embedding_on_scalar(eng, sem, buf, ps)
            root_on_scalar(eng, sem, buf, 0)
            eng.wait_ge(sem["vs_clear"], 1)
            attention_on_scalar(nc, eng, sem, buf, ps)
            root_on_scalar(eng, sem, buf, 1)
            ffn0_on_scalar(eng, sem, buf, ps)
            root_on_scalar(eng, sem, buf, 2)
            attn1_on_scalar(eng, sem, buf, ps)
            root_on_scalar(eng, sem, buf, 3)
            ffn1_on_scalar(eng, sem, buf, ps)

        @block.vector
        def _(eng):
            link = Chain(eng, sem["dve_step"])
            clear_operands(eng, link, sem, buf, 0)
            circuit_on_vector(eng, link, sem, buf)
            eng.wait_ge(sem["h_ready"], 8)
            moments(eng, link, buf, range(NT))
            statistics_on_vector(eng, link, sem, buf, 0)
            eng.wait_ge(sem["vsign_in"], 16)
            attention_on_vector(nc, eng, link, sem, buf, ps)
            ffn0_on_vector(eng, link, sem, buf, ps)
            attn1_on_vector(eng, link, sem, buf, ps)
            eng.wait_ge(sem["a1_add"], NT)
            ffn1_on_vector(eng, link, sem, buf, ps)

        @block.tensor
        def _(eng):
            embedding_on_tensor(eng, sem, buf, ps)
            eng.wait_ge(sem["h_ready"], 8)
            attention_on_tensor(nc, eng, sem, buf, ps)
            ffn0_on_tensor(eng, sem, buf, ps)
            attn1_on_tensor(eng, sem, buf, ps)
            ffn1_on_tensor(eng, sem, buf, ps)


def quaternion_layout(parts):
    return np.concatenate([np.concatenate([parts[r ^ c] for c in range(NC)], 1) for r in range(NC)], 0)


def arrange(inputs):
    a = {}
    get = lambda n: np.asarray(inputs[n])
    a["ids"] = get("x").reshape(NT, P).T
    a["qp"] = get("L0_tok_quantum_params").transpose(0, 1, 3, 2).reshape(VOCAB, NANG)
    a["post"] = np.concatenate([get("L0_tok_post_w").T, get("L0_tok_post_b")[None]], 0)
    full = quaternion_layout([get(f"L0_attn_wqkv_{c}") for c in "rijk"])
    sign = np.repeat(np.repeat(np.array(LSIGN, np.float32), D // NC, 0), 3 * D // NC, 1)
    w = np.zeros((D, NQKV), np.float32)
    s = np.zeros((D, NQKV), np.float32)
    for u in range(NU):
        for h in range(NH):
            for comp in range(NC):
                src = (0 if u < NC else D) + h * HD + ((u ^ comp) if u < NC else comp) * QD
                dst = (2 * u + h % 2) * P + 32 * (h // 2) + comp * QD
                w[:, dst:dst + QD] = full[:, src:src + QD]
                s[:, dst:dst + QD] = sign[:, src:src + QD] * (QSIGN[u][comp] if u < NC else 1)
    w[:, 2 * NU * P:] = full[:, 2 * D:]
    s[:, 2 * NU * P:] = sign[:, 2 * D:]
    a["wqkv"], a["wqkv_sign"] = w, s
    a["wp"] = quaternion_layout([get(f"L0_attn_wp_{c}") for c in "rijk"])
    a["wp_sign"] = np.repeat(np.repeat(np.array(LSIGN, np.float32), D // NC, 0), D // NC, 1)
    a["bp"] = get("L0_attn_bp")
    a["vsign"] = np.array(VSIGN, np.float32)
    left, right = [n // 2 for n in range(NCLS)], [LEFT + n % 2 for n in range(NCLS)]
    a["fc1"], a["fc1_b"] = get("L0_ffn_fc1_w").T, get("L0_ffn_fc1_b").reshape(MF, P).T
    a["fc2"], a["fc2_b"] = get("L0_ffn_fc2_w").T, get("L0_ffn_fc2_b")
    a["gate_pair"] = np.concatenate([get("L0_ffn_gate_pair")] * B, 0)
    a["balance"] = np.concatenate([get("L0_ffn_balance_bias")] * B, 0)
    ob = get("L0_ffn_atom_out_b")
    a["atom_out_b"] = np.concatenate([np.stack([ob[right], ob[left]], 1)] * B, 0)
    a["atom_in"] = np.concatenate([get("L0_ffn_atom_in_w").transpose(0, 2, 1), get("L0_ffn_atom_in_b")[:, None]], 1)
    a["atom_out"] = get("L0_ffn_atom_out_w").transpose(0, 2, 1)
    flat = lambda n: get(n).transpose(1, 0, 2).reshape(D, NE * HE)
    a["w_gate_up"] = np.concatenate([flat("L1_ffn_w_gate"), get("L1_ffn_ws_gate"), flat("L1_ffn_w_up"), get("L1_ffn_ws_up")], 1)
    a["w_down"] = np.concatenate([get("L1_ffn_w_down").reshape(NE * HE, D), get("L1_ffn_ws_down")], 0)
    a["router"] = np.concatenate([get("L1_ffn_router_w"), get("L1_ffn_sg_w"), np.zeros((D, 1), np.float32)], 1)
    a["sg_b"] = get("L1_ffn_sg_b")
    select = np.zeros((2 * LOROW, MR + 1, P), np.float32)
    for m in range(MR + 1):
        for p in range(P):
            e = min((P * m + p) // HE, NE)
            select[e, m, p] = select[LOROW + e, m, p] = 1
    a["select"] = select
    return {n: np.ascontiguousarray(x) for n, x in a.items()}


def kernel(**inputs):
    import concourse.bacc as _bacc
    from concourse import mybir as _mybir
    from concourse.bass_utils import run_bass_kernel_spmd as _run
    arrays = arrange(inputs)
    nc = _bacc.Bacc("TRN2", target_bir_lowering=False, num_devices=1)
    io = {n: nc.dram_tensor("in_" + n, a.shape, _mybir.dt.from_np(a.dtype), kind="ExternalInput").ap() for n, a in arrays.items()}
    o = nc.dram_tensor("out0", (B, SEQ, D), _mybir.dt.float32, kind="ExternalOutput").ap()
    program(nc, io, o)
    r = _run(nc, [{"in_" + n: a for n, a in arrays.items()}], core_ids=[0])
    return r.results[0]["out0"]
```
